# Optimizing a Trainium2 kernel written in Bass

```python
import numpy as np
import jax
import jax.numpy as jnp

def _softmax(x, axis=-1):
    return jax.nn.softmax(x, axis=axis)

def _gelu(x):
    return jax.nn.gelu(x, approximate=True)

def _silu(x):
    return jax.nn.silu(x)

def _sigmoid(x):
    return jax.nn.sigmoid(x)

def _layernorm(x, axis=-1, eps=1e-05):
    m = jnp.mean(x, axis=axis, keepdims=True)
    v = jnp.var(x, axis=axis, keepdims=True)
    return (x - m) / jnp.sqrt(v + eps)

def _scatter_add(tgt, idx, src, axis=0):
    return tgt.at[idx].add(src)

def _segment_sum(src, seg, n):
    return jax.ops.segment_sum(src, seg, n)
kernel_name = 'mk_hybrid_d1_jaxref_r4_b17724'

def setup_inputs(seed: int=0):
    np.random.seed(seed)
    _w = jnp.asarray

    def _L0_attn_a_setup():
        import jax, jax.numpy as jnp
        import numpy as np
        B, T, D_MODEL, N_HEADS = (2, 512, 256, 16)
        key = jax.random.key(seed)
        ks = jax.random.split(key, 5)
        w_scale = 0.02
        return {'x': jax.random.normal(ks[0], (B, T, D_MODEL), jnp.float32), 'Wq': jax.random.normal(ks[1], (D_MODEL, D_MODEL), jnp.float32) * w_scale, 'Wk': jax.random.normal(ks[2], (D_MODEL, D_MODEL), jnp.float32) * w_scale, 'Wv': jax.random.normal(ks[3], (D_MODEL, D_MODEL), jnp.float32) * w_scale, 'Wo': jax.random.normal(ks[4], (D_MODEL, D_MODEL), jnp.float32) * w_scale}
    _L0_attn_a_in = _L0_attn_a_setup()

    def _L0_attn_b_setup():
        import jax, jax.numpy as jnp
        import numpy as np
        BSZ, SEQ, EMBED = (2, 1024, 256)
        NUM_HEADS = 16
        HEAD_DIM = EMBED // NUM_HEADS
        WINDOW = 64

        def _blocks3(x, nb, w):
            b = x.shape[0]
            xb = x.reshape(b, nb + 2, w, NUM_HEADS, HEAD_DIM)
            return jnp.concatenate([xb[:, i:i + nb] for i in range(3)], axis=2)
        key = jax.random.key(seed)
        ks = jax.random.split(key, 7)
        s = 1.0 / np.sqrt(EMBED)
        return {'hidden_states': jax.random.normal(ks[0], (BSZ, SEQ, EMBED), jnp.float32), 'Wq': jax.random.normal(ks[1], (EMBED, EMBED), jnp.float32) * s, 'bq': jnp.zeros((EMBED,), jnp.float32), 'Wk': jax.random.normal(ks[2], (EMBED, EMBED), jnp.float32) * s, 'bk': jnp.zeros((EMBED,), jnp.float32), 'Wv': jax.random.normal(ks[3], (EMBED, EMBED), jnp.float32) * s, 'bv': jnp.zeros((EMBED,), jnp.float32)}
    _L0_attn_b_in = _L0_attn_b_setup()

    def _L0_ffn_setup():
        import jax, jax.numpy as jnp
        import numpy as np
        DIM = 256

        def _reference_tuple_inner(x, W_r, W_k, W_v, mu_r, mu_k):
            B, T, C = x.shape
            x_prev = jnp.concatenate([jnp.zeros((B, 1, C), x.dtype), x[:, :-1, :]], axis=1)
            xr = mu_r * x + (1.0 - mu_r) * x_prev
            xk = mu_k * x + (1.0 - mu_k) * x_prev
            r = jax.nn.sigmoid(jnp.einsum('btc,dc->btd', xr, W_r))
            k = jnp.einsum('btc,dc->btd', xk, W_k)
            k_act = jnp.square(jax.nn.relu(k))
            out = r * jnp.einsum('btc,dc->btd', k_act, W_v)
            new_state = x[:, -1, :]
            return (out, new_state)
        key = jax.random.key(seed)
        ks = jax.random.split(key, 6)
        B, T, C = (8, 512, DIM)
        x = jax.random.normal(ks[0], (B, T, C), dtype=jnp.float32)
        s = 1.0 / np.sqrt(C)
        W_r = jax.random.uniform(ks[1], (C, C), jnp.float32, -s, s)
        W_k = jax.random.uniform(ks[2], (C, C), jnp.float32, -s, s)
        W_v = jax.random.uniform(ks[3], (C, C), jnp.float32, -s, s)
        mu_r = jax.random.uniform(ks[4], (C,), jnp.float32)
        mu_k = jax.random.uniform(ks[5], (C,), jnp.float32)
        return {'x': x, 'W_r': W_r, 'W_k': W_k, 'W_v': W_v, 'mu_r': mu_r, 'mu_k': mu_k}
    _L0_ffn_in = _L0_ffn_setup()
    _d = {'L0_attn_a_x': _L0_attn_a_in['x'], 'L0_attn_a_Wq': _L0_attn_a_in['Wq'], 'L0_attn_a_Wk': _L0_attn_a_in['Wk'], 'L0_attn_a_Wv': _L0_attn_a_in['Wv'], 'L0_attn_a_Wo': _L0_attn_a_in['Wo'], 'L0_attn_b_Wq': _L0_attn_b_in['Wq'], 'L0_attn_b_bq': _L0_attn_b_in['bq'], 'L0_attn_b_Wk': _L0_attn_b_in['Wk'], 'L0_attn_b_bk': _L0_attn_b_in['bk'], 'L0_attn_b_Wv': _L0_attn_b_in['Wv'], 'L0_attn_b_bv': _L0_attn_b_in['bv'], 'L0_ffn_W_r': _L0_ffn_in['W_r'], 'L0_ffn_W_k': _L0_ffn_in['W_k'], 'L0_ffn_W_v': _L0_ffn_in['W_v'], 'L0_ffn_mu_r': _L0_ffn_in['mu_r'], 'L0_ffn_mu_k': _L0_ffn_in['mu_k']}
    _x0 = _d['L0_attn_a_x']
    _d['L0_attn_a_x'] = jax.random.normal(jax.random.fold_in(jax.random.key(seed), 1), (4, 2048, 256), dtype=_x0.dtype)
    del _x0
    return _d

def reference(L0_attn_a_x, L0_attn_a_Wq, L0_attn_a_Wk, L0_attn_a_Wv, L0_attn_a_Wo, L0_attn_b_Wq, L0_attn_b_bq, L0_attn_b_Wk, L0_attn_b_bk, L0_attn_b_Wv, L0_attn_b_bv, L0_ffn_W_r, L0_ffn_W_k, L0_ffn_W_v, L0_ffn_mu_r, L0_ffn_mu_k):

    def _L0_attn_a_ref(x, Wq, Wk, Wv, Wo):
        import jax, jax.numpy as jnp
        import numpy as np
        B, T, D_MODEL, N_HEADS = (2, 512, 256, 16)
        Bv, Tv, _ = x.shape
        H = N_HEADS
        D = D_MODEL // H
        q = (x @ Wq.T).reshape(Bv, Tv, H, D).transpose(0, 2, 1, 3)
        k = (x @ Wk.T).reshape(Bv, Tv, H, D).transpose(0, 2, 1, 3)
        v = (x @ Wv.T).reshape(Bv, Tv, H, D).transpose(0, 2, 1, 3)
        scale = jnp.sqrt(jnp.asarray(D, jnp.float32))
        scores = jnp.einsum('bhqd,bhkd->bhqk', q, k) / scale
        slopes = jnp.asarray([2.0 ** (-8.0 * h / H) for h in range(1, H + 1)], jnp.float32)
        pos = jnp.arange(Tv)
        dist = jnp.abs(pos[None, :] - pos[:, None]).astype(jnp.float32)
        bias = -dist[None, :, :] * slopes[:, None, None]
        causal_mask = jnp.triu(jnp.ones((Tv, Tv), dtype=bool), 1)
        bias = jnp.where(causal_mask[None, :, :], -jnp.inf, bias)
        scores = scores + bias[None]
        attn = jax.nn.softmax(scores, axis=-1)
        out = jnp.einsum('bhqk,bhkd->bhqd', attn, v)
        out = out.transpose(0, 2, 1, 3).reshape(Bv, Tv, D_MODEL)
        return out @ Wo.T

    def _L0_attn_b_ref(hidden_states, Wq, bq, Wk, bk, Wv, bv):
        import jax, jax.numpy as jnp
        import numpy as np
        BSZ, SEQ, EMBED = (2, 1024, 256)
        NUM_HEADS = 16
        HEAD_DIM = EMBED // NUM_HEADS
        WINDOW = 64

        def _blocks3(x, nb, w):
            b = x.shape[0]
            xb = x.reshape(b, nb + 2, w, NUM_HEADS, HEAD_DIM)
            return jnp.concatenate([xb[:, i:i + nb] for i in range(3)], axis=2)
        b, s, e = hidden_states.shape
        w = WINDOW
        nb = s // w
        q = (hidden_states @ Wq + bq) * (1.0 / np.sqrt(HEAD_DIM))
        k = hidden_states @ Wk + bk
        v = hidden_states @ Wv + bv
        q = q.reshape(b, nb, w, NUM_HEADS, HEAD_DIM)
        k = k.reshape(b, s, NUM_HEADS, HEAD_DIM)
        v = v.reshape(b, s, NUM_HEADS, HEAD_DIM)
        pad = ((0, 0), (w, w), (0, 0), (0, 0))
        kb = _blocks3(jnp.pad(k, pad), nb, w)
        vb = _blocks3(jnp.pad(v, pad), nb, w)
        scores = jnp.einsum('bnxhd,bnyhd->bnhxy', q, kb)
        x_idx = jnp.arange(w)
        y_idx = jnp.arange(3 * w)
        band = jnp.abs(y_idx[None, :] - x_idx[:, None] - w) <= w
        kpos = jnp.arange(nb)[:, None] * w - w + y_idx[None, :]
        inb = (kpos >= 0) & (kpos < s)
        mask = band[None, :, :] & inb[:, None, :]
        scores = jnp.where(mask[None, :, None, :, :], scores, -jnp.inf)
        probs = jax.nn.softmax(scores.astype(jnp.float32), axis=-1).astype(v.dtype)
        attn = jnp.einsum('bnhxy,bnyhd->bnxhd', probs, vb)
        return attn.reshape(b, s, e)

    def _L0_ffn_ref(x, W_r, W_k, W_v, mu_r, mu_k):
        import jax, jax.numpy as jnp
        import numpy as np
        DIM = 256

        def _reference_tuple_inner(x, W_r, W_k, W_v, mu_r, mu_k):
            B, T, C = x.shape
            x_prev = jnp.concatenate([jnp.zeros((B, 1, C), x.dtype), x[:, :-1, :]], axis=1)
            xr = mu_r * x + (1.0 - mu_r) * x_prev
            xk = mu_k * x + (1.0 - mu_k) * x_prev
            r = jax.nn.sigmoid(jnp.einsum('btc,dc->btd', xr, W_r))
            k = jnp.einsum('btc,dc->btd', xk, W_k)
            k_act = jnp.square(jax.nn.relu(k))
            out = r * jnp.einsum('btc,dc->btd', k_act, W_v)
            new_state = x[:, -1, :]
            return (out, new_state)
        return _reference_tuple_inner(x, W_r, W_k, W_v, mu_r, mu_k)[0]
    x = L0_attn_a_x
    x = x + _L0_attn_a_ref(_layernorm(x, axis=-1), L0_attn_a_Wq, L0_attn_a_Wk, L0_attn_a_Wv, L0_attn_a_Wo)
    x = x + _L0_ffn_ref(_layernorm(x, axis=-1), L0_ffn_W_r, L0_ffn_W_k, L0_ffn_W_v, L0_ffn_mu_r, L0_ffn_mu_k)
    x = x + _L0_attn_b_ref(_layernorm(x, axis=-1), L0_attn_b_Wq, L0_attn_b_bq, L0_attn_b_Wk, L0_attn_b_bk, L0_attn_b_Wv, L0_attn_b_bv)
    x = x + _L0_ffn_ref(_layernorm(x, axis=-1), L0_ffn_W_r, L0_ffn_W_k, L0_ffn_W_v, L0_ffn_mu_r, L0_ffn_mu_k)
    return x

_drawn_inputs = setup_inputs


def setup_inputs(seed=0):
    import zlib

    import numpy as np

    out = dict(_drawn_inputs(seed))
    spreads = {'L0_attn_b_bq': (0.0, 0.519), 'L0_attn_b_bk': (0.0, 0.8), 'L0_attn_b_bv': (0.0, 0.1)}
    factors = {'L0_attn_a_Wq': 8.0, 'L0_attn_a_Wk': 8.0, 'L0_ffn_mu_r': 3.277}
    for name, (base, spread) in spreads.items():
        noise = np.random.default_rng([zlib.crc32(name.encode()), seed]).standard_normal(out[name].shape)
        drawn = base * np.exp(spread * noise) if base else spread * noise
        out[name] = jnp.asarray(drawn.astype(out[name].dtype))
    for name, factor in factors.items():
        out[name] = (out[name] * factor).astype(out[name].dtype)
    return out
```

```python
from contextlib import ExitStack

import concourse.bass as bass
from concourse import mybir

F32 = mybir.dt.float32
BF16 = mybir.dt.bfloat16
ALU = mybir.AluOpType
ACT = mybir.ActivationFunctionType
AX = mybir.AxisListType

P = 128
B, T, C = 4, 2048, 256
H, D = 16, 16
CH = C // P
NK = 4
TC = T // NK
NJ = TC // P
G = 4
HG = H // G
VW = 32
TILES = T // P
W = 64
EPS = 1e-5
NEG = -1e30

Q_PART = [0, 0, 1, 1, 0, 2]
K_PART = [0, 1, 0, 1, 2, 0]
NPROD = len(Q_PART) * D
POS_STEP = 256
NPOS = T // POS_STEP * 3 + 3
FULL_ROWS = NPROD + NPOS + 3
BAND_ROWS = NPROD + 3


def start_at_one(eng, *semaphores):
    for s in semaphores:
        eng.sem_inc(s, 1)


def over_batches(eng, body):
    with eng.Fori(0, B - 1) as b:
        body(b, False)
    body(B - 1, True)


def project(nc, stage, consts, x, wq, wk, wv, bias, qk_parts, v_rows):
    with ExitStack() as ctx:
        def sb(name, shape, dt=F32):
            return ctx.enter_context(nc.sbuf_tensor(f"{stage}_{name}", shape, dt))

        def sem(name):
            return ctx.enter_context(nc.semaphore(f"{stage}_{name}"))

        def psum(name, shape):
            return ctx.enter_context(nc.psum_tensor(f"{stage}_{name}", shape, F32))

        w_sb = [sb(f"w{n}_sb", [P, CH, C]) for n in "qkv"]
        qk_bias = sb("qk_bias", [P, 2, CH])
        v_bias = sb("v_bias", [P, C])
        ident = sb("ident", [P, P])
        zeros = sb("zeros", [W, H * VW])
        xt = sb("xt", [P, 2, NJ, C])
        stats = sb("stats", [P, 2, NJ, 6])
        meanvar = sb("meanvar", [P, 2, NJ, 2])
        vareps = sb("vareps", [P, 2, NJ])
        held = sb("held", [P, 1])
        power = sb("power", [P, NJ])
        eps = sb("eps", [P, NJ])
        rstd = sb("rstd", [P, 2, NJ])
        xn = sb("xn", [P, 2, NJ, C])
        xnT = sb("xnT", [P, 2, CH, TC])
        full = sb("full", [P, 4, TC])
        rest = sb("rest", [P, 4, TC])
        parts = sb("parts", [P, 4, 3, TC], BF16)
        vst = sb("vst", [P, 2, NJ, H, VW])
        pT = psum("pT", [P, CH, TC])
        pQK = psum("pQK", [P, 4, TC])
        pV = psum("pV", [P, 2, 2, C])

        w_loaded = sem("w_loaded")
        x_loaded = [sem(f"x_loaded{i}") for i in range(2)]
        const_set = sem("const_set")
        stats_done = sem("stats_done")
        aggr_done = sem("aggr_done")
        vareps_done = sem("vareps_done")
        rstd_done = sem("rstd_done")
        xn_done = sem("xn_done")
        xT_ready = sem("xT_ready")
        xnT_done = sem("xnT_done")
        qk_ready = sem("qk_ready")
        full_done = sem("full_done")
        high_done = sem("high_done")
        rest_done = sem("rest_done")
        mid_done = sem("mid_done")
        low_done = sem("low_done")
        v_ready = sem("v_ready")
        v_done = sem("v_done")
        qk_stored = [sem(f"qk_stored{i}") for i in range(4)]
        v_stored = [sem(f"v_stored{i}") for i in range(2)]
        pad_stored = sem("pad_stored")
        n_w = 4 if bias is None else 7

        block = ctx.enter_context(nc.Block())

        @block.sync
        def _(sp):
            start_at_one(sp, *qk_stored, *v_stored)
            def load_x(b, k):
                sp.dma_start(xt[:, k % 2], x[b, k * TC:(k + 1) * TC, :].rearrange(
                    "(j p) c -> p j c", p=P)).then_inc(x_loaded[k % 2], 16)

            load_x(0, 0)
            sp.dma_start(ident[:], consts["ident"]).then_inc(w_loaded, 16)
            for w, src in zip(w_sb, (wq, wk, wv)):
                sp.dma_start(w[:], src.rearrange("(h p) d -> p h d", p=P)).then_inc(w_loaded, 16)
            if bias is not None:
                with nc.allow_non_contiguous_dma(reason="256 biases, one a partition"):
                    for n in range(2):
                        sp.dma_start(qk_bias[:, n], bias[n].rearrange("(h p) -> p h", p=P)).then_inc(w_loaded, 16)
                sp.dma_start(v_bias[:], bias[2].rearrange("(a c) -> a c", a=1).to_broadcast([P, C])
                             ).then_inc(w_loaded, 16)
            load_x(0, 1)
            sp.wait_ge(const_set, 4)
            for b in range(B):
                for at in (0, W + T):
                    sp.dma_start(v_rows[b, at:at + W].rearrange("t h d -> t (h d)"), zeros[:]
                                 ).then_inc(pad_stored, 16)

            def body(b, last):
                for k in range(NK):
                    c = b * NK + k
                    if not (last and k + 2 >= NK):
                        sp.wait_ge(xn_done, c + 1)
                        load_x(b + (k + 2) // NK, (k + 2) % NK)
                    for i in range(4):
                        sp.wait_ge(low_done, 1 + 4 * c + i + 1)
                        sp.dma_start(qk_parts[i // 2, b, :, i % 2 * P:(i % 2 + 1) * P, k * TC:(k + 1) * TC]
                                     .rearrange("s p t -> p s t"), parts[:, i]).then_inc(qk_stored[i], 16)
                    sp.wait_ge(v_done, 1 + 2 * c + 2)
                    sp.dma_start(v_rows[b, W + k * TC:W + (k + 1) * TC].rearrange("(j p) h d -> p j (h d)", p=P),
                                 vst[:, k % 2].rearrange("p j h d -> p j (h d)")).then_inc(v_stored[k % 2], 16)

            over_batches(sp, body)
            for s in qk_stored:
                sp.wait_ge(s, 1 + 16 * B * NK)
            for s in v_stored:
                sp.wait_ge(s, 1 + 16 * B * NK // 2)
            sp.wait_ge(pad_stored, 16 * B * 2)

        @block.gpsimd
        def _(pool):
            start_at_one(pool, low_done)
            pool.memset(eps[:], EPS)
            pool.memset(power[:], -0.5).then_inc(const_set, 1)
            pool.memset(zeros[:], 0.0).then_inc(const_set, 1)
            for i in range(2):
                pool.memset(vst[:, i, :, :, D:VW], 0.0)
            pool.memset(rest[:, 0, 0:1], 0.0).then_inc(const_set, 1)
            pool.wait_ge(const_set, 3)
            for i in range(2):
                last = pool.memset(vst[:, i, :, :, D:D + 1], 1.0)
            last.then_inc(const_set, 1)

            def norm(c, k):
                pool.wait_ge(aggr_done, c + 1)
                pool.tensor_tensor(vareps[:, k % 2], meanvar[:, k % 2, :, 1], eps[:], ALU.add).then_inc(vareps_done, 1)
                pool.wait_ge(vareps_done, c + 1)
                pool.tensor_tensor(rstd[:, k % 2], vareps[:, k % 2], power[:], ALU.pow).then_inc(rstd_done, 1)

            norm(0, 0)

            def body(b, last):
                for k in range(NK):
                    c = b * NK + k
                    if not (last and k == NK - 1):
                        norm(c + 1, k + 1)

                    def take_high(i):
                        pool.wait_ge(high_done, 4 * c + i + 1)
                        pool.tensor_tensor(rest[:, i], full[:, i], parts[:, i, 0], ALU.subtract
                                           ).then_inc(rest_done, 1)

                    def take_mid(i):
                        pool.wait_ge(mid_done, 4 * c + i + 1)
                        pool.tensor_tensor(parts[:, i, 2], rest[:, i], parts[:, i, 1], ALU.subtract
                                           ).then_inc(low_done, 1)

                    take_high(0)
                    for i in range(1, 4):
                        take_high(i)
                        take_mid(i - 1)
                    take_mid(3)

            over_batches(pool, body)

        @block.vector
        def _(dve):
            start_at_one(dve, full_done, v_done)
            if bias is None:
                dve.memset(qk_bias[:], 0.0)
                dve.memset(v_bias[:], 0.0).then_inc(stats_done, 1)
                dve.wait_ge(stats_done, 1)
            first = 1 if bias is None else 0

            def norm(c, k, turn):
                dve.wait_ge(x_loaded[k % 2], 16 * turn)
                for j in range(NJ):
                    dve.bn_stats(stats[:, k % 2, j], xt[:, k % 2, j]).then_inc(stats_done, 1)
                dve.wait_ge(stats_done, first + NJ * (c + 1))
                dve.memset(held[:], 0.0)
                for j in range(NJ):
                    last = dve.bn_aggr(meanvar[:, k % 2, j], stats[:, k % 2, j])
                last.then_inc(aggr_done, 1)
                dve.wait_ge(rstd_done, c + 1)
                if not (isinstance(c, int) and c == 0):
                    dve.wait_ge(xT_ready, 1 + 2 * (c - 1))
                for j in range(NJ):
                    last = dve.tensor_scalar(xn[:, k % 2, j], xt[:, k % 2, j], meanvar[:, k % 2, j, 0:1],
                                             rstd[:, k % 2, j:j + 1], ALU.subtract, ALU.mult)
                last.then_inc(xn_done, 1)

            norm(0, 0, 1)
            dve.wait_ge(w_loaded, 16 * n_w)
            dve.wait_ge(const_set, 4)

            def body(b, last):
                for k in range(NK):
                    c = b * NK + k
                    if not (last and k == NK - 1):
                        norm(c + 1, k + 1, b * (NK // 2) + (k + 1) // 2 + 1)
                    for i in range(4):
                        dve.wait_ge(qk_ready, 4 * c + i + 1)
                        dve.wait_ge(low_done, 1 + 4 * c)
                        dve.tensor_scalar(full[:, i], pQK[:, i], qk_bias[:, i // 2, i % 2:i % 2 + 1],
                                          0.25 if i < 2 else 1.0, ALU.add, ALU.mult).then_inc(full_done, 1)
                    for n in range(2):
                        dve.wait_ge(v_ready, 1 + 2 * c + n + 1)
                        if n == 0:
                            dve.wait_ge(v_stored[k % 2], 1 + 16 * (b * (NK // 2) + k // 2))
                        for j in range(2):
                            op = dve.tensor_tensor(
                                vst[:, k % 2, 2 * n + j, :, 0:D], pV[:, n, j].rearrange("p (h d) -> p h d", d=D),
                                v_bias[:].rearrange("p (h d) -> p h d", d=D), ALU.add)
                        op.then_inc(v_done, 1)

            over_batches(dve, body)

        @block.scalar
        def _(act):
            def copy_T(c, k):
                for h in range(CH):
                    act.wait_ge(xT_ready, 1 + 2 * c + h + 1)
                    if h == 0 and not (isinstance(c, int) and c == 0):
                        act.wait_ge(v_ready, 1 + 2 * (c - 1))
                    act.activation(xnT[:, k % 2, h], pT[:, h], ACT.Copy).then_inc(xnT_done, 1)

            copy_T(0, 0)

            def body(b, last):
                for k in range(NK):
                    c = b * NK + k

                    def high(i):
                        act.wait_ge(full_done, 1 + 4 * c + i + 1)
                        act.wait_ge(qk_stored[i], 1 + 16 * c)
                        act.activation(parts[:, i, 0], full[:, i], ACT.Copy).then_inc(high_done, 1)

                    def mid(i):
                        act.wait_ge(rest_done, 4 * c + i + 1)
                        act.activation(parts[:, i, 1], rest[:, i], ACT.Copy).then_inc(mid_done, 1)

                    high(0)
                    for i in range(1, 4):
                        high(i)
                        mid(i - 1)
                    mid(3)
                    if not (last and k == NK - 1):
                        copy_T(c + 1, k + 1)

            over_batches(act, body)

        @block.tensor
        def _(pe):
            start_at_one(pe, xT_ready, v_ready)
            pe.wait_ge(w_loaded, 16 * n_w)

            def transpose(c, k):
                pe.wait_ge(xn_done, c + 1)
                pe.wait_ge(xnT_done, 2 * c)
                for h in range(CH):
                    for j in range(NJ):
                        last = pe.transpose(pT[:, h, j * P:(j + 1) * P], xn[:, k % 2, j, h * P:(h + 1) * P], ident[:])
                    last.then_inc(xT_ready, 1)

            transpose(0, 0)

            def body(b, last):
                for k in range(NK):
                    c = b * NK + k
                    pe.wait_ge(xnT_done, 2 * c + 2)
                    pe.wait_ge(full_done, 1 + 4 * c)
                    for i in range(4):
                        for h in range(CH):
                            mm = pe.matmul(pQK[:, i], w_sb[i // 2][:, h, i % 2 * P:(i % 2 + 1) * P],
                                           xnT[:, k % 2, h], start=(h == 0), stop=(h == CH - 1))
                        mm.then_inc(qk_ready, 1)
                    if not (last and k == NK - 1):
                        transpose(c + 1, k + 1)
                    pe.wait_ge(v_done, 1 + 2 * c)
                    for n in range(2):
                        for j in range(2):
                            t = 2 * n + j
                            for h in range(CH):
                                mm = pe.matmul(pV[:, n, j], xnT[:, k % 2, h, t * P:(t + 1) * P],
                                               w_sb[2][:, h], start=(h == 0), stop=(h == CH - 1))
                        mm.then_inc(v_ready, 1)

            over_batches(pe, body)


CHUNK_ENDS = [NJ * (q + 1) * (q + 2) // 2 - 1 for q in range(NK)]
UNITS = CHUNK_ENDS[-1] + 1
UNIT = [(q, t) for q in range(NK) for t in range(NJ * (q + 1))]
PIECES = [(h, t, s) for t in range(TILES) for s in range(t // NJ + 1) for h in range(HG)]
PIECES_A_UNIT = 5
MAX_AT = len(PIECES) // PIECES_A_UNIT
FLIP_AT = MAX_AT + 2
AUX = NK + 1


def aux_count(n, q, flipped):
    return AUX * n + 1 + q + flipped


def attend_full(nc, stage, consts, qk_parts, v_rows, o_rows):
    with ExitStack() as ctx:
        def sb(name, shape, dt=F32):
            return ctx.enter_context(nc.sbuf_tensor(f"{stage}_{name}", shape, dt))

        def sem(name):
            return ctx.enter_context(nc.semaphore(f"{stage}_{name}"))

        def psum(name, shape):
            return ctx.enter_context(nc.psum_tensor(f"{stage}_{name}", shape, F32))

        q_op = [sb(f"q_op{g}", [FULL_ROWS, HG, T], BF16) for g in range(G)]
        k_op = [sb(f"k_op{g}", [FULL_ROWS, HG, T], BF16) for g in range(G)]
        v_sb = [sb(f"v_sb{i}", [P, TILES, HG, VW]) for i in range(2)]
        probs = sb("probs", [P, 2, HG, TC])
        ident = sb("ident", [P, P])
        identb = sb("identb", [P, P], BF16)
        mask_q = sb("mask_q", [P, P], BF16)
        mask_k = sb("mask_k", [P, P], BF16)
        spread = sb("spread", [P, P])
        maxes = sb("maxes", [P, HG, TILES, NK])
        negmax = sb("negmax", [P, P])
        max_rest = sb("max_rest", [HG * TILES, 2, P])
        max_parts = sb("max_parts", [HG * TILES, 3, P], BF16)
        o_sb = sb("o_sb", [P, TC])
        inv = sb("inv", [P, TC])
        o_norm = sb("o_norm", [P, TC])
        pS = psum("pS", [P, 2, 2, TC])
        pM = psum("pM", [P, 2, TC])
        pO = psum("pO", [P, TC])
        pX = psum("pX", [P, TC])

        c_loaded = sem("c_loaded")
        qk_loaded = [sem(f"qk_loaded{g}") for g in range(G)]
        v_loaded = [sem(f"v_loaded{i}") for i in range(2)]
        max_loaded = sem("max_loaded")
        maxes_set = sem("maxes_set")
        s_ready = sem("s_ready")
        p_ready = sem("p_ready")
        p_used = sem("p_used")
        m_ready = sem("m_ready")
        m_used = sem("m_used")
        negmax_done = sem("negmax_done")
        split_step = sem("split_step")
        o_copied = sem("o_copied")
        aux_ready = sem("aux_ready")
        aux_free = sem("aux_free")
        o_done = sem("o_done")
        o_stored = sem("o_stored")
        N_C, N_QK = 5 + 2 * G, 13

        block = ctx.enter_context(nc.Block())

        @block.sync
        def _(sp):
            start_at_one(sp, o_stored)
            def load_qk(b, g):
                heads = slice(g * HG * D, (g + 1) * HG * D)
                for s in range(6):
                    for n, (dst, part) in enumerate(((q_op, Q_PART), (k_op, K_PART))):
                        sp.dma_start(dst[g][s * D:(s + 1) * D], qk_parts[n, b, part[s], heads].rearrange(
                            "(h d) t -> d h t", d=D)).then_inc(qk_loaded[g], 16)
                sp.dma_start(q_op[g][NPROD:NPROD + NPOS], consts["slopes"][g * HG:(g + 1) * HG].rearrange(
                    "h r t -> r h t")).then_inc(qk_loaded[g], 16)

            def load_v(b, g):
                sp.dma_start(v_sb[g % 2][:].rearrange("p t h d -> p t (h d)"),
                             v_rows[b, W:W + T, g * HG:(g + 1) * HG].rearrange("(t p) h d -> p t (h d)", p=P)
                             ).then_inc(v_loaded[g % 2], 16)

            for dst, name in ((ident, "ident"), (identb, "identb"), (mask_q, "mask_q"),
                              (mask_k, "mask_k"), (spread, "spread")):
                sp.dma_start(dst[:], consts[name]).then_inc(c_loaded, 16)
            for g in range(G):
                for half in range(2):
                    sp.dma_start(k_op[g][NPROD:FULL_ROWS, 2 * half:2 * half + 2], consts["positions"].rearrange(
                        "r (a t) -> r a t", a=1).to_broadcast([NPOS + 3, 2, T])).then_inc(c_loaded, 16)
            load_qk(0, 0)
            load_qk(0, 1)
            load_v(0, 0)
            load_v(0, 1)
            load_qk(0, 2)
            load_qk(0, 3)

            def store_max(n, g):
                sp.wait_ge(split_step, 4 * n + 4)
                for s in range(3):
                    row = FULL_ROWS - 3 + s
                    sp.dma_start(q_op[g][row:row + 1].rearrange("r h (t q) -> r (h t) q", q=P),
                                 max_parts[:, s]).then_inc(max_loaded, 16)

            store_max(0, 0)

            def body(b, last):
                for g in range(G):
                    n = b * G + g
                    for q in range(NK):
                        if q == NK - 1 and not (last and g == G - 1):
                            store_max(n + 1, (g + 1) % G)
                        sp.wait_ge(o_done, 1 + NK * n + q + 1)
                        sp.dma_start(o_rows[b, g, :, q * TC:(q + 1) * TC], o_norm[:]).then_inc(o_stored, 16)
                    sp.wait_ge(p_used, UNITS * (n + 1) + 2)
                    if not last:
                        load_qk(b + 1, g)
                    if not (last and g >= 2):
                        load_v(b + (g + 2) // G, (g + 2) % G)

            over_batches(sp, body)
            sp.wait_ge(o_stored, 1 + 16 * B * G * NK)

        @block.gpsimd
        def _(pool):
            start_at_one(pool, o_done)
            pool.memset(negmax[:, HG * TILES:], 0.0)
            pool.memset(maxes[:], -3e38).then_inc(maxes_set, 1)

            def body(b, last):
                for g in range(G):
                    for q in range(NK):
                        i = (b * G + g) * NK + q
                        flipped = q == NK - 1 and not (last and g == G - 1)
                        pool.wait_ge(aux_free, aux_count(b * G + g, q, flipped) + 1)
                        pool.wait_ge(o_stored, 1 + 16 * i)
                        pool.tensor_tensor(o_norm[:], o_sb[:], inv[:], ALU.mult).then_inc(o_done, 1)

            over_batches(pool, body)

        @block.tensor
        def _(pe):
            pe.sem_inc(p_used, 2)
            pe.wait_ge(c_loaded, 16 * N_C)

            def piece(n, g, i):
                h, t, s = PIECES[i]
                w = min(TC, (t + 1) * P - s * TC)
                if not (isinstance(n, int) and n == 0 and i < 2):
                    pe.wait_ge(m_used, len(PIECES) * n + i - 1)
                diag = s == t // NJ
                mm = pe.matmul(pM[:, i % 2, 0:w], q_op[g][0:FULL_ROWS - 3, h, t * P:(t + 1) * P],
                               k_op[g][0:FULL_ROWS - 3, h, s * TC:s * TC + w], start=True, stop=not diag)
                if diag:
                    mm = pe.matmul(pM[:, i % 2, w - P:w], identb[:], mask_q[:], start=False, stop=True)
                mm.then_inc(m_ready, 1)

            def flip_maxima(n, uses):
                pe.wait_ge(negmax_done, n + 1)
                pe.wait_ge(aux_free, uses)
                pe.transpose(pX[:, 0:P], negmax[:], ident[:]).then_inc(aux_ready, 1)

            def spread_sums(n, q, uses):
                pe.wait_ge(o_copied, 1 + NK * n + q + 1)
                pe.wait_ge(aux_free, uses)
                pe.matmul(pX[:], spread[:], o_sb[:], start=True, stop=True).then_inc(aux_ready, 1)

            def scores(n, g, u):
                q, t = UNIT[u]
                lo = max(0, t * P - q * TC)
                for pair in range(2):
                    pe.wait_ge(p_ready, 2 * (UNITS * n + u) + pair + 1)
                    for a in range(2):
                        h = 2 * pair + a
                        diag = t * P >= q * TC
                        mm = pe.matmul(pS[:, pair, a, lo:TC], k_op[g][:, h, t * P:(t + 1) * P],
                                       q_op[g][:, h, q * TC + lo:(q + 1) * TC], start=True, stop=not diag)
                        if diag:
                            mm = pe.matmul(pS[:, pair, a, lo:lo + P], identb[:], mask_k[:], start=False, stop=True)
                    mm.then_inc(s_ready, 1)

            def values(n, g, u):
                q, t = UNIT[u]
                lo = max(0, t * P - q * TC)
                pe.wait_ge(p_ready, 2 * (UNITS * n + u + 1) + 2)
                if t == 0:
                    pe.wait_ge(o_copied, 1 + NK * n + q)
                for h in range(HG):
                    mm = pe.matmul(pO[VW * h:VW * (h + 1), lo:TC], v_sb[g % 2][:, t, h], probs[:, u % 2, h, lo:TC],
                                   start=(t == 0), stop=(u in CHUNK_ENDS))
                mm.then_inc(p_used, 1)

            pe.wait_ge(qk_loaded[0], 16 * N_QK)
            for i in range(len(PIECES)):
                piece(0, 0, i)
            flip_maxima(0, 0)

            def body(b, last):
                for g in range(G):
                    n = b * G + g
                    ahead = not (last and g == G - 1)
                    pe.wait_ge(max_loaded, 48 * (n + 1))
                    pe.wait_ge(v_loaded[g % 2], 16 * (b * 2 + g // 2 + 1))
                    if ahead:
                        pe.wait_ge(qk_loaded[(g + 1) % G], 16 * N_QK * (b + (g + 1) // G + 1))
                    for u in range(UNITS):
                        scores(n, g, u)
                        if ahead:
                            for i in range(u * PIECES_A_UNIT, min((u + 1) * PIECES_A_UNIT, len(PIECES))):
                                piece(n + 1, (g + 1) % G, i)
                        if u > 0:
                            values(n, g, u - 1)
                        if u >= 3 and u - 3 in CHUNK_ENDS:
                            q = CHUNK_ENDS.index(u - 3)
                            spread_sums(n, q, aux_count(n, q, 0))
                        if ahead and u == FLIP_AT:
                            flip_maxima(n + 1, aux_count(n, NK - 1, 0))
                    values(n, g, UNITS - 1)
                    spread_sums(n, NK - 1, aux_count(n, NK - 1, ahead))

            over_batches(pe, body)

        @block.scalar
        def _(act):
            act.sem_inc(p_ready, 2)

            def body(b, last):
                for g in range(G):
                    n = b * G + g
                    for u in range(UNITS):
                        q, t = UNIT[u]
                        lo = max(0, t * P - q * TC)
                        act.wait_ge(p_used, UNITS * n + u + 1)
                        for pair in range(2):
                            act.wait_ge(s_ready, 2 * (UNITS * n + u) + pair + 1)
                            act.activation(probs[:, u % 2, 2 * pair:2 * pair + 2, lo:TC], pS[:, pair, :, lo:TC],
                                           ACT.Exp).then_inc(p_ready, 1)

            over_batches(act, body)

        @block.vector
        def _(dve):
            start_at_one(dve, o_copied)
            def piece(n, i):
                h, t, s = PIECES[i]
                w = min(TC, (t + 1) * P - s * TC)
                dve.wait_ge(m_ready, len(PIECES) * n + i + 1)
                dve.reduce_max(maxes[:, h, t, s:s + 1], pM[:, i % 2, 0:w], AX.X).then_inc(m_used, 1)

            def finish_maxima(n):
                dve.wait_ge(m_used, len(PIECES) * (n + 1))
                dve.tensor_reduce(negmax[:, 0:HG * TILES], maxes[:].rearrange("p h t s -> p (h t) s"), AX.X, ALU.max,
                                  negate=True).then_inc(negmax_done, 1)

            def split_maxima(n, uses):
                split_rows(dve, n, uses, pX, max_parts, max_rest, aux_ready, aux_free, max_loaded, split_step)

            dve.wait_ge(maxes_set, 1)
            for i in range(len(PIECES)):
                piece(0, i)
            finish_maxima(0)
            split_maxima(0, 0)

            def copy_sums(n, q, done):
                dve.wait_ge(p_used, UNITS * n + done + 2)
                dve.wait_ge(o_done, 1 + NK * n + q)
                dve.tensor_copy(o_sb[:], pO[:]).then_inc(o_copied, 1)

            def invert(n, q, flipped):
                dve.wait_ge(aux_ready, aux_count(n, q, flipped) + 1)
                dve.reciprocal(inv[:], pX[:]).then_inc(aux_free, 1)

            def body(b, last):
                for g in range(G):
                    n = b * G + g
                    ahead = not (last and g == G - 1)
                    for u in range(UNITS):
                        if ahead:
                            for i in range(u * PIECES_A_UNIT, min((u + 1) * PIECES_A_UNIT, len(PIECES))):
                                piece(n + 1, i)
                        if u - 1 in CHUNK_ENDS:
                            copy_sums(n, CHUNK_ENDS.index(u - 1), u)
                        if u - 3 in CHUNK_ENDS:
                            invert(n, CHUNK_ENDS.index(u - 3), 0)
                        if ahead and u == MAX_AT:
                            finish_maxima(n + 1)
                        if ahead and u == FLIP_AT:
                            split_maxima(n + 1, aux_count(n, NK - 1, 0))
                    copy_sums(n, NK - 1, UNITS)
                    invert(n, NK - 1, ahead)

            over_batches(dve, body)


def split_rows(dve, n, uses, pX, max_parts, max_rest, aux_ready, aux_free, max_loaded, split_step):
    flipped = pX[0:HG * TILES, 0:P]
    dve.wait_ge(aux_ready, uses + 1)
    dve.wait_ge(max_loaded, 48 * n)
    dve.tensor_copy(max_parts[:, 0], flipped).then_inc(split_step, 1)
    dve.wait_ge(split_step, 4 * n + 1)
    dve.tensor_tensor(max_rest[:, 0], flipped, max_parts[:, 0], ALU.subtract).then_inc(aux_free, 1)
    dve.wait_ge(aux_free, uses + 1)
    dve.tensor_copy(max_parts[:, 1], max_rest[:, 0]).then_inc(split_step, 1)
    dve.wait_ge(split_step, 4 * n + 2)
    dve.tensor_tensor(max_rest[:, 1], max_rest[:, 0], max_parts[:, 1], ALU.subtract).then_inc(split_step, 1)
    dve.wait_ge(split_step, 4 * n + 3)
    dve.tensor_copy(max_parts[:, 2], max_rest[:, 1]).then_inc(split_step, 1)


KT = TILES + 1
BAND_PIECES = [(h, t) for t in range(0, TILES, 2) for h in range(HG)]
BAND_PIECES_A_STEP = 3
BAND_MAX_AT = len(BAND_PIECES) // BAND_PIECES_A_STEP + 1
BAND_FLIP_AT = BAND_MAX_AT + 2
RING = 4


def band_aux(n, q, ahead):
    return AUX * n + 1 + q + (1 if ahead and q >= 2 else 0)


def attend_band(nc, stage, consts, qk_parts, v_rows, o_rows):
    with ExitStack() as ctx:
        def sb(name, shape, dt=F32):
            return ctx.enter_context(nc.sbuf_tensor(f"{stage}_{name}", shape, dt))

        def sem(name):
            return ctx.enter_context(nc.semaphore(f"{stage}_{name}"))

        def psum(name, shape):
            return ctx.enter_context(nc.psum_tensor(f"{stage}_{name}", shape, F32))

        q_op = [sb(f"q_op{g}", [BAND_ROWS, HG, T], BF16) for g in range(G)]
        k_op = [sb(f"k_op{g}", [BAND_ROWS, HG, W + T + W], BF16) for g in range(G)]
        v_sb = [sb(f"v_sb{i}", [P, KT, HG, VW]) for i in range(2)]
        probs = sb("probs", [P, RING, HG, 2 * P])
        ident = sb("ident", [P, P])
        identb = sb("identb", [P, P], BF16)
        mask_q = sb("mask_q", [P, 3, 2, 2 * P], BF16)
        mask_k = sb("mask_k", [P, 3, 2, 2 * P], BF16)
        spread = sb("spread", [P, P])
        maxes = sb("maxes", [P, HG, TILES])
        negmax = sb("negmax", [P, P])
        max_rest = sb("max_rest", [HG * TILES, 2, P])
        max_parts = sb("max_parts", [HG * TILES, 3, P], BF16)
        o_sb = sb("o_sb", [P, TC])
        inv = sb("inv", [P, TC])
        o_norm = sb("o_norm", [P, TC])
        pS = psum("pS", [P, 2, HG, 2 * P])
        pM = psum("pM", [P, 2, 2, 2 * P])
        pO = psum("pO", [P, TC])
        pX = psum("pX", [P, TC])

        c_loaded = sem("c_loaded")
        pads_set = sem("pads_set")
        qk_loaded = [sem(f"qk_loaded{g}") for g in range(G)]
        v_loaded = [sem(f"v_loaded{i}") for i in range(2)]
        max_loaded = sem("max_loaded")
        s_ready = sem("s_ready")
        p_ready = sem("p_ready")
        o_ready = sem("o_ready")
        m_ready = sem("m_ready")
        m_used = sem("m_used")
        negmax_done = sem("negmax_done")
        split_step = sem("split_step")
        o_copied = sem("o_copied")
        aux_ready = sem("aux_ready")
        aux_free = sem("aux_free")
        o_done = sem("o_done")
        o_stored = sem("o_stored")
        N_C, N_QK = 5 + G, 12

        block = ctx.enter_context(nc.Block())

        @block.sync
        def _(sp):
            start_at_one(sp, o_stored)
            def load_qk(b, g):
                heads = slice(g * HG * D, (g + 1) * HG * D)
                for s in range(6):
                    sp.dma_start(q_op[g][s * D:(s + 1) * D], qk_parts[0, b, Q_PART[s], heads].rearrange(
                        "(h d) t -> d h t", d=D)).then_inc(qk_loaded[g], 16)
                    sp.dma_start(k_op[g][s * D:(s + 1) * D, :, W:W + T], qk_parts[1, b, K_PART[s], heads].rearrange(
                        "(h d) t -> d h t", d=D)).then_inc(qk_loaded[g], 16)

            def load_v(b, g):
                sp.dma_start(v_sb[g % 2][:].rearrange("p t h d -> p t (h d)"),
                             v_rows[b, :, g * HG:(g + 1) * HG].rearrange("(t p) h d -> p t (h d)", p=P)
                             ).then_inc(v_loaded[g % 2], 16)

            for dst, name in ((ident, "ident"), (identb, "identb"), (mask_q, "band_q"),
                              (mask_k, "band_k"), (spread, "spread")):
                sp.dma_start(dst[:], consts[name]).then_inc(c_loaded, 16)
            for g in range(G):
                sp.dma_start(k_op[g][NPROD:BAND_ROWS, :, W:W + T], consts["positions"][NPOS:NPOS + 3].rearrange(
                    "r (a t) -> r a t", a=1).to_broadcast([3, HG, T])).then_inc(c_loaded, 16)
            load_qk(0, 0)
            load_qk(0, 1)
            load_v(0, 0)
            load_v(0, 1)
            load_qk(0, 2)
            load_qk(0, 3)

            def store_max(n, g):
                sp.wait_ge(split_step, 4 * n + 4)
                for s in range(3):
                    row = BAND_ROWS - 3 + s
                    sp.dma_start(q_op[g][row:row + 1].rearrange("r h (t q) -> r (h t) q", q=P),
                                 max_parts[:, s]).then_inc(max_loaded, 16)

            store_max(0, 0)

            def body(b, last):
                for g in range(G):
                    n = b * G + g
                    for q in range(NK):
                        if q == 2 and not (last and g == G - 1):
                            store_max(n + 1, (g + 1) % G)
                        sp.wait_ge(o_done, 1 + NK * n + q + 1)
                        sp.dma_start(o_rows[b, g, :, q * TC:(q + 1) * TC], o_norm[:]).then_inc(o_stored, 16)
                    sp.wait_ge(o_ready, 1 + TILES * (n + 1))
                    if not last:
                        load_qk(b + 1, g)
                    if not (last and g >= 2):
                        load_v(b + (g + 2) // G, (g + 2) % G)

            over_batches(sp, body)
            sp.wait_ge(o_stored, 1 + 16 * B * G * NK)

        @block.gpsimd
        def _(pool):
            start_at_one(pool, o_done)
            pool.memset(negmax[:, HG * TILES:], 0.0)
            for g in range(G):
                pool.memset(k_op[g][:, :, 0:W], 0.0)
                last = pool.memset(k_op[g][:, :, W + T:], 0.0)
            last.then_inc(pads_set, 1)

            def body(b, last):
                for g in range(G):
                    ahead = not (last and g == G - 1)
                    for q in range(NK):
                        i = (b * G + g) * NK + q
                        pool.wait_ge(aux_free, band_aux(b * G + g, q, ahead) + 1)
                        pool.wait_ge(o_stored, 1 + 16 * i)
                        pool.tensor_tensor(o_norm[:], o_sb[:], inv[:], ALU.mult).then_inc(o_done, 1)

            over_batches(pool, body)

        @block.tensor
        def _(pe):
            start_at_one(pe, o_ready)
            pe.wait_ge(c_loaded, 16 * N_C)
            pe.wait_ge(pads_set, 1)

            def piece(n, g, i):
                h, t = BAND_PIECES[i]
                if not (isinstance(n, int) and n == 0 and i < 2):
                    pe.wait_ge(m_used, len(BAND_PIECES) * n + i - 1)
                edge = 0 if t == 0 else 2 if t == TILES - 2 else 1
                pe.matmul(pM[:, i % 2], identb[:], mask_q[:, edge], start=True, stop=False)
                for a in range(2):
                    mm = pe.matmul(pM[:, i % 2, a], q_op[g][0:NPROD, h, (t + a) * P:(t + a + 1) * P],
                                   k_op[g][0:NPROD, h, (t + a) * P:(t + a + 2) * P], start=False, stop=(a == 1))
                mm.then_inc(m_ready, 1)

            def flip_maxima(n, uses):
                pe.wait_ge(negmax_done, n + 1)
                pe.wait_ge(aux_free, uses)
                pe.transpose(pX[:, 0:P], negmax[:], ident[:]).then_inc(aux_ready, 1)

            def spread_sums(n, q, ahead):
                pe.wait_ge(o_copied, 1 + NK * n + q + 1)
                pe.wait_ge(aux_free, band_aux(n, q, ahead))
                pe.matmul(pX[:], spread[:], o_sb[:], start=True, stop=True).then_inc(aux_ready, 1)

            def scores(n, g, j):
                lo, hi = (P if j == 0 else 0), (P if j == KT - 1 else 2 * P)
                edge = 0 if j == 0 else 2 if j == KT - 1 else 1
                pe.wait_ge(p_ready, 1 + KT * n + max(j - 1, 0))
                for h in range(HG):
                    if h % 2 == 0:
                        pe.matmul(pS[:, j % 2, h:h + 2, lo:hi], identb[:], mask_k[:, edge, :, lo:hi],
                                  start=True, stop=False)
                    mm = pe.matmul(pS[:, j % 2, h, lo:hi], k_op[g][:, h, j * P:(j + 1) * P],
                                   q_op[g][:, h, (j - 1) * P + lo:(j - 1) * P + hi], start=False, stop=(h % 2 == 1))
                mm.then_inc(s_ready, 1)

            def values(n, g, t):
                pe.wait_ge(p_ready, 1 + KT * n + t + 2)
                if t % NJ == 0:
                    pe.wait_ge(o_copied, 1 + NK * n + t // NJ)
                for a in range(2):
                    for h in range(HG):
                        mm = pe.matmul(pO[VW * h:VW * (h + 1), t % NJ * P:(t % NJ + 1) * P], v_sb[g % 2][:, t + a, h],
                                       probs[:, (t + a) % RING, h, P * (1 - a):P * (2 - a)],
                                       start=(a == 0), stop=(a == 1))
                mm.then_inc(o_ready, 1)

            pe.wait_ge(qk_loaded[0], 16 * N_QK)
            for i in range(len(BAND_PIECES)):
                piece(0, 0, i)
            flip_maxima(0, 0)

            def body(b, last):
                for g in range(G):
                    n = b * G + g
                    ahead = not (last and g == G - 1)
                    pe.wait_ge(max_loaded, 48 * (n + 1))
                    pe.wait_ge(v_loaded[g % 2], 16 * (b * 2 + g // 2 + 1))
                    if ahead:
                        pe.wait_ge(qk_loaded[(g + 1) % G], 16 * N_QK * (b + (g + 1) // G + 1))
                    for j in range(KT):
                        scores(n, g, j)
                        if ahead:
                            for i in range(j * BAND_PIECES_A_STEP, min((j + 1) * BAND_PIECES_A_STEP,
                                                                       len(BAND_PIECES))):
                                piece(n + 1, (g + 1) % G, i)
                        if j >= 2:
                            values(n, g, j - 2)
                        if j >= NJ + 3 and (j - NJ - 3) % NJ == 0:
                            spread_sums(n, (j - NJ - 3) // NJ, ahead)
                        if ahead and j == BAND_FLIP_AT:
                            flip_maxima(n + 1, band_aux(n, 2, False))
                    values(n, g, TILES - 1)
                    spread_sums(n, NK - 1, ahead)

            over_batches(pe, body)

        @block.scalar
        def _(act):
            start_at_one(act, p_ready)
            def body(b, last):
                for g in range(G):
                    n = b * G + g
                    for j in range(KT):
                        lo, hi = (P if j == 0 else 0), (P if j == KT - 1 else 2 * P)
                        act.wait_ge(o_ready, 1 + TILES * n + max(j - RING + 1, 0))
                        act.wait_ge(s_ready, KT * n + j + 1)
                        act.activation(probs[:, j % RING, :, lo:hi], pS[:, j % 2, :, lo:hi],
                                       ACT.Exp).then_inc(p_ready, 1)

            over_batches(act, body)

        @block.vector
        def _(dve):
            start_at_one(dve, o_copied)
            def piece(n, i):
                h, t = BAND_PIECES[i]
                dve.wait_ge(m_ready, len(BAND_PIECES) * n + i + 1)
                dve.reduce_max(maxes[:, h, t:t + 2], pM[:, i % 2], AX.X).then_inc(m_used, 1)

            def finish_maxima(n):
                dve.wait_ge(m_used, len(BAND_PIECES) * (n + 1))
                dve.tensor_scalar(negmax[:, 0:HG * TILES], maxes[:].rearrange("p h t -> p (h t)"), -1.0, None, ALU.mult
                                  ).then_inc(negmax_done, 1)

            def split_maxima(n, uses):
                split_rows(dve, n, uses, pX, max_parts, max_rest, aux_ready, aux_free, max_loaded, split_step)

            for i in range(len(BAND_PIECES)):
                piece(0, i)
            finish_maxima(0)
            split_maxima(0, 0)

            def copy_sums(n, q):
                dve.wait_ge(o_ready, 1 + TILES * n + NJ * (q + 1))
                dve.wait_ge(o_done, 1 + NK * n + q)
                dve.tensor_copy(o_sb[:], pO[:]).then_inc(o_copied, 1)

            def invert(n, q, ahead):
                dve.wait_ge(aux_ready, band_aux(n, q, ahead) + 1)
                dve.reciprocal(inv[:], pX[:]).then_inc(aux_free, 1)

            def body(b, last):
                for g in range(G):
                    n = b * G + g
                    ahead = not (last and g == G - 1)
                    for j in range(KT):
                        if ahead:
                            for i in range(j * BAND_PIECES_A_STEP, min((j + 1) * BAND_PIECES_A_STEP,
                                                                       len(BAND_PIECES))):
                                piece(n + 1, i)
                        if j >= NJ + 1 and (j - NJ - 1) % NJ == 0:
                            copy_sums(n, (j - NJ - 1) // NJ)
                        if j >= NJ + 3 and (j - NJ - 3) % NJ == 0:
                            invert(n, (j - NJ - 3) // NJ, ahead)
                        if ahead and j == BAND_MAX_AT:
                            finish_maxima(n + 1)
                        if ahead and j == BAND_FLIP_AT:
                            split_maxima(n + 1, band_aux(n, 2, False))
                    copy_sums(n, NK - 1)
                    invert(n, NK - 1, ahead)

            over_batches(dve, body)


def mix(nc, stage, consts, x, o_rows, wo, wr, wk, wv, mu_r, mu_k, out):
    with ExitStack() as ctx:
        def sb(name, shape, dt=F32):
            return ctx.enter_context(nc.sbuf_tensor(f"{stage}_{name}", shape, dt))

        def sem(name):
            return ctx.enter_context(nc.semaphore(f"{stage}_{name}"))

        def psum(name, shape):
            return ctx.enter_context(nc.psum_tensor(f"{stage}_{name}", shape, F32))

        wr_sb, wk_sb, wv_sb = [sb(f"w{n}_sb", [P, CH, C]) for n in "rkv"]
        wo_sb = sb("wo_sb", [P, G, C])
        mu = sb("mu", [P, 2, CH])
        ident = sb("ident", [P, P])
        xt = sb("xt", [P, 2, NJ, C])
        ot = sb("ot", [P, 2, G, TC])
        x1 = sb("x1", [P, 2, NJ, C])
        stats = sb("stats", [P, 2, NJ, 6])
        meanvar = sb("meanvar", [P, 2, NJ, 2])
        vareps = sb("vareps", [P, 2, NJ])
        held = sb("held", [P, 1])
        power = sb("power", [P, NJ])
        eps = sb("eps", [P, NJ])
        rstd = sb("rstd", [P, 2, NJ])
        xn = sb("xn", [P, 2, NJ, C])
        xnT = sb("xnT", [P, 2, CH, TC + 1])
        step = sb("step", [P, CH, TC])
        zero = sb("zero", [P, CH, 1])
        xk = sb("xk", [P, CH, TC])
        xr = sb("xr", [P, CH, TC])
        relu = sb("relu", [P, CH, TC])
        act_k = sb("act_k", [P, CH, TC])
        gate = sb("gate", [P, 2, 2, C])
        prod = sb("prod", [P, 2, 2, C])
        x2 = sb("x2", [P, 2, NJ, C])
        pA = psum("pA", [P, 2, 2, C])
        pT = psum("pT", [P, CH, TC])
        pKV = psum("pKV", [P, 2, 2, C])
        pR = psum("pR", [P, 2, 2, C])

        w_loaded = sem("w_loaded")
        x_loaded = [sem(f"x_loaded{i}") for i in range(2)]
        const_set = sem("const_set")
        a_ready = sem("a_ready")
        x1_done = sem("x1_done")
        stats_done = sem("stats_done")
        aggr_done = sem("aggr_done")
        vareps_done = sem("vareps_done")
        rstd_done = sem("rstd_done")
        xn_done = sem("xn_done")
        xT_ready = sem("xT_ready")
        xnT_done = sem("xnT_done")
        edge_done = sem("edge_done")
        step_done = sem("step_done")
        blend_done = sem("blend_done")
        k_ready = sem("k_ready")
        relu_done = sem("relu_done")
        act_k_done = sem("act_k_done")
        r_ready = sem("r_ready")
        gate_done = sem("gate_done")
        mv_ready = sem("mv_ready")
        prod_done = sem("prod_done")
        x2_done = sem("x2_done")
        x_stored = [sem(f"x_stored{i}") for i in range(2)]
        N_W = 4 + 4 + 2
        rows = out.rearrange("b t c -> (b t) c")

        block = ctx.enter_context(nc.Block())

        @block.sync
        def _(sp):
            start_at_one(sp, *x_stored)
            def load(b, k):
                sp.dma_start(ot[:, k % 2], o_rows[b, :, :, k * TC:(k + 1) * TC].rearrange("g p t -> p g t")
                             ).then_inc(x_loaded[k % 2], 16)
                sp.dma_start(xt[:, k % 2], x[b, k * TC:(k + 1) * TC, :].rearrange("(j p) c -> p j c", p=P)
                             ).then_inc(x_loaded[k % 2], 16)

            load(0, 0)
            sp.wait_ge(const_set, 2)
            for a in range(HG):
                sp.dma_start(wo_sb[VW * a:VW * a + D], wo.rearrange("(g a d) n -> a d g n", a=HG, d=D)[a]
                             ).then_inc(w_loaded, 16)
            sp.dma_start(ident[:], consts["ident"]).then_inc(w_loaded, 16)
            for dst, src in ((wr_sb, wr), (wk_sb, wk), (wv_sb, wv)):
                sp.dma_start(dst[:], src.rearrange("(h p) d -> p h d", p=P)).then_inc(w_loaded, 16)
            with nc.allow_non_contiguous_dma(reason="256 factors, one a partition"):
                for n, src in enumerate((mu_k, mu_r)):
                    sp.dma_start(mu[:, n], src.rearrange("(h p) -> p h", p=P)).then_inc(w_loaded, 16)
            load(0, 1)

            def body(b, last):
                for k in range(NK):
                    c = b * NK + k
                    if not (last and k + 2 >= NK):
                        sp.wait_ge(x1_done, c + 1)
                        load(b + (k + 2) // NK, (k + 2) % NK)
                    sp.wait_ge(x2_done, 1 + 2 * c + 2)
                    sp.dma_start(rows[bass.ds(c * TC, TC), :].rearrange("(j p) c -> p j c", p=P), x2[:, k % 2]
                                 ).then_inc(x_stored[k % 2], 16)

            over_batches(sp, body)
            for s in x_stored:
                sp.wait_ge(s, 1 + 16 * B * NK // 2)

        @block.gpsimd
        def _(pool):
            start_at_one(pool, x2_done, act_k_done)
            pool.memset(eps[:], EPS)
            pool.memset(power[:], -0.5).then_inc(const_set, 1)
            pool.memset(zero[:], 0.0)
            pool.memset(wo_sb[:], 0.0).then_inc(const_set, 1)
            pool.wait_ge(const_set, 2)

            def norm(c, k):
                pool.wait_ge(aggr_done, c + 1)
                pool.tensor_tensor(vareps[:, k % 2], meanvar[:, k % 2, :, 1], eps[:], ALU.add).then_inc(vareps_done, 1)
                pool.wait_ge(vareps_done, c + 1)
                pool.tensor_tensor(rstd[:, k % 2], vareps[:, k % 2], power[:], ALU.pow).then_inc(rstd_done, 1)

            norm(0, 0)

            def body(b, last):
                for k in range(NK):
                    c = b * NK + k
                    pool.wait_ge(blend_done, 1 + 2 * c)
                    if k == 0:
                        pool.tensor_tensor(xnT[:, 0, :, 0:1], zero[:], zero[:], ALU.add).then_inc(edge_done, 1)
                    else:
                        pool.tensor_tensor(xnT[:, k % 2, :, 0:1], xnT[:, (k - 1) % 2, :, TC:TC + 1], zero[:],
                                           ALU.add).then_inc(edge_done, 1)
                    pool.wait_ge(edge_done, c + 1)
                    pool.wait_ge(xnT_done, 1 + 2 * c + 2)
                    pool.tensor_tensor(step[:], xnT[:, k % 2, :, 1:TC + 1], xnT[:, k % 2, :, 0:TC], ALU.subtract
                                       ).then_inc(step_done, 1)
                    if not (last and k == NK - 1):
                        norm(c + 1, k + 1)
                    pool.wait_ge(relu_done, 2 * c + 2)
                    pool.wait_ge(mv_ready, 1 + 2 * c)
                    pool.tensor_tensor(act_k[:], relu[:], relu[:], ALU.mult).then_inc(act_k_done, 1)
                    pool.wait_ge(x_stored[k % 2], 1 + 16 * (b * (NK // 2) + k // 2))
                    for n in range(2):
                        pool.wait_ge(prod_done, 1 + 2 * c + n + 1)
                        pool.tensor_tensor(x2[:, k % 2, 2 * n:2 * n + 2], x1[:, k % 2, 2 * n:2 * n + 2], prod[:, n],
                                           ALU.add).then_inc(x2_done, 1)

            over_batches(pool, body)

        @block.vector
        def _(dve):
            start_at_one(dve, blend_done, prod_done)
            def residual_norm(c, k, turn):
                first = isinstance(c, int) and c == 0
                dve.wait_ge(x_loaded[k % 2], 32 * turn)
                if not first:
                    dve.wait_ge(x2_done, 1 + 2 * (c - 1))
                for n in range(2):
                    dve.wait_ge(a_ready, 2 * c + n + 1)
                    last = dve.tensor_tensor(x1[:, k % 2, 2 * n:2 * n + 2], xt[:, k % 2, 2 * n:2 * n + 2], pA[:, n],
                                             ALU.add)
                last.then_inc(x1_done, 1)
                dve.wait_ge(x1_done, c + 1)
                for j in range(NJ):
                    last = dve.bn_stats(stats[:, k % 2, j], x1[:, k % 2, j])
                last.then_inc(stats_done, 1)
                dve.wait_ge(stats_done, c + 1)
                dve.memset(held[:], 0.0)
                for j in range(NJ):
                    last = dve.bn_aggr(meanvar[:, k % 2, j], stats[:, k % 2, j])
                last.then_inc(aggr_done, 1)
                dve.wait_ge(rstd_done, c + 1)
                if not first:
                    dve.wait_ge(xT_ready, 1 + 2 * (c - 1))
                for j in range(NJ):
                    last = dve.tensor_scalar(xn[:, k % 2, j], x1[:, k % 2, j], meanvar[:, k % 2, j, 0:1],
                                             rstd[:, k % 2, j:j + 1], ALU.subtract, ALU.mult)
                last.then_inc(xn_done, 1)

            residual_norm(0, 0, 1)
            dve.wait_ge(w_loaded, 16 * N_W)

            def body(b, last):
                for k in range(NK):
                    c = b * NK + k
                    dve.wait_ge(step_done, c + 1)
                    for n, (dst, used) in enumerate(((xk, k_ready), (xr, r_ready))):
                        dve.wait_ge(used, 1 + 2 * c)
                        for h in range(CH):
                            op = dve.scalar_tensor_tensor(
                                out=dst[:, h], in0=step[:, h], scalar=mu[:, n, h:h + 1], in1=xnT[:, k % 2, h, 0:TC],
                                op0=ALU.mult, op1=ALU.add)
                        op.then_inc(blend_done, 1)
                    if not (last and k == NK - 1):
                        residual_norm(c + 1, k + 1, b * (NK // 2) + (k + 1) // 2 + 1)
                    for n in range(2):
                        dve.wait_ge(gate_done, 1 + 2 * c + n + 1)
                        dve.wait_ge(mv_ready, 1 + 2 * c + n + 1)
                        dve.wait_ge(x2_done, 1 + 2 * c)
                        dve.tensor_tensor(prod[:, n], gate[:, n], pKV[:, n], ALU.mult).then_inc(prod_done, 1)

            over_batches(dve, body)

        @block.scalar
        def _(act):
            start_at_one(act, gate_done, xnT_done)
            def body(b, last):
                for k in range(NK):
                    c = b * NK + k
                    act.wait_ge(blend_done, 1 + 2 * c)
                    for h in range(CH):
                        act.wait_ge(xT_ready, 1 + 2 * c + h + 1)
                        act.activation(xnT[:, k % 2, h, 1:TC + 1], pT[:, h], ACT.Copy).then_inc(xnT_done, 1)
                    act.wait_ge(act_k_done, 1 + c)
                    for h in range(CH):
                        act.wait_ge(k_ready, 1 + 2 * c + h + 1)
                        act.activation(relu[:, h], pKV[:, h].rearrange("p a c -> p (a c)"), ACT.Relu
                                       ).then_inc(relu_done, 1)
                    act.wait_ge(prod_done, 1 + 2 * c)
                    for n in range(2):
                        act.wait_ge(r_ready, 1 + 2 * c + n + 1)
                        act.activation(gate[:, n], pR[:, n], ACT.Sigmoid).then_inc(gate_done, 1)

            over_batches(act, body)

        @block.tensor
        def _(pe):
            start_at_one(pe, xT_ready, k_ready, r_ready, mv_ready)
            pe.wait_ge(w_loaded, 16 * N_W)

            def project_heads(c, k, turn):
                pe.wait_ge(x_loaded[k % 2], 32 * turn)
                pe.wait_ge(x1_done, c)
                for n in range(2):
                    for a in range(2):
                        t = 2 * n + a
                        for g in range(G):
                            mm = pe.matmul(pA[:, n, a], ot[:, k % 2, g, t * P:(t + 1) * P], wo_sb[:, g],
                                           start=(g == 0), stop=(g == G - 1))
                    mm.then_inc(a_ready, 1)

            project_heads(0, 0, 1)

            def body(b, last):
                for k in range(NK):
                    c = b * NK + k
                    pe.wait_ge(xn_done, c + 1)
                    pe.wait_ge(xnT_done, 1 + 2 * c)
                    for h in range(CH):
                        for j in range(NJ):
                            mm = pe.transpose(pT[:, h, j * P:(j + 1) * P], xn[:, k % 2, j, h * P:(h + 1) * P],
                                              ident[:])
                        mm.then_inc(xT_ready, 1)
                    if not (last and k == NK - 1):
                        project_heads(c + 1, k + 1, b * (NK // 2) + (k + 1) // 2 + 1)
                    pe.wait_ge(blend_done, 1 + 2 * c + 1)
                    pe.wait_ge(prod_done, 1 + 2 * c)
                    for m in range(CH):
                        for h in range(CH):
                            mm = pe.matmul(pKV[:, m].rearrange("p a c -> p (a c)"), wk_sb[:, h, m * P:(m + 1) * P],
                                           xk[:, h], start=(h == 0), stop=(h == CH - 1))
                        mm.then_inc(k_ready, 1)
                    pe.wait_ge(blend_done, 1 + 2 * c + 2)
                    pe.wait_ge(gate_done, 1 + 2 * c)
                    for n in range(2):
                        for a in range(2):
                            t = 2 * n + a
                            for h in range(CH):
                                mm = pe.matmul(pR[:, n, a], xr[:, h, t * P:(t + 1) * P], wr_sb[:, h],
                                               start=(h == 0), stop=(h == CH - 1))
                        mm.then_inc(r_ready, 1)
                    pe.wait_ge(act_k_done, 1 + c + 1)
                    for n in range(2):
                        for a in range(2):
                            t = 2 * n + a
                            for h in range(CH):
                                mm = pe.matmul(pKV[:, n, a], act_k[:, h, t * P:(t + 1) * P], wv_sb[:, h],
                                               start=(h == 0), stop=(h == CH - 1))
                        mm.then_inc(mv_ready, 1)

            over_batches(pe, body)


def build(nc, ins, consts, out):
    def scratch(name, shape, dt=F32):
        return nc.dram_tensor(name, shape, dt, kind="Internal").ap()

    qk_parts = scratch("qk_parts", [2, B, 3, C, T], BF16)
    v_rows = scratch("v_rows", [B, W + T + W, H, VW])
    o_rows = scratch("o_rows", [B, G, P, T])
    x2 = scratch("x_after_first", [B, T, C])
    ffn = [ins[n] for n in ("L0_ffn_W_r", "L0_ffn_W_k", "L0_ffn_W_v", "L0_ffn_mu_r", "L0_ffn_mu_k")]
    project(nc, "proj_a", consts, ins["L0_attn_a_x"], ins["L0_attn_a_Wq"], ins["L0_attn_a_Wk"], ins["L0_attn_a_Wv"],
            None, qk_parts, v_rows)
    attend_full(nc, "full", consts, qk_parts, v_rows, o_rows)
    mix(nc, "mix_a", consts, ins["L0_attn_a_x"], o_rows, ins["L0_attn_a_Wo"], *ffn, x2)
    project(nc, "proj_b", consts, x2, ins["L0_attn_b_Wq"], ins["L0_attn_b_Wk"], ins["L0_attn_b_Wv"],
            [ins[f"L0_attn_b_b{n}"] for n in "qkv"], qk_parts, v_rows)
    attend_band(nc, "band", consts, qk_parts, v_rows, o_rows)
    mix(nc, "mix_b", consts, x2, o_rows, consts["eye"], *ffn, out)


def constants():
    import numpy as np

    bf16 = mybir.dt.np(BF16)

    def three_parts(a):
        parts = []
        for _ in range(3):
            parts.append(a.astype(bf16))
            a = a - parts[-1].astype(np.float32)
        return parts

    p = np.arange(P)
    eye = np.eye(P, dtype=np.float32)
    slope = three_parts(np.array([2.0 ** (-8.0 * h / H) for h in range(1, H + 1)], np.float32))
    pos = np.arange(T)
    slopes = np.zeros((H, NPOS, T), bf16)
    positions = np.ones((NPOS + 3, T), bf16)
    for s in range(T // POS_STEP):
        for i in range(3):
            slopes[:, 3 * s + i, s * POS_STEP:(s + 1) * POS_STEP] = slope[i][:, None]
            positions[3 * s + i] = (pos // P * P - s * POS_STEP).astype(bf16)
    for i in range(3):
        slopes[:, NPOS - 3 + i] = slope[i][:, None]
        positions[NPOS - 3 + i] = (pos % P).astype(bf16)

    def masked(valid):
        return np.where(valid, 0.0, NEG).astype(bf16)

    c = np.arange(2 * P)
    band = (c[None, :] >= p[:, None]) & (c[None, :] - p[:, None] <= P)
    left, right = c[None, :] >= W, c[None, :] < 3 * W
    lower, upper = p[:, None] >= W, p[:, None] < W
    band_q = np.stack([masked(np.stack(v, 1)) for v in ((band & left, band), (band, band), (band, band & right))], 1)
    band_k = np.stack([masked(np.stack(v, 1)) for v in ((band & lower,) * 2, (band,) * 2, (band & upper,) * 2)], 1)
    spread = np.zeros((P, P), np.float32)
    for a in range(HG):
        spread[VW * a + D, VW * a:VW * (a + 1)] = 1.0
    return {
        "ident": eye, "identb": eye.astype(bf16), "eye": np.eye(C, dtype=np.float32),
        "mask_q": masked(p[None, :] <= p[:, None]), "mask_k": masked(p[None, :] >= p[:, None]),
        "spread": spread, "slopes": slopes, "positions": positions, "band_q": band_q, "band_k": band_k,
    }


_TRANSPOSED = {"L0_attn_a_Wq", "L0_attn_a_Wk", "L0_attn_a_Wv", "L0_attn_a_Wo", "L0_ffn_W_r", "L0_ffn_W_k",
               "L0_ffn_W_v"}


def kernel(**inputs):
    import numpy as _np
    import concourse.bacc as _bacc
    from concourse import mybir as _mybir
    from concourse.bass_utils import run_bass_kernel_spmd as _run

    nc = _bacc.Bacc("TRN2", target_bir_lowering=False, num_devices=1)
    arrays = {}

    def given(name, a):
        arrays[name] = _np.ascontiguousarray(a)
        return nc.dram_tensor(name, a.shape, _mybir.dt.from_np(a.dtype), kind="ExternalInput").ap()

    ins = {n: given(f"in_{n}", _np.asarray(a).T if n in _TRANSPOSED else _np.asarray(a)) for n, a in inputs.items()}
    consts = {n: given(f"const_{n}", a) for n, a in constants().items()}
    out = nc.dram_tensor("out_x", (B, T, C), F32, kind="ExternalOutput").ap()
    build(nc, ins, consts, out)
    r = _run(nc, [arrays], core_ids=[0])
    return r.results[0]["out_x"]
```

```python
from contextlib import ExitStack

import concourse.bass as bass
from concourse import mybir

F32 = mybir.dt.float32
BF16 = mybir.dt.bfloat16
ALU = mybir.AluOpType
ACT = mybir.ActivationFunctionType
AX = mybir.AxisListType

P = 128
B, T, C = 4, 2048, 256
H, D = 16, 16
CH = C // P
NK = 4
TC = T // NK
NJ = TC // P
G = 4
HG = H // G
VW = 32
TILES = T // P
W = 64
EPS = 1e-5
LOWEST = -3e38
NEG = -1e30

Q_PART = [0, 0, 1, 1, 0, 2]
K_PART = [0, 1, 0, 1, 2, 0]
NPROD = len(Q_PART) * D
POS_STEP = 256
NPOS = T // POS_STEP * 3 + 3
FULL_ROWS = NPROD + NPOS + 3
BAND_ROWS = NPROD + 3


def start_at_one(eng, *semaphores):
    for s in semaphores:
        eng.sem_inc(s, 1)


def over_batches(eng, body):
    with eng.Fori(0, B - 1) as b:
        body(b, False)
    body(B - 1, True)


def project(nc, stage, consts, x, wq, wk, wv, bias, qk_parts, v_rows):
    with ExitStack() as ctx:
        def sb(name, shape, dt=F32):
            return ctx.enter_context(nc.sbuf_tensor(f"{stage}_{name}", shape, dt))

        def sem(name):
            return ctx.enter_context(nc.semaphore(f"{stage}_{name}"))

        def psum(name, shape):
            return ctx.enter_context(nc.psum_tensor(f"{stage}_{name}", shape, F32))

        w_sb = [sb(f"w{n}_sb", [P, CH, C]) for n in "qkv"]
        qk_bias = sb("qk_bias", [P, 2, CH])
        v_bias = sb("v_bias", [P, C])
        ident = sb("ident", [P, P])
        zeros = sb("zeros", [W, H * VW])
        xt = sb("xt", [P, 2, NJ, C])
        stats = sb("stats", [P, 2, NJ, 6])
        meanvar = sb("meanvar", [P, 2, NJ, 2])
        vareps = sb("vareps", [P, 2, NJ])
        held = sb("held", [P, 1])
        power = sb("power", [P, NJ])
        eps = sb("eps", [P, NJ])
        rstd = sb("rstd", [P, 2, NJ])
        xn = sb("xn", [P, 2, NJ, C])
        xnT = sb("xnT", [P, 2, CH, TC])
        full = sb("full", [P, 4, TC])
        rest = sb("rest", [P, 4, TC])
        parts = sb("parts", [P, 4, 3, TC], BF16)
        vst = sb("vst", [P, 2, NJ, H, VW])
        pT = psum("pT", [P, CH, TC])
        pQK = psum("pQK", [P, 4, TC])
        pV = psum("pV", [P, 2, 2, C])

        w_loaded = sem("w_loaded")
        x_loaded = [sem(f"x_loaded{i}") for i in range(2)]
        const_set = sem("const_set")
        stats_done = sem("stats_done")
        aggr_done = sem("aggr_done")
        vareps_done = sem("vareps_done")
        rstd_done = sem("rstd_done")
        xn_done = sem("xn_done")
        xT_ready = sem("xT_ready")
        xnT_done = sem("xnT_done")
        qk_ready = sem("qk_ready")
        full_done = sem("full_done")
        high_done = sem("high_done")
        rest_done = sem("rest_done")
        mid_done = sem("mid_done")
        low_done = sem("low_done")
        v_ready = sem("v_ready")
        v_done = sem("v_done")
        qk_stored = [sem(f"qk_stored{i}") for i in range(4)]
        v_stored = [sem(f"v_stored{i}") for i in range(2)]
        pad_stored = sem("pad_stored")
        n_w = 4 if bias is None else 7

        block = ctx.enter_context(nc.Block())

        @block.sync
        def _(sp):
            start_at_one(sp, *qk_stored, *v_stored)
            def load_x(b, k):
                sp.dma_start(xt[:, k % 2], x[b, k * TC:(k + 1) * TC, :].rearrange(
                    "(j p) c -> p j c", p=P)).then_inc(x_loaded[k % 2], 16)

            load_x(0, 0)
            sp.dma_start(ident[:], consts["ident"]).then_inc(w_loaded, 16)
            for w, src in zip(w_sb, (wq, wk, wv)):
                sp.dma_start(w[:], src.rearrange("(h p) d -> p h d", p=P)).then_inc(w_loaded, 16)
            if bias is not None:
                with nc.allow_non_contiguous_dma(reason="256 biases, one a partition"):
                    for n in range(2):
                        sp.dma_start(qk_bias[:, n], bias[n].rearrange("(h p) -> p h", p=P)).then_inc(w_loaded, 16)
                sp.dma_start(v_bias[:], bias[2].rearrange("(a c) -> a c", a=1).to_broadcast([P, C])
                             ).then_inc(w_loaded, 16)
            load_x(0, 1)
            sp.wait_ge(const_set, 4)
            for b in range(B):
                for at in (0, W + T):
                    sp.dma_start(v_rows[b, at:at + W].rearrange("t h d -> t (h d)"), zeros[:]
                                 ).then_inc(pad_stored, 16)

            def body(b, last):
                for k in range(NK):
                    c = b * NK + k
                    if not (last and k + 2 >= NK):
                        sp.wait_ge(xn_done, c + 1)
                        load_x(b + (k + 2) // NK, (k + 2) % NK)
                    for i in range(4):
                        sp.wait_ge(low_done, 1 + 4 * c + i + 1)
                        sp.dma_start(qk_parts[i // 2, b, :, i % 2 * P:(i % 2 + 1) * P, k * TC:(k + 1) * TC]
                                     .rearrange("s p t -> p s t"), parts[:, i]).then_inc(qk_stored[i], 16)
                    sp.wait_ge(v_done, 1 + 2 * c + 2)
                    sp.dma_start(v_rows[b, W + k * TC:W + (k + 1) * TC].rearrange("(j p) h d -> p j (h d)", p=P),
                                 vst[:, k % 2].rearrange("p j h d -> p j (h d)")).then_inc(v_stored[k % 2], 16)

            over_batches(sp, body)
            for s in qk_stored:
                sp.wait_ge(s, 1 + 16 * B * NK)
            for s in v_stored:
                sp.wait_ge(s, 1 + 16 * B * NK // 2)
            sp.wait_ge(pad_stored, 16 * B * 2)

        @block.gpsimd
        def _(pool):
            start_at_one(pool, low_done)
            pool.memset(eps[:], EPS)
            pool.memset(power[:], -0.5).then_inc(const_set, 1)
            pool.memset(zeros[:], 0.0).then_inc(const_set, 1)
            for i in range(2):
                pool.memset(vst[:, i, :, :, D:VW], 0.0)
            pool.memset(rest[:, 0, 0:1], 0.0).then_inc(const_set, 1)
            pool.wait_ge(const_set, 3)
            for i in range(2):
                last = pool.memset(vst[:, i, :, :, D:D + 1], 1.0)
            last.then_inc(const_set, 1)

            def norm(c, k):
                pool.wait_ge(aggr_done, c + 1)
                pool.tensor_tensor(vareps[:, k % 2], meanvar[:, k % 2, :, 1], eps[:], ALU.add).then_inc(vareps_done, 1)
                pool.wait_ge(vareps_done, c + 1)
                pool.tensor_tensor(rstd[:, k % 2], vareps[:, k % 2], power[:], ALU.pow).then_inc(rstd_done, 1)

            norm(0, 0)

            def body(b, last):
                for k in range(NK):
                    c = b * NK + k
                    if not (last and k == NK - 1):
                        norm(c + 1, k + 1)

                    def take_high(i):
                        pool.wait_ge(high_done, 4 * c + i + 1)
                        pool.tensor_tensor(rest[:, i], full[:, i], parts[:, i, 0], ALU.subtract
                                           ).then_inc(rest_done, 1)

                    def take_mid(i):
                        pool.wait_ge(mid_done, 4 * c + i + 1)
                        pool.tensor_tensor(parts[:, i, 2], rest[:, i], parts[:, i, 1], ALU.subtract
                                           ).then_inc(low_done, 1)

                    take_high(0)
                    for i in range(1, 4):
                        take_high(i)
                        take_mid(i - 1)
                    take_mid(3)

            over_batches(pool, body)

        @block.vector
        def _(dve):
            start_at_one(dve, full_done, v_done)
            if bias is None:
                dve.memset(qk_bias[:], 0.0)
                dve.memset(v_bias[:], 0.0).then_inc(stats_done, 1)
                dve.wait_ge(stats_done, 1)
            first = 1 if bias is None else 0

            def norm(c, k, turn):
                dve.wait_ge(x_loaded[k % 2], 16 * turn)
                for j in range(NJ):
                    dve.bn_stats(stats[:, k % 2, j], xt[:, k % 2, j]).then_inc(stats_done, 1)
                dve.wait_ge(stats_done, first + NJ * (c + 1))
                dve.memset(held[:], 0.0)
                for j in range(NJ):
                    last = dve.bn_aggr(meanvar[:, k % 2, j], stats[:, k % 2, j])
                last.then_inc(aggr_done, 1)
                dve.wait_ge(rstd_done, c + 1)
                if not (isinstance(c, int) and c == 0):
                    dve.wait_ge(xT_ready, 1 + 2 * (c - 1))
                for j in range(NJ):
                    last = dve.tensor_scalar(xn[:, k % 2, j], xt[:, k % 2, j], meanvar[:, k % 2, j, 0:1],
                                             rstd[:, k % 2, j:j + 1], ALU.subtract, ALU.mult)
                last.then_inc(xn_done, 1)

            norm(0, 0, 1)
            dve.wait_ge(w_loaded, 16 * n_w)
            dve.wait_ge(const_set, 4)

            def body(b, last):
                for k in range(NK):
                    c = b * NK + k
                    if not (last and k == NK - 1):
                        norm(c + 1, k + 1, b * (NK // 2) + (k + 1) // 2 + 1)
                    for i in range(4):
                        dve.wait_ge(qk_ready, 4 * c + i + 1)
                        dve.wait_ge(low_done, 1 + 4 * c)
                        dve.tensor_scalar(full[:, i], pQK[:, i], qk_bias[:, i // 2, i % 2:i % 2 + 1],
                                          0.25 if i < 2 else 1.0, ALU.add, ALU.mult).then_inc(full_done, 1)
                    for n in range(2):
                        dve.wait_ge(v_ready, 1 + 2 * c + n + 1)
                        if n == 0:
                            dve.wait_ge(v_stored[k % 2], 1 + 16 * (b * (NK // 2) + k // 2))
                        for j in range(2):
                            op = dve.tensor_tensor(
                                vst[:, k % 2, 2 * n + j, :, 0:D], pV[:, n, j].rearrange("p (h d) -> p h d", d=D),
                                v_bias[:].rearrange("p (h d) -> p h d", d=D), ALU.add)
                        op.then_inc(v_done, 1)

            over_batches(dve, body)

        @block.scalar
        def _(act):
            def copy_T(c, k):
                for h in range(CH):
                    act.wait_ge(xT_ready, 1 + 2 * c + h + 1)
                    if h == 0 and not (isinstance(c, int) and c == 0):
                        act.wait_ge(v_ready, 1 + 2 * (c - 1))
                    act.activation(xnT[:, k % 2, h], pT[:, h], ACT.Copy).then_inc(xnT_done, 1)

            copy_T(0, 0)

            def body(b, last):
                for k in range(NK):
                    c = b * NK + k

                    def high(i):
                        act.wait_ge(full_done, 1 + 4 * c + i + 1)
                        act.wait_ge(qk_stored[i], 1 + 16 * c)
                        act.activation(parts[:, i, 0], full[:, i], ACT.Copy).then_inc(high_done, 1)

                    def mid(i):
                        act.wait_ge(rest_done, 4 * c + i + 1)
                        act.activation(parts[:, i, 1], rest[:, i], ACT.Copy).then_inc(mid_done, 1)

                    high(0)
                    high(1)
                    mid(0)
                    high(2)
                    high(3)
                    if not (last and k == NK - 1):
                        copy_T(c + 1, k + 1)
                    for i in range(1, 4):
                        mid(i)

            over_batches(act, body)

        @block.tensor
        def _(pe):
            start_at_one(pe, xT_ready, v_ready)
            pe.wait_ge(w_loaded, 16 * n_w)

            def transpose(c, k):
                pe.wait_ge(xn_done, c + 1)
                pe.wait_ge(xnT_done, 2 * c)
                for h in range(CH):
                    for j in range(NJ):
                        last = pe.transpose(pT[:, h, j * P:(j + 1) * P], xn[:, k % 2, j, h * P:(h + 1) * P], ident[:])
                    last.then_inc(xT_ready, 1)

            transpose(0, 0)

            def body(b, last):
                for k in range(NK):
                    c = b * NK + k
                    pe.wait_ge(xnT_done, 2 * c + 2)
                    pe.wait_ge(full_done, 1 + 4 * c)
                    for i in range(4):
                        for h in range(CH):
                            mm = pe.matmul(pQK[:, i], w_sb[i // 2][:, h, i % 2 * P:(i % 2 + 1) * P],
                                           xnT[:, k % 2, h], start=(h == 0), stop=(h == CH - 1))
                        mm.then_inc(qk_ready, 1)
                    if not (last and k == NK - 1):
                        transpose(c + 1, k + 1)
                    pe.wait_ge(v_done, 1 + 2 * c)
                    for n in range(2):
                        for j in range(2):
                            t = 2 * n + j
                            for h in range(CH):
                                mm = pe.matmul(pV[:, n, j], xnT[:, k % 2, h, t * P:(t + 1) * P],
                                               w_sb[2][:, h], start=(h == 0), stop=(h == CH - 1))
                        mm.then_inc(v_ready, 1)

            over_batches(pe, body)


UNIT = [(q, t) for q in range(NK) for t in range(NJ * (q + 1))]
UNITS = len(UNIT)
CHUNK_ENDS = [NJ * (q + 1) * (q + 2) // 2 - 1 for q in range(NK)]


def unit_width(u):
    q, t = UNIT[u]
    return TC - max(0, t * P - q * TC)


def piece_width(i):
    h, t, s = PIECES[i]
    return min(TC, (t + 1) * P - s * TC)


def alternate(order):
    half = len(order) // 2
    return [i for pair in zip(order[half:][::-1], order[:half]) for i in pair]


def shares(unit_costs, piece_costs, by):
    whole, total, seen, done, out = sum(unit_costs[:by]), sum(piece_costs), 0, 0, []
    for u, cost in enumerate(unit_costs):
        seen += cost
        while done < len(piece_costs) and (sum(piece_costs[:done + 1]) <= total * seen / whole or u >= by - 1):
            done += 1
        out.append(done)
    return out


PIECES = alternate([(h, t, s) for t in range(TILES) for s in range(t // NJ + 1) for h in range(HG)])
MAX_AT = UNITS - 6
FLIP_AT = MAX_AT + 1
PIECES_BY = shares([unit_width(u) for u in range(UNITS)], [piece_width(i) + 60 for i in range(len(PIECES))], MAX_AT)
LEAD_BANKS = 6
AUX = NK + 1


def unit_pieces(u, by):
    return range(by[u - 1] if u else 0, by[u])


def aux_count(n, q, flipped):
    return AUX * n + 1 + q + flipped


def attend_full(nc, stage, consts, qk_parts, v_rows, o_rows):
    with ExitStack() as ctx:
        def sb(name, shape, dt=F32):
            return ctx.enter_context(nc.sbuf_tensor(f"{stage}_{name}", shape, dt))

        def sem(name):
            return ctx.enter_context(nc.semaphore(f"{stage}_{name}"))

        def psum(name, shape):
            return ctx.enter_context(nc.psum_tensor(f"{stage}_{name}", shape, F32))

        q_op = [sb(f"q_op{g}", [FULL_ROWS, HG, T], BF16) for g in range(G)]
        k_op = [sb(f"k_op{g}", [FULL_ROWS, HG, T], BF16) for g in range(G)]
        v_sb = [sb(f"v_sb{i}", [P, TILES, HG, VW]) for i in range(2)]
        probs = sb("probs", [P, 2, HG, TC])
        ident = sb("ident", [P, P])
        identb = sb("identb", [P, P], BF16)
        mask_q = sb("mask_q", [P, P], BF16)
        mask_k = sb("mask_k", [P, P], BF16)
        maxes = sb("maxes", [P, HG, TILES, NK])
        negmax = sb("negmax", [P, P])
        max_rest = sb("max_rest", [HG * TILES, 2, P])
        max_parts = sb("max_parts", [HG * TILES, 3, P], BF16)
        o_sb = sb("o_sb", [P, TC])
        inv = sb("inv", [P, NJ, HG, 1])
        o_norm = sb("o_norm", [P, NJ, HG, D])
        pS = psum("pS", [P, 2, 2, TC])
        pM = psum("pM", [P, 2, TC])
        pO = psum("pO", [P, TC])
        pX = psum("pX", [P, NJ, HG, VW])

        c_loaded = sem("c_loaded")
        qk_loaded = [sem(f"qk_loaded{g}") for g in range(G)]
        v_loaded = [sem(f"v_loaded{i}") for i in range(2)]
        max_loaded = sem("max_loaded")
        maxes_set = sem("maxes_set")
        s_ready = sem("s_ready")
        p_ready = sem("p_ready")
        p_used = sem("p_used")
        m_ready = sem("m_ready")
        m_used = sem("m_used")
        negmax_done = sem("negmax_done")
        split_step = sem("split_step")
        o_copied = sem("o_copied")
        aux_ready = sem("aux_ready")
        aux_free = sem("aux_free")
        inv_done = sem("inv_done")
        o_stored = sem("o_stored")
        N_C, N_QK = 4 + 2 * G, 13

        def lead_bank(i):
            i = i % LEAD_BANKS
            return pM[:, i] if i < 2 else pS[:, i // 2 - 1, i % 2]

        block = ctx.enter_context(nc.Block())

        @block.sync
        def _(sp):
            start_at_one(sp, o_stored)
            def load_qk(b, g):
                heads = slice(g * HG * D, (g + 1) * HG * D)
                for s in range(6):
                    for n, (dst, part) in enumerate(((q_op, Q_PART), (k_op, K_PART))):
                        sp.dma_start(dst[g][s * D:(s + 1) * D], qk_parts[n, b, part[s], heads].rearrange(
                            "(h d) t -> d h t", d=D)).then_inc(qk_loaded[g], 16)
                sp.dma_start(q_op[g][NPROD:NPROD + NPOS], consts["slopes"][g * HG:(g + 1) * HG].rearrange(
                    "h r t -> r h t")).then_inc(qk_loaded[g], 16)

            def load_v(b, g):
                sp.dma_start(v_sb[g % 2][:].rearrange("p t h d -> p t (h d)"),
                             v_rows[b, W:W + T, g * HG:(g + 1) * HG].rearrange("(t p) h d -> p t (h d)", p=P)
                             ).then_inc(v_loaded[g % 2], 16)

            for dst, name in ((ident, "ident"), (identb, "identb"), (mask_q, "mask_q"),
                              (mask_k, "mask_k")):
                sp.dma_start(dst[:], consts[name]).then_inc(c_loaded, 16)
            for g in range(G):
                for half in range(2):
                    sp.dma_start(k_op[g][NPROD:FULL_ROWS, 2 * half:2 * half + 2], consts["positions"].rearrange(
                        "r (a t) -> r a t", a=1).to_broadcast([NPOS + 3, 2, T])).then_inc(c_loaded, 16)
            load_qk(0, 0)
            load_qk(0, 1)
            load_v(0, 0)
            load_v(0, 1)
            load_qk(0, 2)
            load_qk(0, 3)

            def store_max(n, g):
                sp.wait_ge(split_step, 4 * n + 4)
                for s in range(3):
                    row = FULL_ROWS - 3 + s
                    sp.dma_start(q_op[g][row:row + 1].rearrange("r h (t q) -> r (h t) q", q=P),
                                 max_parts[:, s]).then_inc(max_loaded, 16)

            store_max(0, 0)

            def body(b, last):
                for g in range(G):
                    n = b * G + g
                    for q in range(NK):
                        flipped = q == NK - 1 and not (last and g == G - 1)
                        if flipped:
                            store_max(n + 1, (g + 1) % G)
                        sp.wait_ge(aux_free, aux_count(n, q, flipped) + 1)
                        store_heads(sp, o_rows, o_norm, o_stored, b, g, q)
                    sp.wait_ge(p_used, UNITS * (n + 1) + 2)
                    if not last:
                        load_qk(b + 1, g)
                    if not (last and g >= 2):
                        load_v(b + (g + 2) // G, (g + 2) % G)

            over_batches(sp, body)
            sp.wait_ge(o_stored, 1 + 16 * B * G * NK)

        @block.gpsimd
        def _(pool):
            pool.memset(negmax[:, HG * TILES:], 0.0)
            pool.memset(maxes[:], LOWEST).then_inc(maxes_set, 1)

        @block.tensor
        def _(pe):
            pe.sem_inc(p_used, 2)
            pe.wait_ge(c_loaded, 16 * N_C)

            def piece_into(bank, g, i):
                h, t, s = PIECES[i]
                w = piece_width(i)
                diag = s == t // NJ
                mm = pe.matmul(bank[:, 0:w], q_op[g][0:FULL_ROWS - 3, h, t * P:(t + 1) * P],
                               k_op[g][0:FULL_ROWS - 3, h, s * TC:s * TC + w], start=True, stop=not diag)
                if diag:
                    mm = pe.matmul(bank[:, w - P:w], identb[:], mask_q[:], start=False, stop=True)
                mm.then_inc(m_ready, 1)

            def piece(n, g, i):
                pe.wait_ge(m_used, len(PIECES) * n + i - 1)
                piece_into(pM[:, i % 2], g, i)

            def flip_maxima(n, uses):
                pe.wait_ge(negmax_done, n + 1)
                pe.wait_ge(aux_free, uses)
                pe.transpose(flat(pX)[:, 0:P], negmax[:], ident[:]).then_inc(aux_ready, 1)

            def turn_sums(n, q, flipped):
                pe.wait_ge(o_copied, 1 + NK * n + q + 1)
                pe.wait_ge(aux_free, aux_count(n, q, flipped))
                for j in range(NJ):
                    mm = pe.transpose(flat(pX)[:, j * P:(j + 1) * P], o_sb[:, j * P:(j + 1) * P], ident[:])
                mm.then_inc(aux_ready, 1)

            def scores(n, g, u, pair):
                q, t = UNIT[u]
                lo = max(0, t * P - q * TC)
                pe.wait_ge(p_ready, 2 * (UNITS * n + u) + pair + 1)
                for a in range(2):
                    h = 2 * pair + a
                    diag = t * P >= q * TC
                    mm = pe.matmul(pS[:, pair, a, lo:TC], k_op[g][:, h, t * P:(t + 1) * P],
                                   q_op[g][:, h, q * TC + lo:(q + 1) * TC], start=True, stop=not diag)
                    if diag:
                        mm = pe.matmul(pS[:, pair, a, lo:lo + P], identb[:], mask_k[:], start=False, stop=True)
                mm.then_inc(s_ready, 1)

            def values(n, g, u):
                q, t = UNIT[u]
                lo = max(0, t * P - q * TC)
                pe.wait_ge(p_ready, 2 * (UNITS * n + u + 1) + 2)
                if t == 0:
                    pe.wait_ge(o_copied, 1 + NK * n + q)
                for h in range(HG):
                    mm = pe.matmul(pO[VW * h:VW * (h + 1), lo:TC], v_sb[g % 2][:, t, h], probs[:, u % 2, h, lo:TC],
                                   start=(t == 0), stop=(u in CHUNK_ENDS))
                mm.then_inc(p_used, 1)

            pe.wait_ge(qk_loaded[0], 16 * N_QK)
            for i in range(len(PIECES)):
                if i >= LEAD_BANKS:
                    pe.wait_ge(m_used, i - LEAD_BANKS + 1)
                piece_into(lead_bank(i), 0, i)
            flip_maxima(0, 0)

            def body(b, last):
                for at in range(G * UNITS + 2):
                    g, u = divmod(at, UNITS)
                    n = b * G + g
                    ahead = not (last and g == G - 1)
                    todo = []
                    if g < G:
                        if u == 0:
                            pe.wait_ge(max_loaded, 48 * (n + 1))
                            pe.wait_ge(v_loaded[g % 2], 16 * (b * 2 + g // 2 + 1))
                            if ahead:
                                pe.wait_ge(qk_loaded[(g + 1) % G], 16 * N_QK * (b + (g + 1) // G + 1))
                        todo = list(unit_pieces(u, PIECES_BY)) if ahead else []
                        cuts = [round(len(todo) * f) for f in (0, 0.2, 0.6)]
                        scores(n, g, u, 0)
                        for i in todo[cuts[0]:cuts[1]]:
                            piece(n + 1, (g + 1) % G, i)
                        scores(n, g, u, 1)
                        for i in todo[cuts[1]:cuts[2]]:
                            piece(n + 1, (g + 1) % G, i)
                        todo = todo[cuts[2]:]
                    if 1 <= at <= G * UNITS:
                        past, v = divmod(at - 1, UNITS)
                        values(b * G + past, past, v)
                    for i in todo:
                        piece(n + 1, (g + 1) % G, i)
                    if at >= 2 and (at - 2) % UNITS in CHUNK_ENDS:
                        past, v = divmod(at - 2, UNITS)
                        q = CHUNK_ENDS.index(v)
                        turn_sums(b * G + past, q, q == NK - 1 and not (last and past == G - 1))
                    if ahead and g < G and u == FLIP_AT:
                        flip_maxima(n + 1, aux_count(n, NK - 1, 0))

            over_batches(pe, body)

        @block.scalar
        def _(act):
            act.sem_inc(p_ready, 2)

            def body(b, last):
                for g in range(G):
                    n = b * G + g
                    for u in range(UNITS):
                        q, t = UNIT[u]
                        lo = max(0, t * P - q * TC)
                        act.wait_ge(p_used, UNITS * n + u + 1)
                        for pair in range(2):
                            act.wait_ge(s_ready, 2 * (UNITS * n + u) + pair + 1)
                            act.activation(probs[:, u % 2, 2 * pair:2 * pair + 2, lo:TC], pS[:, pair, :, lo:TC],
                                           ACT.Exp).then_inc(p_ready, 1)

            over_batches(act, body)

        @block.vector
        def _(dve):
            start_at_one(dve, o_copied)
            def piece(n, i, bank):
                h, t, s = PIECES[i]
                dve.wait_ge(m_ready, len(PIECES) * n + i + 1)
                dve.reduce_max(maxes[:, h, t, s:s + 1], bank[:, 0:piece_width(i)], AX.X).then_inc(m_used, 1)

            def finish_maxima(n):
                dve.wait_ge(m_used, len(PIECES) * (n + 1))
                dve.tensor_reduce(negmax[:, 0:HG * TILES], maxes[:].rearrange("p h t s -> p (h t) s"), AX.X, ALU.max,
                                  negate=True).then_inc(negmax_done, 1)

            def split_maxima(n, uses):
                split_rows(dve, n, uses, pX, max_parts, max_rest, aux_ready, aux_free, max_loaded, split_step)

            dve.wait_ge(maxes_set, 1)
            for i in range(len(PIECES)):
                piece(0, i, lead_bank(i))
            finish_maxima(0)
            split_maxima(0, 0)

            def copy_sums(n, q):
                dve.wait_ge(p_used, UNITS * n + CHUNK_ENDS[q] + 1 + 2)
                dve.tensor_copy(o_sb[:], pO[:]).then_inc(o_copied, 1)

            def body(b, last):
                for at in range(G * UNITS + 2):
                    g, u = divmod(at, UNITS)
                    n = b * G + g
                    ahead = g < G and not (last and g == G - 1)
                    if ahead:
                        for i in unit_pieces(u, PIECES_BY):
                            piece(n + 1, i, pM[:, i % 2])
                    if at >= 1 and (at - 1) % UNITS in CHUNK_ENDS:
                        past, v = divmod(at - 1, UNITS)
                        copy_sums(b * G + past, CHUNK_ENDS.index(v))
                    if at >= 2 and (at - 2) % UNITS in CHUNK_ENDS:
                        past, v = divmod(at - 2, UNITS)
                        q = CHUNK_ENDS.index(v)
                        normalise(dve, b * G + past, q, q == NK - 1 and not (last and past == G - 1),
                                  pX, inv, o_norm, aux_ready, inv_done, o_stored, aux_free)
                    if ahead and u == MAX_AT:
                        finish_maxima(n + 1)
                    if ahead and u == FLIP_AT:
                        split_maxima(n + 1, aux_count(n, NK - 1, 0))

            over_batches(dve, body)


def flat(psum):
    return psum[:].rearrange("p j h d -> p (j h d)")


def normalise(dve, n, q, flipped, pX, inv, o_norm, aux_ready, inv_done, o_stored, aux_free):
    dve.wait_ge(aux_ready, aux_count(n, q, flipped) + 1)
    dve.reciprocal(inv[:], pX[:, :, :, D:D + 1]).then_inc(inv_done, 1)
    dve.wait_ge(inv_done, NK * n + q + 1)
    dve.wait_ge(o_stored, 1 + 16 * (NK * n + q))
    dve.tensor_tensor(o_norm[:], pX[:, :, :, 0:D], inv[:].to_broadcast([P, NJ, HG, D]), ALU.mult
                      ).then_inc(aux_free, 1)


def store_heads(sp, o_rows, o_norm, o_stored, b, g, q):
    sp.dma_start(o_rows[b, q * TC:(q + 1) * TC, g * HG * D:(g + 1) * HG * D].rearrange("(j p) c -> p j c", p=P),
                 o_norm[:].rearrange("p j h d -> p j (h d)")).then_inc(o_stored, 16)


def split_rows(dve, n, uses, pX, max_parts, max_rest, aux_ready, aux_free, max_loaded, split_step):
    flipped = flat(pX)[0:HG * TILES, 0:P]
    dve.wait_ge(aux_ready, uses + 1)
    dve.wait_ge(max_loaded, 48 * n)
    dve.tensor_copy(max_parts[:, 0], flipped).then_inc(split_step, 1)
    dve.wait_ge(split_step, 4 * n + 1)
    dve.tensor_tensor(max_rest[:, 0], flipped, max_parts[:, 0], ALU.subtract).then_inc(aux_free, 1)
    dve.wait_ge(aux_free, uses + 1)
    dve.tensor_copy(max_parts[:, 1], max_rest[:, 0]).then_inc(split_step, 1)
    dve.wait_ge(split_step, 4 * n + 2)
    dve.tensor_tensor(max_rest[:, 1], max_rest[:, 0], max_parts[:, 1], ALU.subtract).then_inc(split_step, 1)
    dve.wait_ge(split_step, 4 * n + 3)
    dve.tensor_copy(max_parts[:, 2], max_rest[:, 1]).then_inc(split_step, 1)


KT = TILES + 1
BAND_PIECES = [(h, t) for t in range(0, TILES, 2) for h in range(HG)]
BAND_MAX_AT = KT - 4
BAND_FLIP_AT = BAND_MAX_AT + 1
BAND_PIECES_BY = shares([1] * KT, [1] * len(BAND_PIECES), BAND_MAX_AT)
BAND_ENDS = [NJ * (q + 1) - 1 for q in range(NK)]
RING = 4


def attend_band(nc, stage, consts, qk_parts, v_rows, o_rows):
    with ExitStack() as ctx:
        def sb(name, shape, dt=F32):
            return ctx.enter_context(nc.sbuf_tensor(f"{stage}_{name}", shape, dt))

        def sem(name):
            return ctx.enter_context(nc.semaphore(f"{stage}_{name}"))

        def psum(name, shape):
            return ctx.enter_context(nc.psum_tensor(f"{stage}_{name}", shape, F32))

        q_op = [sb(f"q_op{g}", [BAND_ROWS, HG, T], BF16) for g in range(G)]
        k_op = [sb(f"k_op{g}", [BAND_ROWS, HG, W + T + W], BF16) for g in range(G)]
        v_sb = [sb(f"v_sb{i}", [P, KT, HG, VW]) for i in range(2)]
        probs = sb("probs", [P, RING, HG, 2 * P])
        ident = sb("ident", [P, P])
        identb = sb("identb", [P, P], BF16)
        mask_q = sb("mask_q", [P, 3, 2, 2 * P])
        mask_k = sb("mask_k", [P, 3, 2, 2 * P], BF16)
        held = sb("held", [P, LEAD_BANKS])
        masked = sb("masked", [P, LEAD_BANKS, 2, 2 * P], BF16)
        maxes = sb("maxes", [P, HG, TILES])
        negmax = sb("negmax", [P, P])
        max_rest = sb("max_rest", [HG * TILES, 2, P])
        max_parts = sb("max_parts", [HG * TILES, 3, P], BF16)
        o_sb = sb("o_sb", [P, TC])
        inv = sb("inv", [P, NJ, HG, 1])
        o_norm = sb("o_norm", [P, NJ, HG, D])
        pS = psum("pS", [P, 2, HG, 2 * P])
        pM = psum("pM", [P, 2, 2, 2 * P])
        pO = psum("pO", [P, TC])
        pX = psum("pX", [P, NJ, HG, VW])

        c_loaded = sem("c_loaded")
        pads_set = sem("pads_set")
        qk_loaded = [sem(f"qk_loaded{g}") for g in range(G)]
        v_loaded = [sem(f"v_loaded{i}") for i in range(2)]
        max_loaded = sem("max_loaded")
        s_ready = sem("s_ready")
        p_ready = sem("p_ready")
        o_ready = sem("o_ready")
        m_ready = sem("m_ready")
        m_used = sem("m_used")
        negmax_done = sem("negmax_done")
        split_step = sem("split_step")
        o_copied = sem("o_copied")
        aux_ready = sem("aux_ready")
        aux_free = sem("aux_free")
        inv_done = sem("inv_done")
        o_stored = sem("o_stored")
        N_C, N_QK = 4 + G, 12

        def lead_bank(i):
            i = i % LEAD_BANKS
            return pM[:, i] if i < 2 else pS[:, i // 2 - 1, i % 2 * 2:i % 2 * 2 + 2]

        block = ctx.enter_context(nc.Block())

        @block.sync
        def _(sp):
            start_at_one(sp, o_stored)
            def load_qk(b, g):
                heads = slice(g * HG * D, (g + 1) * HG * D)
                for s in range(6):
                    sp.dma_start(q_op[g][s * D:(s + 1) * D], qk_parts[0, b, Q_PART[s], heads].rearrange(
                        "(h d) t -> d h t", d=D)).then_inc(qk_loaded[g], 16)
                    sp.dma_start(k_op[g][s * D:(s + 1) * D, :, W:W + T], qk_parts[1, b, K_PART[s], heads].rearrange(
                        "(h d) t -> d h t", d=D)).then_inc(qk_loaded[g], 16)

            def load_v(b, g):
                sp.dma_start(v_sb[g % 2][:].rearrange("p t h d -> p t (h d)"),
                             v_rows[b, :, g * HG:(g + 1) * HG].rearrange("(t p) h d -> p t (h d)", p=P)
                             ).then_inc(v_loaded[g % 2], 16)

            for dst, name in ((ident, "ident"), (identb, "identb"), (mask_q, "band_q"),
                              (mask_k, "band_k")):
                sp.dma_start(dst[:], consts[name]).then_inc(c_loaded, 16)
            for g in range(G):
                sp.dma_start(k_op[g][NPROD:BAND_ROWS, :, W:W + T], consts["positions"][NPOS:NPOS + 3].rearrange(
                    "r (a t) -> r a t", a=1).to_broadcast([3, HG, T])).then_inc(c_loaded, 16)
            load_qk(0, 0)
            load_qk(0, 1)
            load_v(0, 0)
            load_v(0, 1)
            load_qk(0, 2)
            load_qk(0, 3)

            def store_max(n, g):
                sp.wait_ge(split_step, 4 * n + 4)
                for s in range(3):
                    row = BAND_ROWS - 3 + s
                    sp.dma_start(q_op[g][row:row + 1].rearrange("r h (t q) -> r (h t) q", q=P),
                                 max_parts[:, s]).then_inc(max_loaded, 16)

            store_max(0, 0)

            def body(b, last):
                for g in range(G):
                    n = b * G + g
                    for q in range(NK):
                        flipped = q == NK - 1 and not (last and g == G - 1)
                        if flipped:
                            store_max(n + 1, (g + 1) % G)
                        sp.wait_ge(aux_free, aux_count(n, q, flipped) + 1)
                        store_heads(sp, o_rows, o_norm, o_stored, b, g, q)
                    sp.wait_ge(o_ready, 1 + TILES * (n + 1))
                    if not last:
                        load_qk(b + 1, g)
                    if not (last and g >= 2):
                        load_v(b + (g + 2) // G, (g + 2) % G)

            over_batches(sp, body)
            sp.wait_ge(o_stored, 1 + 16 * B * G * NK)

        @block.gpsimd
        def _(pool):
            pool.memset(negmax[:, HG * TILES:], 0.0)
            for g in range(G):
                pool.memset(k_op[g][:, :, 0:W], 0.0)
                last = pool.memset(k_op[g][:, :, W + T:], 0.0)
            last.then_inc(pads_set, 1)

        @block.tensor
        def _(pe):
            start_at_one(pe, o_ready)
            pe.wait_ge(c_loaded, 16 * N_C)
            pe.wait_ge(pads_set, 1)

            def piece_into(bank, g, i):
                h, t = BAND_PIECES[i]
                for a in range(2):
                    mm = pe.matmul(bank[:, a], q_op[g][0:NPROD, h, (t + a) * P:(t + a + 1) * P],
                                   k_op[g][0:NPROD, h, (t + a) * P:(t + a + 2) * P], start=(a == 0), stop=(a == 1))
                mm.then_inc(m_ready, 1)

            def piece(n, g, i):
                pe.wait_ge(m_used, len(BAND_PIECES) * n + i - 1)
                piece_into(pM[:, i % 2], g, i)

            def flip_maxima(n, uses):
                pe.wait_ge(negmax_done, n + 1)
                pe.wait_ge(aux_free, uses)
                pe.transpose(flat(pX)[:, 0:P], negmax[:], ident[:]).then_inc(aux_ready, 1)

            def turn_sums(n, q, flipped):
                pe.wait_ge(o_copied, 1 + NK * n + q + 1)
                pe.wait_ge(aux_free, aux_count(n, q, flipped))
                for j in range(NJ):
                    mm = pe.transpose(flat(pX)[:, j * P:(j + 1) * P], o_sb[:, j * P:(j + 1) * P], ident[:])
                mm.then_inc(aux_ready, 1)

            def scores(n, g, j):
                lo, hi = (P if j == 0 else 0), (P if j == KT - 1 else 2 * P)
                edge = 0 if j == 0 else 2 if j == KT - 1 else 1
                pe.wait_ge(p_ready, KT * n + j + 1)
                for h in range(HG):
                    if h % 2 == 0:
                        pe.matmul(pS[:, (g * KT + j) % 2, h:h + 2, lo:hi], identb[:], mask_k[:, edge, :, lo:hi],
                                  start=True, stop=False)
                    mm = pe.matmul(pS[:, (g * KT + j) % 2, h, lo:hi], k_op[g][:, h, j * P:(j + 1) * P],
                                   q_op[g][:, h, (j - 1) * P + lo:(j - 1) * P + hi], start=False, stop=(h % 2 == 1))
                mm.then_inc(s_ready, 1)

            def values(n, g, t):
                pe.wait_ge(p_ready, KT * n + t + 2 + 2)
                if t % NJ == 0:
                    pe.wait_ge(o_copied, 1 + NK * n + t // NJ)
                for a in range(2):
                    for h in range(HG):
                        mm = pe.matmul(pO[VW * h:VW * (h + 1), t % NJ * P:(t % NJ + 1) * P], v_sb[g % 2][:, t + a, h],
                                       probs[:, (g * KT + t + a) % RING, h, P * (1 - a):P * (2 - a)],
                                       start=(a == 0), stop=(a == 1))
                mm.then_inc(o_ready, 1)

            pe.wait_ge(qk_loaded[0], 16 * N_QK)
            for i in range(len(BAND_PIECES)):
                if i >= LEAD_BANKS:
                    pe.wait_ge(m_used, i - LEAD_BANKS + 1)
                piece_into(lead_bank(i), 0, i)
            flip_maxima(0, 0)

            def body(b, last):
                for at in range(G * KT + 2):
                    g, j = divmod(at, KT)
                    n = b * G + g
                    ahead = g < G and not (last and g == G - 1)
                    if g < G:
                        if j == 0:
                            pe.wait_ge(max_loaded, 48 * (n + 1))
                            pe.wait_ge(v_loaded[g % 2], 16 * (b * 2 + g // 2 + 1))
                            if ahead:
                                pe.wait_ge(qk_loaded[(g + 1) % G], 16 * N_QK * (b + (g + 1) // G + 1))
                        scores(n, g, j)
                    todo = list(unit_pieces(j, BAND_PIECES_BY)) if ahead else []
                    for i in todo[:1]:
                        piece(n + 1, (g + 1) % G, i)
                    if at >= 2 and (at - 2) % KT < TILES:
                        past, t = divmod(at - 2, KT)
                        values(b * G + past, past, t)
                    for i in todo[1:]:
                        piece(n + 1, (g + 1) % G, i)
                    if at >= 3 and (at - 3) % KT in BAND_ENDS:
                        past, t = divmod(at - 3, KT)
                        q = BAND_ENDS.index(t)
                        turn_sums(b * G + past, q, q == NK - 1 and not (last and past == G - 1))
                    if ahead and j == BAND_FLIP_AT:
                        flip_maxima(n + 1, aux_count(n, NK - 1, 0))

            over_batches(pe, body)

        @block.scalar
        def _(act):
            act.sem_inc(p_ready, 2)
            def body(b, last):
                for at in range(G * KT):
                    g, j = divmod(at, KT)
                    n = b * G + g
                    lo, hi = (P if j == 0 else 0), (P if j == KT - 1 else 2 * P)
                    past, t = divmod(at - RING, KT)
                    done = TILES * past + min(t, TILES - 1) + 1 if at >= RING else 0
                    act.wait_ge(o_ready, 1 + b * (G * TILES) + done)
                    act.wait_ge(s_ready, KT * n + j + 1)
                    act.activation(probs[:, at % RING, :, lo:hi], pS[:, at % 2, :, lo:hi], ACT.Exp
                                   ).then_inc(p_ready, 1)

            over_batches(act, body)

        @block.vector
        def _(dve):
            start_at_one(dve, o_copied)
            def piece(n, i, bank):
                h, t = BAND_PIECES[i]
                edge = 0 if t == 0 else 2 if t == TILES - 2 else 1
                dve.wait_ge(m_ready, len(BAND_PIECES) * n + i + 1)
                dve.memset(held[:, i % LEAD_BANKS:i % LEAD_BANKS + 1], 0.0)
                for a in range(2):
                    op = dve.tensor_tensor_reduce(masked[:, i % LEAD_BANKS, a], bank[:, a], mask_q[:, edge, a], 1.0, LOWEST,
                                                  ALU.add, ALU.max, accum_out=maxes[:, h, t + a:t + a + 1])
                op.then_inc(m_used, 1)

            def finish_maxima(n):
                dve.wait_ge(m_used, len(BAND_PIECES) * (n + 1))
                dve.tensor_scalar(negmax[:, 0:HG * TILES], maxes[:].rearrange("p h t -> p (h t)"), -1.0, None, ALU.mult
                                  ).then_inc(negmax_done, 1)

            def split_maxima(n, uses):
                split_rows(dve, n, uses, pX, max_parts, max_rest, aux_ready, aux_free, max_loaded, split_step)

            dve.wait_ge(c_loaded, 16 * N_C)
            for i in range(len(BAND_PIECES)):
                piece(0, i, lead_bank(i))
            finish_maxima(0)
            split_maxima(0, 0)

            def copy_sums(n, q):
                dve.wait_ge(o_ready, 1 + TILES * n + NJ * (q + 1))
                dve.tensor_copy(o_sb[:], pO[:]).then_inc(o_copied, 1)

            def body(b, last):
                for at in range(G * KT + 2):
                    g, j = divmod(at, KT)
                    n = b * G + g
                    ahead = g < G and not (last and g == G - 1)
                    if ahead:
                        for i in unit_pieces(j, BAND_PIECES_BY):
                            piece(n + 1, i, pM[:, i % 2])
                    if at >= 2 and (at - 2) % KT in BAND_ENDS:
                        past, t = divmod(at - 2, KT)
                        copy_sums(b * G + past, BAND_ENDS.index(t))
                    if at >= 3 and (at - 3) % KT in BAND_ENDS:
                        past, t = divmod(at - 3, KT)
                        q = BAND_ENDS.index(t)
                        normalise(dve, b * G + past, q, q == NK - 1 and not (last and past == G - 1),
                                  pX, inv, o_norm, aux_ready, inv_done, o_stored, aux_free)
                    if ahead and j == BAND_MAX_AT:
                        finish_maxima(n + 1)
                    if ahead and j == BAND_FLIP_AT:
                        split_maxima(n + 1, aux_count(n, NK - 1, 0))

            over_batches(dve, body)


def mix(nc, stage, consts, x, o_rows, wo, wr, wk, wv, mu_r, mu_k, out):
    with ExitStack() as ctx:
        def sb(name, shape, dt=F32):
            return ctx.enter_context(nc.sbuf_tensor(f"{stage}_{name}", shape, dt))

        def sem(name):
            return ctx.enter_context(nc.semaphore(f"{stage}_{name}"))

        def psum(name, shape):
            return ctx.enter_context(nc.psum_tensor(f"{stage}_{name}", shape, F32))

        wr_sb, wk_sb, wv_sb = [sb(f"w{n}_sb", [P, CH, C]) for n in "rkv"]
        wo_sb = sb("wo_sb", [P, CH, C])
        mu = sb("mu", [P, 2, CH])
        ident = sb("ident", [P, P])
        xt = sb("xt", [P, 2, NJ, C])
        ot = sb("ot", [P, 2, NJ, C])
        oT = sb("oT", [P, CH, TC])
        x1 = sb("x1", [P, NK, NJ, C])
        stats = sb("stats", [P, 2, NJ, 6])
        meanvar = sb("meanvar", [P, 2, NJ, 2])
        vareps = sb("vareps", [P, 2, NJ])
        held = sb("held", [P, 1])
        power = sb("power", [P, NJ])
        eps = sb("eps", [P, NJ])
        rstd = sb("rstd", [P, 2, NJ])
        xn = sb("xn", [P, 2, NJ, C])
        xnT = sb("xnT", [P, 2, CH, TC + 1])
        step = sb("step", [P, CH, TC])
        zero = sb("zero", [P, CH, 1])
        xk = sb("xk", [P, 2, CH, TC])
        xr = sb("xr", [P, 2, CH, TC])
        relu = sb("relu", [P, CH, TC])
        act_k = sb("act_k", [P, CH, TC])
        gate = sb("gate", [P, 2, 2, C])
        prod = sb("prod", [P, 2, 2, C])
        x2 = sb("x2", [P, 2, NJ, C])
        pA = psum("pA", [P, 2, 2, C])
        pT = psum("pT", [P, CH, TC])
        pKV = psum("pKV", [P, 2, 2, C])
        pR = psum("pR", [P, 2, 2, C])

        w_loaded = sem("w_loaded")
        x_loaded = [sem(f"x_loaded{i}") for i in range(2)]
        const_set = sem("const_set")
        oT_ready = sem("oT_ready")
        oT_done = sem("oT_done")
        a_ready = sem("a_ready")
        x1_done = sem("x1_done")
        stats_done = sem("stats_done")
        aggr_done = sem("aggr_done")
        vareps_done = sem("vareps_done")
        rstd_done = sem("rstd_done")
        xn_done = sem("xn_done")
        xT_ready = sem("xT_ready")
        xnT_done = sem("xnT_done")
        edge_done = sem("edge_done")
        step_done = sem("step_done")
        blend_done = sem("blend_done")
        k_ready = sem("k_ready")
        relu_done = sem("relu_done")
        act_k_done = sem("act_k_done")
        r_ready = sem("r_ready")
        gate_done = sem("gate_done")
        mv_ready = sem("mv_ready")
        prod_done = sem("prod_done")
        x2_done = sem("x2_done")
        x_stored = [sem(f"x_stored{i}") for i in range(2)]
        N_W = 6 if wo is None else 7
        rows = out.rearrange("b t c -> (b t) c")

        def turn(b, k):
            return b * (NK // 2) + k // 2 + 1

        block = ctx.enter_context(nc.Block())

        @block.sync
        def _(sp):
            start_at_one(sp, *x_stored)

            def load(b, k):
                for dst, src in ((ot, o_rows), (xt, x)):
                    sp.dma_start(dst[:, k % 2], src[b, k * TC:(k + 1) * TC, :].rearrange("(j p) c -> p j c", p=P)
                                 ).then_inc(x_loaded[k % 2], 16)

            load(0, 0)
            load(0, 1)
            if wo is not None:
                sp.dma_start(wo_sb[:], wo.rearrange("(h p) d -> p h d", p=P)).then_inc(w_loaded, 16)
            sp.dma_start(ident[:], consts["ident"]).then_inc(w_loaded, 16)
            for dst, src in ((wr_sb, wr), (wk_sb, wk), (wv_sb, wv)):
                sp.dma_start(dst[:], src.rearrange("(h p) d -> p h d", p=P)).then_inc(w_loaded, 16)
            with nc.allow_non_contiguous_dma(reason="256 factors, one a partition"):
                for n, src in enumerate((mu_k, mu_r)):
                    sp.dma_start(mu[:, n], src.rearrange("(h p) -> p h", p=P)).then_inc(w_loaded, 16)
            for k in range(2):
                sp.wait_ge(x1_done, k + 1)
                load(0, k + 2)

            def body(b, last):
                for k in range(NK):
                    c = b * NK + k
                    if not last:
                        sp.wait_ge(x1_done, c + 3)
                        load(b + 1, k)
                    sp.wait_ge(x2_done, 1 + 2 * c + 2)
                    sp.dma_start(rows[bass.ds(c * TC, TC), :].rearrange("(j p) c -> p j c", p=P), x2[:, k % 2]
                                 ).then_inc(x_stored[k % 2], 16)

            over_batches(sp, body)
            for s in x_stored:
                sp.wait_ge(s, 1 + 16 * B * NK // 2)

        @block.gpsimd
        def _(pool):
            start_at_one(pool, x2_done, act_k_done)
            pool.memset(eps[:], EPS)
            pool.memset(zero[:], 0.0)
            pool.memset(power[:], -0.5).then_inc(const_set, 1)
            pool.wait_ge(const_set, 1)

            def norm(c, k):
                pool.wait_ge(aggr_done, c + 1)
                pool.tensor_tensor(vareps[:, k % 2], meanvar[:, k % 2, :, 1], eps[:], ALU.add).then_inc(vareps_done, 1)
                pool.wait_ge(vareps_done, c + 1)
                pool.tensor_tensor(rstd[:, k % 2], vareps[:, k % 2], power[:], ALU.pow).then_inc(rstd_done, 1)

            def differ(c, k):
                pool.wait_ge(blend_done, 1 + 2 * c)
                pool.wait_ge(xnT_done, 2 * c + 2)
                before = zero[:] if k % NK == 0 else xnT[:, (k - 1) % 2, :, TC:TC + 1]
                pool.tensor_tensor(xnT[:, k % 2, :, 0:1], before, zero[:], ALU.add).then_inc(edge_done, 1)
                pool.wait_ge(edge_done, c + 1)
                pool.tensor_tensor(step[:], xnT[:, k % 2, :, 1:TC + 1], xnT[:, k % 2, :, 0:TC], ALU.subtract
                                   ).then_inc(step_done, 1)

            norm(0, 0)
            norm(1, 1)
            differ(0, 0)

            def body(b, last):
                for k in range(NK):
                    c = b * NK + k
                    pool.wait_ge(relu_done, 2 * c + 2)
                    pool.wait_ge(mv_ready, 1 + 2 * c)
                    pool.tensor_tensor(act_k[:], relu[:], relu[:], ALU.mult).then_inc(act_k_done, 1)
                    if not (last and k == NK - 1):
                        differ(c + 1, k + 1)
                    if not (last and k >= NK - 2):
                        norm(c + 2, k + 2)
                    pool.wait_ge(x_stored[k % 2], 1 + 16 * (b * (NK // 2) + k // 2))
                    for n in range(2):
                        pool.wait_ge(prod_done, 1 + 2 * c + n + 1)
                        pool.tensor_tensor(x2[:, k % 2, 2 * n:2 * n + 2], x1[:, k, 2 * n:2 * n + 2], prod[:, n],
                                           ALU.add).then_inc(x2_done, 1)

            over_batches(pool, body)

        @block.vector
        def _(dve):
            start_at_one(dve, blend_done, prod_done)

            def residual(c, k, loads):
                dve.wait_ge(x_loaded[k % 2], 32 * loads)
                for n in range(2):
                    tiles = slice(2 * n, 2 * n + 2)
                    if wo is not None:
                        dve.wait_ge(a_ready, 2 * c + n + 1)
                    if n == 0 and not (isinstance(c, int) and c < 3):
                        dve.wait_ge(x2_done, 1 + 2 * (c - 2))
                    op = dve.tensor_tensor(x1[:, k % NK, tiles], xt[:, k % 2, tiles],
                                           ot[:, k % 2, tiles] if wo is None else pA[:, n], ALU.add)
                op.then_inc(x1_done, 1)
                dve.wait_ge(x1_done, c + 1)
                for j in range(NJ):
                    op = dve.bn_stats(stats[:, k % 2, j], x1[:, k % NK, j])
                op.then_inc(stats_done, 1)
                dve.wait_ge(stats_done, c + 1)
                dve.memset(held[:], 0.0)
                for j in range(NJ):
                    op = dve.bn_aggr(meanvar[:, k % 2, j], stats[:, k % 2, j])
                op.then_inc(aggr_done, 1)

            def normal(c, k):
                dve.wait_ge(rstd_done, c + 1)
                if not (isinstance(c, int) and c < 2):
                    dve.wait_ge(xT_ready, 2 * (c - 1))
                for j in range(NJ):
                    op = dve.tensor_scalar(xn[:, k % 2, j], x1[:, k % NK, j], meanvar[:, k % 2, j, 0:1],
                                           rstd[:, k % 2, j:j + 1], ALU.subtract, ALU.mult)
                op.then_inc(xn_done, 1)

            def blend(c, k):
                dve.wait_ge(step_done, c + 1)
                for n, (dst, used) in enumerate(((xk, k_ready), (xr, r_ready))):
                    if not (isinstance(c, int) and c == 0):
                        dve.wait_ge(used, 1 + 2 * (c - 1))
                    for h in range(CH):
                        op = dve.scalar_tensor_tensor(
                            out=dst[:, k % 2, h], in0=step[:, h], scalar=mu[:, n, h:h + 1],
                            in1=xnT[:, k % 2, h, 0:TC], op0=ALU.mult, op1=ALU.add)
                    op.then_inc(blend_done, 1)

            for c in range(2):
                residual(c, c, 1)
                normal(c, c)
            dve.wait_ge(w_loaded, 16 * N_W)
            blend(0, 0)

            def body(b, last):
                for k in range(NK):
                    c = b * NK + k
                    if not (last and k == NK - 1):
                        blend(c + 1, k + 1)
                    if not (last and k >= NK - 2):
                        residual(c + 2, k + 2, turn(b, k + 2))
                    for n in range(2):
                        dve.wait_ge(gate_done, 1 + 2 * c + n + 1)
                        dve.wait_ge(mv_ready, 1 + 2 * c + n + 1)
                        dve.wait_ge(x2_done, 1 + 2 * c)
                        dve.tensor_tensor(prod[:, n], gate[:, n], pKV[:, n], ALU.mult).then_inc(prod_done, 1)
                    if not (last and k >= NK - 2):
                        normal(c + 2, k + 2)

            over_batches(dve, body)

        @block.scalar
        def _(act):
            start_at_one(act, gate_done)

            def copy_oT(c):
                if wo is None:
                    return
                for h in range(CH):
                    act.wait_ge(oT_ready, 2 * c + h + 1)
                    if h == 0:
                        act.wait_ge(a_ready, 2 * c)
                    act.activation(oT[:, h], pA[:, h].rearrange("p a c -> p (a c)"), ACT.Copy).then_inc(oT_done, 1)

            def copy_xnT(c, k):
                act.wait_ge(blend_done, 1 + 2 * c)
                for h in range(CH):
                    act.wait_ge(xT_ready, 2 * c + h + 1)
                    act.activation(xnT[:, k % 2, h, 1:TC + 1], pT[:, h], ACT.Copy).then_inc(xnT_done, 1)

            copy_oT(0)
            copy_oT(1)
            copy_xnT(0, 0)

            def body(b, last):
                for k in range(NK):
                    c = b * NK + k
                    if not (last and k >= NK - 2):
                        copy_oT(c + 2)
                    act.wait_ge(act_k_done, 1 + c)
                    for h in range(CH):
                        act.wait_ge(k_ready, 1 + 2 * c + h + 1)
                        act.activation(relu[:, h], pKV[:, h].rearrange("p a c -> p (a c)"), ACT.Relu
                                       ).then_inc(relu_done, 1)
                    if not (last and k == NK - 1):
                        copy_xnT(c + 1, k + 1)
                    act.wait_ge(prod_done, 1 + 2 * c)
                    for n in range(2):
                        act.wait_ge(r_ready, 1 + 2 * c + n + 1)
                        act.activation(gate[:, n], pR[:, n], ACT.Sigmoid).then_inc(gate_done, 1)

            over_batches(act, body)

        @block.tensor
        def _(pe):
            start_at_one(pe, k_ready, r_ready, mv_ready)
            pe.wait_ge(w_loaded, 16 * N_W)

            def turn_heads(c, k, loads):
                if wo is None:
                    return
                pe.wait_ge(x_loaded[k % 2], 32 * loads)
                pe.wait_ge(x1_done, c)
                for h in range(CH):
                    for j in range(NJ):
                        mm = pe.transpose(pA[:, h].rearrange("p a c -> p (a c)")[:, j * P:(j + 1) * P],
                                          ot[:, k % 2, j, h * P:(h + 1) * P], ident[:])
                    mm.then_inc(oT_ready, 1)

            def project_heads(c):
                if wo is None:
                    return
                pe.wait_ge(oT_done, 2 * c + 2)
                for n in range(2):
                    for a in range(2):
                        t = 2 * n + a
                        for h in range(CH):
                            mm = pe.matmul(pA[:, n, a], oT[:, h, t * P:(t + 1) * P], wo_sb[:, h],
                                           start=(h == 0), stop=(h == CH - 1))
                    mm.then_inc(a_ready, 1)

            def transpose(c, k):
                pe.wait_ge(xn_done, c + 1)
                pe.wait_ge(xnT_done, 2 * c)
                for h in range(CH):
                    for j in range(NJ):
                        mm = pe.transpose(pT[:, h, j * P:(j + 1) * P], xn[:, k % 2, j, h * P:(h + 1) * P], ident[:])
                    mm.then_inc(xT_ready, 1)

            def rows_by(weights, lhs, dst, ready):
                for n in range(2):
                    for a in range(2):
                        t = 2 * n + a
                        for h in range(CH):
                            mm = pe.matmul(dst[:, n, a], lhs[:, h, t * P:(t + 1) * P], weights[:, h],
                                           start=(h == 0), stop=(h == CH - 1))
                    mm.then_inc(ready, 1)

            for c in range(2):
                turn_heads(c, c, 1)
                project_heads(c)
            transpose(0, 0)

            def body(b, last):
                for k in range(NK):
                    c = b * NK + k
                    if not (last and k >= NK - 2):
                        turn_heads(c + 2, k + 2, turn(b, k + 2))
                    pe.wait_ge(blend_done, 1 + 2 * c + 1)
                    pe.wait_ge(prod_done, 1 + 2 * c)
                    for m in range(CH):
                        for h in range(CH):
                            mm = pe.matmul(pKV[:, m].rearrange("p a c -> p (a c)"), wk_sb[:, h, m * P:(m + 1) * P],
                                           xk[:, k % 2, h], start=(h == 0), stop=(h == CH - 1))
                        mm.then_inc(k_ready, 1)
                    if not (last and k == NK - 1):
                        transpose(c + 1, k + 1)
                    pe.wait_ge(blend_done, 1 + 2 * c + 2)
                    pe.wait_ge(gate_done, 1 + 2 * c)
                    rows_by(wr_sb, xr[:, k % 2], pR, r_ready)
                    if not (last and k >= NK - 2):
                        project_heads(c + 2)
                    pe.wait_ge(act_k_done, 1 + c + 1)
                    rows_by(wv_sb, act_k, pKV, mv_ready)

            over_batches(pe, body)


def build(nc, ins, consts, out):
    def scratch(name, shape, dt=F32):
        return nc.dram_tensor(name, shape, dt, kind="Internal").ap()

    qk_parts = scratch("qk_parts", [2, B, 3, C, T], BF16)
    v_rows = scratch("v_rows", [B, W + T + W, H, VW])
    o_rows = scratch("o_rows", [B, T, C])
    x2 = scratch("x_after_first", [B, T, C])
    ffn = [ins[n] for n in ("L0_ffn_W_r", "L0_ffn_W_k", "L0_ffn_W_v", "L0_ffn_mu_r", "L0_ffn_mu_k")]
    project(nc, "proj_a", consts, ins["L0_attn_a_x"], ins["L0_attn_a_Wq"], ins["L0_attn_a_Wk"], ins["L0_attn_a_Wv"],
            None, qk_parts, v_rows)
    attend_full(nc, "full", consts, qk_parts, v_rows, o_rows)
    mix(nc, "mix_a", consts, ins["L0_attn_a_x"], o_rows, ins["L0_attn_a_Wo"], *ffn, x2)
    project(nc, "proj_b", consts, x2, ins["L0_attn_b_Wq"], ins["L0_attn_b_Wk"], ins["L0_attn_b_Wv"],
            [ins[f"L0_attn_b_b{n}"] for n in "qkv"], qk_parts, v_rows)
    attend_band(nc, "band", consts, qk_parts, v_rows, o_rows)
    mix(nc, "mix_b", consts, x2, o_rows, None, *ffn, out)


def constants():
    import numpy as np

    bf16 = mybir.dt.np(BF16)

    def three_parts(a):
        parts = []
        for _ in range(3):
            parts.append(a.astype(bf16))
            a = a - parts[-1].astype(np.float32)
        return parts

    p = np.arange(P)
    eye = np.eye(P, dtype=np.float32)
    slope = three_parts(np.array([2.0 ** (-8.0 * h / H) for h in range(1, H + 1)], np.float32))
    pos = np.arange(T)
    slopes = np.zeros((H, NPOS, T), bf16)
    positions = np.ones((NPOS + 3, T), bf16)
    for s in range(T // POS_STEP):
        for i in range(3):
            slopes[:, 3 * s + i, s * POS_STEP:(s + 1) * POS_STEP] = slope[i][:, None]
            positions[3 * s + i] = (pos // P * P - s * POS_STEP).astype(bf16)
    for i in range(3):
        slopes[:, NPOS - 3 + i] = slope[i][:, None]
        positions[NPOS - 3 + i] = (pos % P).astype(bf16)

    def masked(valid):
        return np.where(valid, 0.0, NEG).astype(bf16)

    c = np.arange(2 * P)
    band = (c[None, :] >= p[:, None]) & (c[None, :] - p[:, None] <= P)
    left, right = c[None, :] >= W, c[None, :] < 3 * W
    lower, upper = p[:, None] >= W, p[:, None] < W
    band_q = np.stack([masked(np.stack(v, 1)) for v in ((band & left, band), (band, band), (band, band & right))], 1)
    band_k = np.stack([masked(np.stack(v, 1)) for v in ((band & lower,) * 2, (band,) * 2, (band & upper,) * 2)], 1)
    return {
        "ident": eye, "identb": eye.astype(bf16),
        "mask_q": masked(p[None, :] <= p[:, None]), "mask_k": masked(p[None, :] >= p[:, None]),
        "slopes": slopes, "positions": positions, "band_q": band_q.astype(np.float32), "band_k": band_k,
    }


_TRANSPOSED = {"L0_attn_a_Wq", "L0_attn_a_Wk", "L0_attn_a_Wv", "L0_attn_a_Wo", "L0_ffn_W_r", "L0_ffn_W_k",
               "L0_ffn_W_v"}


def kernel(**inputs):
    import numpy as _np
    import concourse.bacc as _bacc
    from concourse import mybir as _mybir
    from concourse.bass_utils import run_bass_kernel_spmd as _run

    nc = _bacc.Bacc("TRN2", target_bir_lowering=False, num_devices=1)
    arrays = {}

    def given(name, a):
        arrays[name] = _np.ascontiguousarray(a)
        return nc.dram_tensor(name, a.shape, _mybir.dt.from_np(a.dtype), kind="ExternalInput").ap()

    ins = {n: given(f"in_{n}", _np.asarray(a).T if n in _TRANSPOSED else _np.asarray(a)) for n, a in inputs.items()}
    consts = {n: given(f"const_{n}", a) for n, a in constants().items()}
    out = nc.dram_tensor("out_x", (B, T, C), F32, kind="ExternalOutput").ap()
    build(nc, ins, consts, out)
    r = _run(nc, [arrays], core_ids=[0])
    return r.results[0]["out_x"]
```

```python
from contextlib import ExitStack

import concourse.bass as bass
from concourse import mybir

F32 = mybir.dt.float32
BF16 = mybir.dt.bfloat16
ALU = mybir.AluOpType
ACT = mybir.ActivationFunctionType
AX = mybir.AxisListType

P = 128
B, T, C = 4, 2048, 256
H, D = 16, 16
CH = C // P
NK = 4
TC = T // NK
NJ = TC // P
G = 4
HG = H // G
VW = 32
TILES = T // P
W = 64
EPS = 1e-5
LOWEST = -3e38
NEG = -1e30

Q_PART = [0, 0, 1, 1, 0, 2]
K_PART = [0, 1, 0, 1, 2, 0]
NPROD = len(Q_PART) * D
POS_STEP = 256
NPOS = T // POS_STEP * 3 + 3
FULL_ROWS = NPROD + NPOS + 3
BAND_ROWS = NPROD + 3


def start_at_one(eng, *semaphores):
    for s in semaphores:
        eng.sem_inc(s, 1)


def over_batches(eng, body):
    with eng.Fori(0, B - 1) as b:
        body(b, False)
    body(B - 1, True)


def project(nc, stage, consts, x, wq, wk, wv, bias, qk_parts, v_rows):
    with ExitStack() as ctx:
        def sb(name, shape, dt=F32):
            return ctx.enter_context(nc.sbuf_tensor(f"{stage}_{name}", shape, dt))

        def sem(name):
            return ctx.enter_context(nc.semaphore(f"{stage}_{name}"))

        def psum(name, shape):
            return ctx.enter_context(nc.psum_tensor(f"{stage}_{name}", shape, F32))

        w_sb = [sb(f"w{n}_sb", [P, CH, C]) for n in "qkv"]
        qk_bias = sb("qk_bias", [P, 2, CH])
        v_bias = sb("v_bias", [P, C])
        ident = sb("ident", [P, P])
        zeros = sb("zeros", [W, H * VW])
        xt = sb("xt", [P, 2, NJ, C])
        stats = sb("stats", [P, 2, NJ, 6])
        meanvar = sb("meanvar", [P, 2, NJ, 2])
        vareps = sb("vareps", [P, 2, NJ])
        held = sb("held", [P, 1])
        power = sb("power", [P, NJ])
        eps = sb("eps", [P, NJ])
        rstd = sb("rstd", [P, 2, NJ])
        xn = sb("xn", [P, 2, NJ, C])
        xnT = sb("xnT", [P, 2, CH, TC])
        full = sb("full", [P, 4, TC])
        rest = sb("rest", [P, 4, TC])
        parts = sb("parts", [P, 2, 4, 3, TC], BF16)
        vst = sb("vst", [P, 2, NJ, H, VW])
        pT = psum("pT", [P, CH, TC])
        pQK = psum("pQK", [P, 4, TC])
        pV = psum("pV", [P, 2, 2, C])

        first_loaded = sem("first_loaded")
        w_loaded = sem("w_loaded")
        x_loaded = [sem(f"x_loaded{i}") for i in range(2)]
        const_set = sem("const_set")
        stats_done = sem("stats_done")
        aggr_done = sem("aggr_done")
        vareps_done = sem("vareps_done")
        rstd_done = sem("rstd_done")
        xn_done = sem("xn_done")
        xT_ready = sem("xT_ready")
        xnT_done = sem("xnT_done")
        qk_ready = sem("qk_ready")
        full_done = sem("full_done")
        high_done = sem("high_done")
        rest_done = sem("rest_done")
        mid_done = sem("mid_done")
        low_done = sem("low_done")
        last_rest_done = sem("last_rest_done")
        last_low_done = sem("last_low_done")
        v_ready = sem("v_ready")
        v_done = sem("v_done")
        qk_stored = [sem(f"qk_stored{i}") for i in range(2)]
        v_stored = [sem(f"v_stored{i}") for i in range(2)]
        pad_stored = sem("pad_stored")
        n_w = 3 if bias is None else 6

        block = ctx.enter_context(nc.Block())

        @block.sync
        def _(sp):
            start_at_one(sp, *qk_stored, *v_stored)
            def load_x(b, k):
                sp.dma_start(xt[:, k % 2], x[b, k * TC:(k + 1) * TC, :].rearrange(
                    "(j p) c -> p j c", p=P)).then_inc(x_loaded[k % 2], 16)

            load_x(0, 0)
            sp.dma_start(ident[:], consts["ident"]).then_inc(first_loaded, 16)
            for w, src in zip(w_sb, (wq, wk, wv)):
                sp.dma_start(w[:], src.rearrange("(h p) d -> p h d", p=P)).then_inc(w_loaded, 16)
            if bias is not None:
                with nc.allow_non_contiguous_dma(reason="256 biases, one a partition"):
                    for n in range(2):
                        sp.dma_start(qk_bias[:, n], bias[n].rearrange("(h p) -> p h", p=P)).then_inc(w_loaded, 16)
                sp.dma_start(v_bias[:], bias[2].rearrange("(a c) -> a c", a=1).to_broadcast([P, C])
                             ).then_inc(w_loaded, 16)
            load_x(0, 1)
            for k in range(2):
                sp.wait_ge(xn_done, k + 1)
                load_x(0, k + 2)
            sp.wait_ge(const_set, 4)
            for b in range(B):
                for at in (0, W + T):
                    sp.dma_start(v_rows[b, at:at + W].rearrange("t h d -> t (h d)"), zeros[:]
                                 ).then_inc(pad_stored, 16)

            def body(b, last):
                for k in range(NK):
                    c = b * NK + k
                    if not last:
                        sp.wait_ge(xn_done, c + 3)
                        load_x(b + 1, k)
                    for i in range(4):
                        if i < 3:
                            sp.wait_ge(low_done, 1 + 3 * c + i + 1)
                        else:
                            sp.wait_ge(last_low_done, 1 + c + 1)
                        sp.dma_start(qk_parts[i // 2, b, :, i % 2 * P:(i % 2 + 1) * P, k * TC:(k + 1) * TC]
                                     .rearrange("s p t -> p s t"), parts[:, k % 2, i]
                                     ).then_inc(qk_stored[k % 2], 16)
                    sp.wait_ge(v_done, 1 + 2 * c + 2)
                    sp.dma_start(v_rows[b, W + k * TC:W + (k + 1) * TC].rearrange("(j p) h d -> p j (h d)", p=P),
                                 vst[:, k % 2].rearrange("p j h d -> p j (h d)")).then_inc(v_stored[k % 2], 16)

            over_batches(sp, body)
            for s in qk_stored:
                sp.wait_ge(s, 1 + 64 * B * NK // 2)
            for s in v_stored:
                sp.wait_ge(s, 1 + 16 * B * NK // 2)
            sp.wait_ge(pad_stored, 16 * B * 2)

        @block.gpsimd
        def _(pool):
            start_at_one(pool, low_done)
            pool.memset(eps[:], EPS)
            pool.memset(power[:], -0.5).then_inc(const_set, 1)
            pool.memset(zeros[:], 0.0).then_inc(const_set, 1)
            for i in range(2):
                pool.memset(vst[:, i, :, :, D:VW], 0.0)
            pool.memset(rest[:, 0, 0:1], 0.0).then_inc(const_set, 1)
            pool.wait_ge(const_set, 3)
            for i in range(2):
                last = pool.memset(vst[:, i, :, :, D:D + 1], 1.0)
            last.then_inc(const_set, 1)

            def norm(c, k):
                pool.wait_ge(aggr_done, c + 1)
                pool.tensor_tensor(vareps[:, k % 2], meanvar[:, k % 2, :, 1], eps[:], ALU.add).then_inc(vareps_done, 1)
                pool.wait_ge(vareps_done, c + 1)
                pool.tensor_tensor(rstd[:, k % 2], vareps[:, k % 2], power[:], ALU.pow).then_inc(rstd_done, 1)

            norm(0, 0)
            norm(1, 1)

            def body(b, last):
                for k in range(NK):
                    c = b * NK + k

                    def take_high(i):
                        pool.wait_ge(high_done, 4 * c + i + 1)
                        pool.tensor_tensor(rest[:, i], full[:, i], parts[:, k % 2, i, 0], ALU.subtract
                                           ).then_inc(rest_done, 1)

                    def take_mid(i):
                        pool.wait_ge(mid_done, 4 * c + i + 1)
                        pool.tensor_tensor(parts[:, k % 2, i, 2], rest[:, i], parts[:, k % 2, i, 1], ALU.subtract
                                           ).then_inc(low_done, 1)

                    take_high(0)
                    take_high(1)
                    take_mid(0)
                    take_high(2)
                    take_mid(1)
                    if not (last and k >= NK - 2):
                        norm(c + 2, k + 2)
                    take_mid(2)

            over_batches(pool, body)

        @block.vector
        def _(dve):
            start_at_one(dve, full_done, v_done, last_low_done)
            if bias is None:
                dve.memset(qk_bias[:], 0.0)
                dve.memset(v_bias[:], 0.0).then_inc(stats_done, 1)
                dve.wait_ge(stats_done, 1)
            first = 1 if bias is None else 0

            def statistics(c, k, turn):
                dve.wait_ge(x_loaded[k % 2], 16 * turn)
                for j in range(NJ):
                    dve.bn_stats(stats[:, k % 2, j], xt[:, k % 2, j]).then_inc(stats_done, 1)
                dve.wait_ge(stats_done, first + NJ * (c + 1))
                dve.memset(held[:], 0.0)
                for j in range(NJ):
                    last = dve.bn_aggr(meanvar[:, k % 2, j], stats[:, k % 2, j])
                last.then_inc(aggr_done, 1)

            def normal(c, k):
                dve.wait_ge(rstd_done, c + 1)
                if not (isinstance(c, int) and c < 2):
                    dve.wait_ge(xT_ready, 1 + 2 * (c - 1))
                for j in range(NJ):
                    last = dve.tensor_scalar(xn[:, k % 2, j], xt[:, k % 2, j], meanvar[:, k % 2, j, 0:1],
                                             rstd[:, k % 2, j:j + 1], ALU.subtract, ALU.mult)
                last.then_inc(xn_done, 1)

            for c in range(2):
                statistics(c, c, 1)
                normal(c, c)
            dve.wait_ge(w_loaded, 16 * n_w)
            dve.wait_ge(const_set, 4)

            def body(b, last):
                for k in range(NK):
                    c = b * NK + k
                    for i in range(4):
                        dve.wait_ge(qk_ready, 4 * c + i + 1)
                        if i < 3:
                            dve.wait_ge(low_done, 1 + 3 * c)
                        else:
                            dve.wait_ge(last_low_done, 1 + c)
                        dve.tensor_scalar(full[:, i], pQK[:, i], qk_bias[:, i // 2, i % 2:i % 2 + 1],
                                          0.25 if i < 2 else 1.0, ALU.add, ALU.mult).then_inc(full_done, 1)
                    if not (last and k >= NK - 2):
                        statistics(c + 2, k + 2, b * (NK // 2) + (k + 2) // 2 + 1)
                    dve.wait_ge(high_done, 4 * c + 4)
                    dve.tensor_tensor(rest[:, 3], full[:, 3], parts[:, k % 2, 3, 0], ALU.subtract
                                      ).then_inc(last_rest_done, 1)
                    for n in range(2):
                        dve.wait_ge(v_ready, 1 + 2 * c + n + 1)
                        if n == 0:
                            dve.wait_ge(v_stored[k % 2], 1 + 16 * (b * (NK // 2) + k // 2))
                        for j in range(2):
                            op = dve.tensor_tensor(
                                vst[:, k % 2, 2 * n + j, :, 0:D], pV[:, n, j].rearrange("p (h d) -> p h d", d=D),
                                v_bias[:].rearrange("p (h d) -> p h d", d=D), ALU.add)
                        op.then_inc(v_done, 1)
                    if not (last and k >= NK - 2):
                        normal(c + 2, k + 2)
                    dve.wait_ge(mid_done, 4 * c + 4)
                    dve.tensor_tensor(parts[:, k % 2, 3, 2], rest[:, 3], parts[:, k % 2, 3, 1], ALU.subtract
                                      ).then_inc(last_low_done, 1)

            over_batches(dve, body)

        @block.scalar
        def _(act):
            def copy_T(c, k):
                for h in range(CH):
                    act.wait_ge(xT_ready, 1 + 2 * c + h + 1)
                    if h == 0 and not (isinstance(c, int) and c == 0):
                        act.wait_ge(v_ready, 1 + 2 * (c - 1))
                    act.activation(xnT[:, k % 2, h], pT[:, h], ACT.Copy).then_inc(xnT_done, 1)

            copy_T(0, 0)

            def body(b, last):
                for k in range(NK):
                    c = b * NK + k

                    def high(i):
                        act.wait_ge(full_done, 1 + 4 * c + i + 1)
                        act.wait_ge(qk_stored[k % 2], 1 + 64 * (b * (NK // 2) + k // 2))
                        act.activation(parts[:, k % 2, i, 0], full[:, i], ACT.Copy).then_inc(high_done, 1)

                    def mid(i):
                        if i < 3:
                            act.wait_ge(rest_done, 3 * c + i + 1)
                        else:
                            act.wait_ge(last_rest_done, c + 1)
                        act.activation(parts[:, k % 2, i, 1], rest[:, i], ACT.Copy).then_inc(mid_done, 1)

                    high(0)
                    high(1)
                    mid(0)
                    high(2)
                    high(3)
                    if not (last and k == NK - 1):
                        copy_T(c + 1, k + 1)
                    for i in range(1, 4):
                        mid(i)

            over_batches(act, body)

        @block.tensor
        def _(pe):
            start_at_one(pe, xT_ready, v_ready)
            pe.wait_ge(first_loaded, 16)

            def transpose(c, k):
                pe.wait_ge(xn_done, c + 1)
                pe.wait_ge(xnT_done, 2 * c)
                for h in range(CH):
                    for j in range(NJ):
                        last = pe.transpose(pT[:, h, j * P:(j + 1) * P], xn[:, k % 2, j, h * P:(h + 1) * P], ident[:])
                    last.then_inc(xT_ready, 1)

            transpose(0, 0)
            pe.wait_ge(w_loaded, 16 * n_w)

            def body(b, last):
                for k in range(NK):
                    c = b * NK + k
                    pe.wait_ge(xnT_done, 2 * c + 2)
                    pe.wait_ge(full_done, 1 + 4 * c)
                    for i in range(4):
                        for h in range(CH):
                            mm = pe.matmul(pQK[:, i], w_sb[i // 2][:, h, i % 2 * P:(i % 2 + 1) * P],
                                           xnT[:, k % 2, h], start=(h == 0), stop=(h == CH - 1))
                        mm.then_inc(qk_ready, 1)
                    if not (last and k == NK - 1):
                        transpose(c + 1, k + 1)
                    pe.wait_ge(v_done, 1 + 2 * c)
                    for n in range(2):
                        for j in range(2):
                            t = 2 * n + j
                            for h in range(CH):
                                mm = pe.matmul(pV[:, n, j], xnT[:, k % 2, h, t * P:(t + 1) * P],
                                               w_sb[2][:, h], start=(h == 0), stop=(h == CH - 1))
                        mm.then_inc(v_ready, 1)

            over_batches(pe, body)


UNIT = [(q, t) for q in range(NK) for t in range(NJ * (q + 1))]
UNITS = len(UNIT)
CHUNK_ENDS = [NJ * (q + 1) * (q + 2) // 2 - 1 for q in range(NK)]


def unit_width(u):
    q, t = UNIT[u]
    return TC - max(0, t * P - q * TC)


def piece_width(i):
    h, t, s = PIECES[i]
    return min(TC, (t + 1) * P - s * TC)


def alternate(order):
    half = len(order) // 2
    return [i for pair in zip(order[half:][::-1], order[:half]) for i in pair]


def shares(unit_costs, piece_costs, by):
    whole, total, seen, done, out = sum(unit_costs[:by]), sum(piece_costs), 0, 0, []
    for u, cost in enumerate(unit_costs):
        seen += cost
        while done < len(piece_costs) and (sum(piece_costs[:done + 1]) <= total * seen / whole or u >= by - 1):
            done += 1
        out.append(done)
    return out


PIECES = alternate([(h, t, s) for t in range(TILES) for s in range(t // NJ + 1) for h in range(HG)])
LEAD_PIECES = sorted(range(len(PIECES)), key=lambda i: PIECES[i][0])
MAX_AT = UNITS - 5
FLIP_AT = MAX_AT + 1
UNIT_COST = PIECE_COST = 60
PIECES_BY = shares([unit_width(u) + UNIT_COST for u in range(UNITS)],
                   [piece_width(i) + PIECE_COST for i in range(len(PIECES))], MAX_AT)
CUTS = (0.3, 0.6)
RING_BANKS = 3
LEAD_BANKS = RING_BANKS + 4


def unit_pieces(u, by):
    return range(by[u - 1] if u else 0, by[u])


def ring_uses(steps, pieces_by, ends, lag, flip_at, last):
    out, place = [], 0
    for at in range(G * steps + 2):
        g, u = divmod(at, steps)
        ahead = g < G and not (last and g == G - 1)
        uses = [("piece", g, i) for i in unit_pieces(u, pieces_by)] if ahead else []
        if at >= lag and (at - lag) % steps in ends:
            past, v = divmod(at - lag, steps)
            uses.append(("turn", past, ends.index(v)))
        if ahead and u == flip_at:
            uses.append(("flip", g, 0))
        out.append([(*use, place + i) for i, use in enumerate(uses)])
        place += len(uses)
    return out


def uses_before(b, place, lead, uses):
    return lead + b * sum(len(step) for step in uses) + place


def bank_free(place):
    return max(0, place - RING_BANKS + 1)


def attend_full(nc, stage, consts, qk_parts, v_rows, o_rows):
    with ExitStack() as ctx:
        def sb(name, shape, dt=F32):
            return ctx.enter_context(nc.sbuf_tensor(f"{stage}_{name}", shape, dt))

        def sem(name):
            return ctx.enter_context(nc.semaphore(f"{stage}_{name}"))

        def psum(name, shape):
            return ctx.enter_context(nc.psum_tensor(f"{stage}_{name}", shape, F32))

        q_op = [sb(f"q_op{g}", [FULL_ROWS, HG, T], BF16) for g in range(G)]
        k_op = [sb(f"k_op{g}", [FULL_ROWS, HG, T], BF16) for g in range(G)]
        v_sb = [sb(f"v_sb{i}", [P, TILES, HG, VW]) for i in range(2)]
        probs = sb("probs", [P, 2, HG, TC])
        ident = sb("ident", [P, P])
        identb = sb("identb", [P, P], BF16)
        mask_q = sb("mask_q", [P, P], BF16)
        mask_k = sb("mask_k", [P, P], BF16)
        maxes = sb("maxes", [P, HG, TILES, NK])
        negmax = sb("negmax", [P, P])
        max_rest = sb("max_rest", [HG * TILES, 2, P])
        max_parts = sb("max_parts", [HG * TILES, 3, P], BF16)
        o_sb = sb("o_sb", [P, TC])
        inv = sb("inv", [P, NJ, HG, 1])
        o_norm = sb("o_norm", [P, NJ, HG, D])
        pS = psum("pS", [P, 2, 2, TC])
        pM = psum("pM", [P, RING_BANKS, TC])
        pO = psum("pO", [P, TC])

        c_loaded = sem("c_loaded")
        half_loaded = sem("half_loaded")
        qk_loaded = [sem(f"qk_loaded{g}") for g in range(G)]
        v_loaded = [sem(f"v_loaded{i}") for i in range(2)]
        max_loaded = sem("max_loaded")
        maxes_set = sem("maxes_set")
        s_ready = sem("s_ready")
        p_ready = sem("p_ready")
        p_used = sem("p_used")
        ring_ready = sem("ring_ready")
        ring_read = sem("ring_read")
        negmax_done = sem("negmax_done")
        split_step = sem("split_step")
        o_copied = sem("o_copied")
        inv_done = sem("inv_done")
        o_stored = sem("o_stored")
        N_C, N_QK = 4, 13

        def n_pos(g):
            return 1 if g == 0 else 2


        pS_banks = [pS[:, i // 2, i % 2] for i in range(4)]

        def lead_bank(i):
            i = i % LEAD_BANKS
            return pM[:, i] if i < RING_BANKS else pS_banks[i - RING_BANKS]

        lead = len(PIECES) + 1
        turn_uses = ring_uses(UNITS, PIECES_BY, CHUNK_ENDS, 2, FLIP_AT, False)
        last_uses = ring_uses(UNITS, PIECES_BY, CHUNK_ENDS, 2, FLIP_AT, True)

        def uses_until(b, place):
            return uses_before(b, place, lead, turn_uses)

        block = ctx.enter_context(nc.Block())

        @block.sync
        def _(sp):
            start_at_one(sp, o_stored)
            def load_qk(b, g, first=0, end=HG, signal=None):
                signal = signal or qk_loaded[g]
                heads = slice((g * HG + first) * D, (g * HG + end) * D)
                for s in range(6):
                    for n, (dst, part) in enumerate(((q_op, Q_PART), (k_op, K_PART))):
                        sp.dma_start(dst[g][s * D:(s + 1) * D, first:end], qk_parts[n, b, part[s], heads].rearrange(
                            "(h d) t -> d h t", d=D)).then_inc(signal, 16)
                sp.dma_start(q_op[g][NPROD:NPROD + NPOS, first:end],
                             consts["slopes"][g * HG + first:g * HG + end].rearrange("h r t -> r h t")
                             ).then_inc(signal, 16)

            def load_v(b, g):
                sp.dma_start(v_sb[g % 2][:].rearrange("p t h d -> p t (h d)"),
                             v_rows[b, W:W + T, g * HG:(g + 1) * HG].rearrange("(t p) h d -> p t (h d)", p=P)
                             ).then_inc(v_loaded[g % 2], 16)

            def load_positions(g, half, signal):
                sp.dma_start(k_op[g][NPROD:FULL_ROWS, 2 * half:2 * half + 2], consts["positions"].rearrange(
                    "r (a t) -> r a t", a=1).to_broadcast([NPOS + 3, 2, T])).then_inc(signal, 16)

            for dst, name in ((ident, "ident"), (identb, "identb"), (mask_q, "mask_q"),
                              (mask_k, "mask_k")):
                sp.dma_start(dst[:], consts[name]).then_inc(c_loaded, 16)
            for half, signal in enumerate((half_loaded, qk_loaded[0])):
                load_positions(0, half, signal)
                load_qk(0, 0, 2 * half, 2 * half + 2, signal)
            load_v(0, 0)

            def load_group(g):
                for half in range(2):
                    load_positions(g, half, qk_loaded[g])
                load_qk(0, g)

            load_group(1)

            def store_max(n, g):
                sp.wait_ge(split_step, 4 * n + 4)
                for s in range(3):
                    row = FULL_ROWS - 3 + s
                    sp.dma_start(q_op[g][row:row + 1].rearrange("r h (t q) -> r (h t) q", q=P),
                                 max_parts[:, s]).then_inc(max_loaded, 16)

            store_max(0, 0)
            load_v(0, 1)
            load_group(2)
            load_group(3)

            def body(b, last):
                for kind, g, q, place in sum(last_uses if last else turn_uses, []):
                    if kind == "flip":
                        store_max(b * G + g + 1, (g + 1) % G)
                    if kind != "turn":
                        continue
                    sp.wait_ge(ring_read, uses_until(b, place + 1))
                    store_heads(sp, o_rows, o_norm, o_stored, b, g, q)
                    if q < NK - 1:
                        continue
                    sp.wait_ge(p_used, UNITS * (b * G + g + 1) + 2)
                    if not last:
                        load_qk(b + 1, g)
                    if not (last and g >= 2):
                        load_v(b + (g + 2) // G, (g + 2) % G)

            over_batches(sp, body)
            sp.wait_ge(o_stored, 1 + 16 * B * G * NK)

        @block.gpsimd
        def _(pool):
            pool.memset(negmax[:, HG * TILES:], 0.0)
            pool.memset(maxes[:], LOWEST).then_inc(maxes_set, 1)

        @block.tensor
        def _(pe):
            pe.sem_inc(p_used, 2)
            pe.wait_ge(c_loaded, 16 * N_C)

            def piece_into(bank, g, i):
                h, t, s = PIECES[i]
                w = piece_width(i)
                diag = s == t // NJ
                mm = pe.matmul(bank[:, 0:w], q_op[g][0:FULL_ROWS - 3, h, t * P:(t + 1) * P],
                               k_op[g][0:FULL_ROWS - 3, h, s * TC:s * TC + w], start=True, stop=not diag)
                if diag:
                    mm = pe.matmul(bank[:, w - P:w], identb[:], mask_q[:], start=False, stop=True)
                mm.then_inc(ring_ready, 1)

            def take_bank(b, place):
                pe.wait_ge(ring_read, uses_until(b, bank_free(place)))
                return pM[:, place % RING_BANKS]

            def flip_maxima(bank, n):
                pe.wait_ge(negmax_done, n + 1)
                pe.transpose(bank[:, 0:P], negmax[:], ident[:]).then_inc(ring_ready, 1)

            def turn_sums(bank, n, q):
                pe.wait_ge(o_copied, 1 + NK * n + q + 1)
                for j in range(NJ):
                    mm = pe.transpose(bank[:, j * P:(j + 1) * P], o_sb[:, j * P:(j + 1) * P], ident[:])
                mm.then_inc(ring_ready, 1)

            def use_ring(b, use):
                kind, g, i, place = use
                bank = take_bank(b, place)
                if kind == "piece":
                    piece_into(bank, (g + 1) % G, i)
                elif kind == "turn":
                    turn_sums(bank, b * G + g, i)
                else:
                    flip_maxima(bank, b * G + g + 1)

            def scores(n, g, u, pair):
                q, t = UNIT[u]
                lo = max(0, t * P - q * TC)
                pe.wait_ge(p_ready, 2 * (UNITS * n + u) + pair + 1)
                for a in range(2):
                    h = 2 * pair + a
                    diag = t * P >= q * TC
                    mm = pe.matmul(pS[:, pair, a, lo:TC], k_op[g][:, h, t * P:(t + 1) * P],
                                   q_op[g][:, h, q * TC + lo:(q + 1) * TC], start=True, stop=not diag)
                    if diag:
                        mm = pe.matmul(pS[:, pair, a, lo:lo + P], identb[:], mask_k[:], start=False, stop=True)
                mm.then_inc(s_ready, 1)

            def values(n, g, u):
                q, t = UNIT[u]
                lo = max(0, t * P - q * TC)
                pe.wait_ge(p_ready, 2 * (UNITS * n + u + 1) + 2)
                if t == 0:
                    pe.wait_ge(o_copied, 1 + NK * n + q)
                for h in range(HG):
                    mm = pe.matmul(pO[VW * h:VW * (h + 1), lo:TC], v_sb[g % 2][:, t, h], probs[:, u % 2, h, lo:TC],
                                   start=(t == 0), stop=(u in CHUNK_ENDS))
                mm.then_inc(p_used, 1)

            pe.wait_ge(half_loaded, 16 * (1 + N_QK))
            for at, i in enumerate(LEAD_PIECES):
                if at == len(PIECES) // 2:
                    pe.wait_ge(qk_loaded[0], 16 * (1 + N_QK))
                if at >= LEAD_BANKS:
                    pe.wait_ge(ring_read, at - LEAD_BANKS + 1)
                piece_into(lead_bank(at), 0, i)
            flip_maxima(lead_bank(lead - 1), 0)

            def body(b, last):
                for at, uses in enumerate(last_uses if last else turn_uses):
                    g, u = divmod(at, UNITS)
                    n = b * G + g
                    pieces = [use for use in uses if use[0] == "piece"]
                    cuts = [round(len(pieces) * f) for f in CUTS]
                    if g < G:
                        if u == 0:
                            pe.wait_ge(max_loaded, 48 * (n + 1))
                            pe.wait_ge(v_loaded[g % 2], 16 * (b * 2 + g // 2 + 1))
                            if not (last and g == G - 1):
                                loads = n_pos((g + 1) % G) + N_QK * (b + (g + 1) // G + 1)
                                pe.wait_ge(qk_loaded[(g + 1) % G], 16 * loads)
                        scores(n, g, u, 0)
                        for use in pieces[:cuts[0]]:
                            use_ring(b, use)
                        scores(n, g, u, 1)
                        for use in pieces[cuts[0]:cuts[1]]:
                            use_ring(b, use)
                    if 1 <= at <= G * UNITS:
                        past, v = divmod(at - 1, UNITS)
                        values(b * G + past, past, v)
                    for use in uses[cuts[1]:]:
                        use_ring(b, use)

            over_batches(pe, body)

        @block.scalar
        def _(act):
            act.sem_inc(p_ready, 2)

            def body(b, last):
                for g in range(G):
                    n = b * G + g
                    for u in range(UNITS):
                        q, t = UNIT[u]
                        lo = max(0, t * P - q * TC)
                        act.wait_ge(p_used, UNITS * n + u + 1)
                        for pair in range(2):
                            act.wait_ge(s_ready, 2 * (UNITS * n + u) + pair + 1)
                            act.activation(probs[:, u % 2, 2 * pair:2 * pair + 2, lo:TC], pS[:, pair, :, lo:TC],
                                           ACT.Exp).then_inc(p_ready, 1)

            over_batches(act, body)

        @block.vector
        def _(dve):
            start_at_one(dve, o_copied)
            def piece(bank, used, i):
                h, t, s = PIECES[i]
                dve.wait_ge(ring_ready, used + 1)
                dve.reduce_max(maxes[:, h, t, s:s + 1], bank[:, 0:piece_width(i)], AX.X).then_inc(ring_read, 1)

            def finish_maxima(used):
                dve.wait_ge(ring_read, used)
                dve.tensor_reduce(negmax[:, 0:HG * TILES], maxes[:].rearrange("p h t s -> p (h t) s"), AX.X, ALU.max,
                                  negate=True).then_inc(negmax_done, 1)

            def split_maxima(bank, n, used):
                split_rows(dve, bank, n, used, max_parts, max_rest, ring_ready, ring_read, max_loaded, split_step)

            dve.wait_ge(maxes_set, 1)
            for at, i in enumerate(LEAD_PIECES):
                piece(lead_bank(at), at, i)
            finish_maxima(lead - 1)
            split_maxima(lead_bank(lead - 1), 0, lead - 1)

            def copy_sums(n, q):
                dve.wait_ge(p_used, UNITS * n + CHUNK_ENDS[q] + 1 + 2)
                dve.tensor_copy(o_sb[:], pO[:]).then_inc(o_copied, 1)

            def body(b, last):
                for at, uses in enumerate(last_uses if last else turn_uses):
                    g, u = divmod(at, UNITS)
                    for kind, _, i, place in uses:
                        if kind == "piece":
                            piece(pM[:, place % RING_BANKS], uses_until(b, place), i)
                            pieces_end = place + 1
                    if at >= 1 and (at - 1) % UNITS in CHUNK_ENDS:
                        past, v = divmod(at - 1, UNITS)
                        copy_sums(b * G + past, CHUNK_ENDS.index(v))
                    if u == MAX_AT and g < G and not (last and g == G - 1):
                        finish_maxima(uses_until(b, pieces_end))
                    for kind, past, i, place in uses:
                        bank, used = pM[:, place % RING_BANKS], uses_until(b, place)
                        if kind == "turn":
                            normalise(dve, bank, used, b * G + past, i, inv, o_norm, ring_ready, inv_done, o_stored,
                                      ring_read)
                        elif kind == "flip":
                            split_maxima(bank, b * G + past + 1, used)

            over_batches(dve, body)


def normalise(dve, bank, used, n, q, inv, o_norm, ring_ready, inv_done, o_stored, ring_read):
    sums = bank.rearrange("p (j h d) -> p j h d", j=NJ, h=HG)
    dve.wait_ge(ring_ready, used + 1)
    dve.reciprocal(inv[:], sums[:, :, :, D:D + 1]).then_inc(inv_done, 1)
    dve.wait_ge(inv_done, NK * n + q + 1)
    dve.wait_ge(o_stored, 1 + 16 * (NK * n + q))
    dve.tensor_tensor(o_norm[:], sums[:, :, :, 0:D], inv[:].to_broadcast([P, NJ, HG, D]), ALU.mult
                      ).then_inc(ring_read, 1)


def store_heads(sp, o_rows, o_norm, o_stored, b, g, q):
    sp.dma_start(o_rows[b, q * TC:(q + 1) * TC, g * HG * D:(g + 1) * HG * D].rearrange("(j p) c -> p j c", p=P),
                 o_norm[:].rearrange("p j h d -> p j (h d)")).then_inc(o_stored, 16)


def split_rows(dve, bank, n, used, max_parts, max_rest, ring_ready, ring_read, max_loaded, split_step):
    flipped = bank[0:HG * TILES, 0:P]
    dve.wait_ge(ring_ready, used + 1)
    dve.wait_ge(max_loaded, 48 * n)
    dve.tensor_copy(max_parts[:, 0], flipped).then_inc(split_step, 1)
    dve.wait_ge(split_step, 4 * n + 1)
    dve.tensor_tensor(max_rest[:, 0], flipped, max_parts[:, 0], ALU.subtract).then_inc(ring_read, 1)
    dve.wait_ge(ring_read, used + 1)
    dve.tensor_copy(max_parts[:, 1], max_rest[:, 0]).then_inc(split_step, 1)
    dve.wait_ge(split_step, 4 * n + 2)
    dve.tensor_tensor(max_rest[:, 1], max_rest[:, 0], max_parts[:, 1], ALU.subtract).then_inc(split_step, 1)
    dve.wait_ge(split_step, 4 * n + 3)
    dve.tensor_copy(max_parts[:, 2], max_rest[:, 1]).then_inc(split_step, 1)


KT = TILES + 1
BAND_PIECES = [(h, t) for t in range(0, TILES, 2) for h in range(HG)]
BAND_LEAD_PIECES = sorted(range(len(BAND_PIECES)), key=lambda i: BAND_PIECES[i][0])
BAND_MAX_AT = KT - 5
BAND_FLIP_AT = BAND_MAX_AT + 1
BAND_PIECES_BY = shares([1] * KT, [1] * len(BAND_PIECES), BAND_MAX_AT)
BAND_ENDS = [NJ * (q + 1) - 1 for q in range(NK)]
RING = 4


def attend_band(nc, stage, consts, qk_parts, v_rows, o_rows):
    with ExitStack() as ctx:
        def sb(name, shape, dt=F32):
            return ctx.enter_context(nc.sbuf_tensor(f"{stage}_{name}", shape, dt))

        def sem(name):
            return ctx.enter_context(nc.semaphore(f"{stage}_{name}"))

        def psum(name, shape):
            return ctx.enter_context(nc.psum_tensor(f"{stage}_{name}", shape, F32))

        q_op = [sb(f"q_op{g}", [BAND_ROWS, HG, T], BF16) for g in range(G)]
        k_op = [sb(f"k_op{g}", [BAND_ROWS, HG, W + T + W], BF16) for g in range(G)]
        v_sb = [sb(f"v_sb{i}", [P, KT, HG, VW]) for i in range(2)]
        probs = sb("probs", [P, RING, HG, 2 * P])
        ident = sb("ident", [P, P])
        identb = sb("identb", [P, P], BF16)
        mask_q = sb("mask_q", [P, 3, 2, 2 * P])
        mask_k = sb("mask_k", [P, 3, 2, 2 * P], BF16)
        held = sb("held", [P, LEAD_BANKS])
        masked = sb("masked", [P, LEAD_BANKS, 2, 2 * P], BF16)
        maxes = sb("maxes", [P, HG, TILES])
        negmax = sb("negmax", [P, P])
        max_rest = sb("max_rest", [HG * TILES, 2, P])
        max_parts = sb("max_parts", [HG * TILES, 3, P], BF16)
        o_sb = sb("o_sb", [P, TC])
        inv = sb("inv", [P, NJ, HG, 1])
        o_norm = sb("o_norm", [P, NJ, HG, D])
        pS = psum("pS", [P, 2, HG, 2 * P])
        pM = psum("pM", [P, RING_BANKS, TC])
        pO = psum("pO", [P, TC])

        c_loaded = sem("c_loaded")
        pads_set = sem("pads_set")
        half_loaded = sem("half_loaded")
        qk_loaded = [sem(f"qk_loaded{g}") for g in range(G)]
        v_loaded = [sem(f"v_loaded{i}") for i in range(2)]
        max_loaded = sem("max_loaded")
        s_ready = sem("s_ready")
        p_ready = sem("p_ready")
        o_ready = sem("o_ready")
        ring_ready = sem("ring_ready")
        ring_read = sem("ring_read")
        negmax_done = sem("negmax_done")
        split_step = sem("split_step")
        o_copied = sem("o_copied")
        inv_done = sem("inv_done")
        o_stored = sem("o_stored")
        N_C, N_QK = 4, 12

        def n_pos(g):
            return 1


        pS_banks = [pS[:, i // 2, i % 2 * 2:i % 2 * 2 + 2].rearrange("p a c -> p (a c)") for i in range(4)]

        def lead_bank(i):
            i = i % LEAD_BANKS
            return pM[:, i] if i < RING_BANKS else pS_banks[i - RING_BANKS]

        lead = len(BAND_PIECES) + 1
        turn_uses = ring_uses(KT, BAND_PIECES_BY, BAND_ENDS, 3, BAND_FLIP_AT, False)
        last_uses = ring_uses(KT, BAND_PIECES_BY, BAND_ENDS, 3, BAND_FLIP_AT, True)

        def uses_until(b, place):
            return uses_before(b, place, lead, turn_uses)

        block = ctx.enter_context(nc.Block())

        @block.sync
        def _(sp):
            start_at_one(sp, o_stored)
            def load_qk(b, g, first=0, end=HG, signal=None):
                signal = signal or qk_loaded[g]
                heads = slice((g * HG + first) * D, (g * HG + end) * D)
                for s in range(6):
                    rows = slice(s * D, (s + 1) * D)
                    sp.dma_start(q_op[g][rows, first:end], qk_parts[0, b, Q_PART[s], heads].rearrange(
                        "(h d) t -> d h t", d=D)).then_inc(signal, 16)
                    sp.dma_start(k_op[g][rows, first:end, W:W + T], qk_parts[1, b, K_PART[s], heads].rearrange(
                        "(h d) t -> d h t", d=D)).then_inc(signal, 16)

            def load_v(b, g):
                sp.dma_start(v_sb[g % 2][:].rearrange("p t h d -> p t (h d)"),
                             v_rows[b, :, g * HG:(g + 1) * HG].rearrange("(t p) h d -> p t (h d)", p=P)
                             ).then_inc(v_loaded[g % 2], 16)

            for dst, name in ((ident, "ident"), (identb, "identb"), (mask_q, "band_q"),
                              (mask_k, "band_k")):
                sp.dma_start(dst[:], consts[name]).then_inc(c_loaded, 16)
            def load_group(g, first=0, end=HG, signal=None):
                load_qk(0, g, first, end, signal)
                sp.dma_start(k_op[g][NPROD:BAND_ROWS, first:end, W:W + T], consts["positions"][NPOS:NPOS + 3].rearrange(
                    "r (a t) -> r a t", a=1).to_broadcast([3, end - first, T])).then_inc(signal or qk_loaded[g], 16)

            load_group(0, 0, 2, half_loaded)
            load_group(0, 2, 4)
            load_v(0, 0)
            load_group(1)

            def store_max(n, g):
                sp.wait_ge(split_step, 4 * n + 4)
                for s in range(3):
                    row = BAND_ROWS - 3 + s
                    sp.dma_start(q_op[g][row:row + 1].rearrange("r h (t q) -> r (h t) q", q=P),
                                 max_parts[:, s]).then_inc(max_loaded, 16)

            store_max(0, 0)
            load_v(0, 1)
            load_group(2)
            load_group(3)

            def body(b, last):
                for kind, g, q, place in sum(last_uses if last else turn_uses, []):
                    if kind == "flip":
                        store_max(b * G + g + 1, (g + 1) % G)
                    if kind != "turn":
                        continue
                    sp.wait_ge(ring_read, uses_until(b, place + 1))
                    store_heads(sp, o_rows, o_norm, o_stored, b, g, q)
                    if q < NK - 1:
                        continue
                    sp.wait_ge(o_ready, 1 + TILES * (b * G + g + 1))
                    if not last:
                        load_qk(b + 1, g)
                    if not (last and g >= 2):
                        load_v(b + (g + 2) // G, (g + 2) % G)

            over_batches(sp, body)
            sp.wait_ge(o_stored, 1 + 16 * B * G * NK)

        @block.gpsimd
        def _(pool):
            pool.memset(negmax[:, HG * TILES:], 0.0)
            for g in range(G):
                pool.memset(k_op[g][:, :, 0:W], 0.0)
                last = pool.memset(k_op[g][:, :, W + T:], 0.0)
            last.then_inc(pads_set, 1)

        @block.tensor
        def _(pe):
            start_at_one(pe, o_ready)
            pe.wait_ge(c_loaded, 16 * N_C)
            pe.wait_ge(pads_set, 1)

            def piece_into(bank, g, i):
                h, t = BAND_PIECES[i]
                for a in range(2):
                    mm = pe.matmul(bank[:, 2 * P * a:2 * P * (a + 1)], q_op[g][0:NPROD, h, (t + a) * P:(t + a + 1) * P],
                                   k_op[g][0:NPROD, h, (t + a) * P:(t + a + 2) * P], start=(a == 0), stop=(a == 1))
                mm.then_inc(ring_ready, 1)

            def take_bank(b, place):
                pe.wait_ge(ring_read, uses_until(b, bank_free(place)))
                return pM[:, place % RING_BANKS]

            def flip_maxima(bank, n):
                pe.wait_ge(negmax_done, n + 1)
                pe.transpose(bank[:, 0:P], negmax[:], ident[:]).then_inc(ring_ready, 1)

            def turn_sums(bank, n, q):
                pe.wait_ge(o_copied, 1 + NK * n + q + 1)
                for j in range(NJ):
                    mm = pe.transpose(bank[:, j * P:(j + 1) * P], o_sb[:, j * P:(j + 1) * P], ident[:])
                mm.then_inc(ring_ready, 1)

            def use_ring(b, use):
                kind, g, i, place = use
                bank = take_bank(b, place)
                if kind == "piece":
                    piece_into(bank, (g + 1) % G, i)
                elif kind == "turn":
                    turn_sums(bank, b * G + g, i)
                else:
                    flip_maxima(bank, b * G + g + 1)

            def scores(n, g, j):
                lo, hi = (P if j == 0 else 0), (P if j == KT - 1 else 2 * P)
                edge = 0 if j == 0 else 2 if j == KT - 1 else 1
                pe.wait_ge(p_ready, KT * n + j + 1)
                for h in range(HG):
                    if h % 2 == 0:
                        pe.matmul(pS[:, (g * KT + j) % 2, h:h + 2, lo:hi], identb[:], mask_k[:, edge, :, lo:hi],
                                  start=True, stop=False)
                    mm = pe.matmul(pS[:, (g * KT + j) % 2, h, lo:hi], k_op[g][:, h, j * P:(j + 1) * P],
                                   q_op[g][:, h, (j - 1) * P + lo:(j - 1) * P + hi], start=False, stop=(h % 2 == 1))
                mm.then_inc(s_ready, 1)

            def values(n, g, t):
                pe.wait_ge(p_ready, KT * n + t + 2 + 2)
                if t % NJ == 0:
                    pe.wait_ge(o_copied, 1 + NK * n + t // NJ)
                for a in range(2):
                    for h in range(HG):
                        mm = pe.matmul(pO[VW * h:VW * (h + 1), t % NJ * P:(t % NJ + 1) * P], v_sb[g % 2][:, t + a, h],
                                       probs[:, (g * KT + t + a) % RING, h, P * (1 - a):P * (2 - a)],
                                       start=(a == 0), stop=(a == 1))
                mm.then_inc(o_ready, 1)

            pe.wait_ge(half_loaded, 16 * (1 + N_QK))
            for at, i in enumerate(BAND_LEAD_PIECES):
                if at == len(BAND_PIECES) // 2:
                    pe.wait_ge(qk_loaded[0], 16 * (1 + N_QK))
                if at >= LEAD_BANKS:
                    pe.wait_ge(ring_read, at - LEAD_BANKS + 1)
                piece_into(lead_bank(at), 0, i)
            flip_maxima(lead_bank(lead - 1), 0)

            def body(b, last):
                for at, uses in enumerate(last_uses if last else turn_uses):
                    g, j = divmod(at, KT)
                    n = b * G + g
                    early = [use for use in uses[:1] if use[0] == "piece"]
                    if g < G:
                        if j == 0:
                            pe.wait_ge(max_loaded, 48 * (n + 1))
                            pe.wait_ge(v_loaded[g % 2], 16 * (b * 2 + g // 2 + 1))
                            if not (last and g == G - 1):
                                loads = n_pos((g + 1) % G) + N_QK * (b + (g + 1) // G + 1)
                                pe.wait_ge(qk_loaded[(g + 1) % G], 16 * loads)
                        scores(n, g, j)
                    for use in early:
                        use_ring(b, use)
                    if at >= 2 and (at - 2) % KT < TILES:
                        past, t = divmod(at - 2, KT)
                        values(b * G + past, past, t)
                    for use in uses[len(early):]:
                        use_ring(b, use)

            over_batches(pe, body)

        @block.scalar
        def _(act):
            act.sem_inc(p_ready, 2)
            def body(b, last):
                for at in range(G * KT):
                    g, j = divmod(at, KT)
                    n = b * G + g
                    lo, hi = (P if j == 0 else 0), (P if j == KT - 1 else 2 * P)
                    past, t = divmod(at - RING, KT)
                    done = TILES * past + min(t, TILES - 1) + 1 if at >= RING else 0
                    act.wait_ge(o_ready, 1 + b * (G * TILES) + done)
                    act.wait_ge(s_ready, KT * n + j + 1)
                    act.activation(probs[:, at % RING, :, lo:hi], pS[:, at % 2, :, lo:hi], ACT.Exp
                                   ).then_inc(p_ready, 1)

            over_batches(act, body)

        @block.vector
        def _(dve):
            start_at_one(dve, o_copied)
            def piece(bank, used, i, at):
                h, t = BAND_PIECES[i]
                edge = 0 if t == 0 else 2 if t == TILES - 2 else 1
                dve.wait_ge(ring_ready, used + 1)
                turn = at % LEAD_BANKS
                dve.memset(held[:, turn:turn + 1], 0.0)
                for a in range(2):
                    op = dve.tensor_tensor_reduce(masked[:, turn, a], bank[:, 2 * P * a:2 * P * (a + 1)],
                                                  mask_q[:, edge, a], 1.0, LOWEST,
                                                  ALU.add, ALU.max, accum_out=maxes[:, h, t + a:t + a + 1])
                op.then_inc(ring_read, 1)

            def finish_maxima(used):
                dve.wait_ge(ring_read, used)
                dve.tensor_scalar(negmax[:, 0:HG * TILES], maxes[:].rearrange("p h t -> p (h t)"), -1.0, None, ALU.mult
                                  ).then_inc(negmax_done, 1)

            def split_maxima(bank, n, used):
                split_rows(dve, bank, n, used, max_parts, max_rest, ring_ready, ring_read, max_loaded, split_step)

            dve.wait_ge(c_loaded, 16 * N_C)
            for at, i in enumerate(BAND_LEAD_PIECES):
                piece(lead_bank(at), at, i, at)
            finish_maxima(lead - 1)
            split_maxima(lead_bank(lead - 1), 0, lead - 1)

            def copy_sums(n, q):
                dve.wait_ge(o_ready, 1 + TILES * n + NJ * (q + 1))
                dve.tensor_copy(o_sb[:], pO[:]).then_inc(o_copied, 1)

            def body(b, last):
                for at, uses in enumerate(last_uses if last else turn_uses):
                    g, u = divmod(at, KT)
                    for kind, _, i, place in uses:
                        if kind == "piece":
                            piece(pM[:, place % RING_BANKS], uses_until(b, place), i, i)
                            pieces_end = place + 1
                    if at >= 2 and (at - 2) % KT in BAND_ENDS:
                        past, v = divmod(at - 2, KT)
                        copy_sums(b * G + past, BAND_ENDS.index(v))
                    if u == BAND_MAX_AT and g < G and not (last and g == G - 1):
                        finish_maxima(uses_until(b, pieces_end))
                    for kind, past, i, place in uses:
                        bank, used = pM[:, place % RING_BANKS], uses_until(b, place)
                        if kind == "turn":
                            normalise(dve, bank, used, b * G + past, i, inv, o_norm, ring_ready, inv_done, o_stored,
                                      ring_read)
                        elif kind == "flip":
                            split_maxima(bank, b * G + past + 1, used)

            over_batches(dve, body)


def mix(nc, stage, consts, x, o_rows, wo, wr, wk, wv, mu_r, mu_k, out):
    with ExitStack() as ctx:
        def sb(name, shape, dt=F32):
            return ctx.enter_context(nc.sbuf_tensor(f"{stage}_{name}", shape, dt))

        def sem(name):
            return ctx.enter_context(nc.semaphore(f"{stage}_{name}"))

        def psum(name, shape):
            return ctx.enter_context(nc.psum_tensor(f"{stage}_{name}", shape, F32))

        wr_sb, wk_sb, wv_sb = [sb(f"w{n}_sb", [P, CH, C]) for n in "rkv"]
        wo_sb = sb("wo_sb", [P, CH, C])
        mu = sb("mu", [P, 2, CH])
        ident = sb("ident", [P, P])
        xt = sb("xt", [P, 2, NJ, C])
        ot = sb("ot", [P, 2, NJ, C])
        oT = sb("oT", [P, CH, TC])
        x1 = sb("x1", [P, NK, NJ, C])
        stats = sb("stats", [P, 2, NJ, 6])
        meanvar = sb("meanvar", [P, 2, NJ, 2])
        vareps = sb("vareps", [P, 2, NJ])
        held = sb("held", [P, 1])
        power = sb("power", [P, NJ])
        eps = sb("eps", [P, NJ])
        rstd = sb("rstd", [P, 2, NJ])
        xn = sb("xn", [P, 2, NJ, C])
        xnT = sb("xnT", [P, 2, CH, TC + 1])
        step = sb("step", [P, CH, TC])
        zero = sb("zero", [P, CH, 1])
        xk = sb("xk", [P, 2, CH, TC])
        xr = sb("xr", [P, 2, CH, TC])
        relu = sb("relu", [P, CH, TC])
        act_k = sb("act_k", [P, CH, TC])
        gate = sb("gate", [P, 2, 2, C])
        prod = sb("prod", [P, 2, 2, C])
        x2 = sb("x2", [P, 2, NJ, C])
        pA = psum("pA", [P, 2, 2, C])
        pT = psum("pT", [P, CH, TC])
        pV = psum("pV", [P, 2, 2, C])
        pK = pA if wo is None else pV
        pR = psum("pR", [P, 2, 2, C])

        first_loaded = sem("first_loaded")
        w_loaded = sem("w_loaded")
        x_loaded = [sem(f"x_loaded{i}") for i in range(2)]
        const_set = sem("const_set")
        oT_ready = sem("oT_ready")
        oT_done = sem("oT_done")
        a_ready = sem("a_ready")
        x1_done = sem("x1_done")
        stats_done = sem("stats_done")
        aggr_done = sem("aggr_done")
        vareps_done = sem("vareps_done")
        rstd_done = sem("rstd_done")
        xn_done = sem("xn_done")
        xT_ready = sem("xT_ready")
        xnT_done = sem("xnT_done")
        edge_done = sem("edge_done")
        step_done = sem("step_done")
        blend_done = sem("blend_done")
        k_ready = sem("k_ready")
        relu_done = sem("relu_done")
        act_k_done = sem("act_k_done")
        r_ready = sem("r_ready")
        gate_done = sem("gate_done")
        mv_ready = sem("mv_ready")
        prod_done = sem("prod_done")
        x2_done = sem("x2_done")
        x_stored = [sem(f"x_stored{i}") for i in range(2)]
        N_FIRST, N_W = 1 if wo is None else 2, 5
        rows = out.rearrange("b t c -> (b t) c")

        def turn(b, k):
            return b * (NK // 2) + k // 2 + 1

        block = ctx.enter_context(nc.Block())

        @block.sync
        def _(sp):
            start_at_one(sp, *x_stored)

            def load(b, k):
                for dst, src in ((ot, o_rows), (xt, x)):
                    sp.dma_start(dst[:, k % 2], src[b, k * TC:(k + 1) * TC, :].rearrange("(j p) c -> p j c", p=P)
                                 ).then_inc(x_loaded[k % 2], 16)

            load(0, 0)
            sp.dma_start(ident[:], consts["ident"]).then_inc(first_loaded, 16)
            if wo is not None:
                sp.dma_start(wo_sb[:], wo.rearrange("(h p) d -> p h d", p=P)).then_inc(first_loaded, 16)
            load(0, 1)
            for dst, src in ((wr_sb, wr), (wk_sb, wk), (wv_sb, wv)):
                sp.dma_start(dst[:], src.rearrange("(h p) d -> p h d", p=P)).then_inc(w_loaded, 16)
            with nc.allow_non_contiguous_dma(reason="256 factors, one a partition"):
                for n, src in enumerate((mu_k, mu_r)):
                    sp.dma_start(mu[:, n], src.rearrange("(h p) -> p h", p=P)).then_inc(w_loaded, 16)
            for k in range(2):
                sp.wait_ge(x1_done, k + 1)
                load(0, k + 2)

            def body(b, last):
                for k in range(NK):
                    c = b * NK + k
                    if not last:
                        sp.wait_ge(x1_done, c + 3)
                        load(b + 1, k)
                    sp.wait_ge(x2_done, 1 + 2 * c + 2)
                    sp.dma_start(rows[bass.ds(c * TC, TC), :].rearrange("(j p) c -> p j c", p=P), x2[:, k % 2]
                                 ).then_inc(x_stored[k % 2], 16)

            over_batches(sp, body)
            for s in x_stored:
                sp.wait_ge(s, 1 + 16 * B * NK // 2)

        @block.gpsimd
        def _(pool):
            start_at_one(pool, x2_done)
            pool.memset(eps[:], EPS)
            pool.memset(zero[:], 0.0)
            pool.memset(power[:], -0.5).then_inc(const_set, 1)
            pool.wait_ge(const_set, 1)

            def norm(c, k):
                pool.wait_ge(aggr_done, c + 1)
                pool.tensor_tensor(vareps[:, k % 2], meanvar[:, k % 2, :, 1], eps[:], ALU.add).then_inc(vareps_done, 1)
                pool.wait_ge(vareps_done, c + 1)
                pool.tensor_tensor(rstd[:, k % 2], vareps[:, k % 2], power[:], ALU.pow).then_inc(rstd_done, 1)

            def differ(c, k):
                pool.wait_ge(blend_done, 1 + 2 * c)
                pool.wait_ge(xnT_done, 2 * c + 2)
                before = zero[:] if k % NK == 0 else xnT[:, (k - 1) % 2, :, TC:TC + 1]
                pool.tensor_tensor(xnT[:, k % 2, :, 0:1], before, zero[:], ALU.add).then_inc(edge_done, 1)
                pool.wait_ge(edge_done, c + 1)
                pool.tensor_tensor(step[:], xnT[:, k % 2, :, 1:TC + 1], xnT[:, k % 2, :, 0:TC], ALU.subtract
                                   ).then_inc(step_done, 1)

            norm(0, 0)
            differ(0, 0)
            norm(1, 1)

            def body(b, last):
                for k in range(NK):
                    c = b * NK + k
                    if not (last and k == NK - 1):
                        differ(c + 1, k + 1)
                    if not (last and k >= NK - 2):
                        norm(c + 2, k + 2)
                    pool.wait_ge(x_stored[k % 2], 1 + 16 * (b * (NK // 2) + k // 2))
                    for n in range(2):
                        pool.wait_ge(prod_done, 1 + 2 * c + n + 1)
                        pool.tensor_tensor(x2[:, k % 2, 2 * n:2 * n + 2], x1[:, k, 2 * n:2 * n + 2], prod[:, n],
                                           ALU.add).then_inc(x2_done, 1)

            over_batches(pool, body)

        @block.vector
        def _(dve):
            start_at_one(dve, blend_done, prod_done)

            def residual(c, k, loads):
                dve.wait_ge(x_loaded[k % 2], 32 * loads)
                for n in range(2):
                    tiles = slice(2 * n, 2 * n + 2)
                    if wo is not None:
                        dve.wait_ge(a_ready, 2 * c + n + 1)
                    if n == 0 and not (isinstance(c, int) and c < 3):
                        dve.wait_ge(x2_done, 1 + 2 * (c - 2))
                    op = dve.tensor_tensor(x1[:, k % NK, tiles], xt[:, k % 2, tiles],
                                           ot[:, k % 2, tiles] if wo is None else pA[:, n], ALU.add)
                op.then_inc(x1_done, 1)
                dve.wait_ge(x1_done, c + 1)
                for j in range(NJ):
                    op = dve.bn_stats(stats[:, k % 2, j], x1[:, k % NK, j])
                op.then_inc(stats_done, 1)
                dve.wait_ge(stats_done, c + 1)
                dve.memset(held[:], 0.0)
                for j in range(NJ):
                    op = dve.bn_aggr(meanvar[:, k % 2, j], stats[:, k % 2, j])
                op.then_inc(aggr_done, 1)

            def normal(c, k):
                dve.wait_ge(rstd_done, c + 1)
                if not (isinstance(c, int) and c < 2):
                    dve.wait_ge(xT_ready, 2 * (c - 1))
                for j in range(NJ):
                    op = dve.tensor_scalar(xn[:, k % 2, j], x1[:, k % NK, j], meanvar[:, k % 2, j, 0:1],
                                           rstd[:, k % 2, j:j + 1], ALU.subtract, ALU.mult)
                op.then_inc(xn_done, 1)

            def blend(c, k):
                dve.wait_ge(step_done, c + 1)
                for n, (dst, used) in enumerate(((xk, k_ready), (xr, r_ready))):
                    if not (isinstance(c, int) and c == 0):
                        dve.wait_ge(used, 1 + 2 * (c - 1))
                    for h in range(CH):
                        op = dve.scalar_tensor_tensor(
                            out=dst[:, k % 2, h], in0=step[:, h], scalar=mu[:, n, h:h + 1],
                            in1=xnT[:, k % 2, h, 0:TC], op0=ALU.mult, op1=ALU.add)
                    op.then_inc(blend_done, 1)

            def multiply(c):
                for n in range(2):
                    dve.wait_ge(gate_done, 1 + 2 * c + n + 1)
                    dve.wait_ge(mv_ready, 1 + 2 * c + n + 1)
                    dve.wait_ge(x2_done, 1 + 2 * c)
                    dve.tensor_tensor(prod[:, n], gate[:, n], pV[:, n], ALU.mult).then_inc(prod_done, 1)

            residual(0, 0, 1)
            normal(0, 0)
            residual(1, 1, 1)
            dve.wait_ge(w_loaded, 16 * N_W)
            blend(0, 0)
            normal(1, 1)

            def body(b, last):
                for k in range(NK):
                    c = b * NK + k
                    more = not (last and k >= NK - 2)
                    if wo is None and more:
                        residual(c + 2, k + 2, turn(b, k + 2))
                    if not (last and k == NK - 1):
                        blend(c + 1, k + 1)
                    if wo is None and more:
                        normal(c + 2, k + 2)
                    if wo is not None and more:
                        residual(c + 2, k + 2, turn(b, k + 2))
                    multiply(c)
                    if wo is not None and more:
                        normal(c + 2, k + 2)

            over_batches(dve, body)

        @block.scalar
        def _(act):
            start_at_one(act, gate_done, act_k_done)

            def copy_oT(c):
                if wo is None:
                    return
                for h in range(CH):
                    act.wait_ge(oT_ready, 2 * c + h + 1)
                    if h == 0:
                        act.wait_ge(a_ready, 2 * c)
                    act.activation(oT[:, h], pA[:, h].rearrange("p a c -> p (a c)"), ACT.Copy).then_inc(oT_done, 1)

            def copy_xnT(c, k):
                act.wait_ge(blend_done, 1 + 2 * c)
                for h in range(CH):
                    act.wait_ge(xT_ready, 2 * c + h + 1)
                    act.activation(xnT[:, k % 2, h, 1:TC + 1], pT[:, h], ACT.Copy).then_inc(xnT_done, 1)

            copy_oT(0)
            copy_oT(1)
            copy_xnT(0, 0)

            def body(b, last):
                for k in range(NK):
                    c = b * NK + k
                    if not (last and k >= NK - 2):
                        copy_oT(c + 2)
                    act.wait_ge(act_k_done, 1 + 2 * c)
                    for h in range(CH):
                        act.wait_ge(k_ready, 1 + 2 * c + h + 1)
                        act.activation(relu[:, h], pK[:, h].rearrange("p a c -> p (a c)"), ACT.Relu
                                       ).then_inc(relu_done, 1)
                    act.wait_ge(mv_ready, 1 + 2 * c)
                    for h in range(CH):
                        act.wait_ge(relu_done, 2 * c + h + 1)
                        act.activation(act_k[:, h], relu[:, h], ACT.Square).then_inc(act_k_done, 1)
                    if not (last and k == NK - 1):
                        copy_xnT(c + 1, k + 1)
                    act.wait_ge(prod_done, 1 + 2 * c)
                    for n in range(2):
                        act.wait_ge(r_ready, 1 + 2 * c + n + 1)
                        act.activation(gate[:, n], pR[:, n], ACT.Sigmoid).then_inc(gate_done, 1)

            over_batches(act, body)

        @block.tensor
        def _(pe):
            start_at_one(pe, k_ready, r_ready, mv_ready)
            pe.wait_ge(first_loaded, 16 * N_FIRST)

            def turn_heads(c, k, loads):
                if wo is None:
                    return
                pe.wait_ge(x_loaded[k % 2], 32 * loads)
                pe.wait_ge(x1_done, c)
                for h in range(CH):
                    for j in range(NJ):
                        mm = pe.transpose(pA[:, h].rearrange("p a c -> p (a c)")[:, j * P:(j + 1) * P],
                                          ot[:, k % 2, j, h * P:(h + 1) * P], ident[:])
                    mm.then_inc(oT_ready, 1)

            def project_heads(c):
                if wo is None:
                    return
                pe.wait_ge(oT_done, 2 * c + 2)
                for n in range(2):
                    for a in range(2):
                        t = 2 * n + a
                        for h in range(CH):
                            mm = pe.matmul(pA[:, n, a], oT[:, h, t * P:(t + 1) * P], wo_sb[:, h],
                                           start=(h == 0), stop=(h == CH - 1))
                    mm.then_inc(a_ready, 1)

            def transpose(c, k):
                pe.wait_ge(xn_done, c + 1)
                pe.wait_ge(xnT_done, 2 * c)
                for h in range(CH):
                    for j in range(NJ):
                        mm = pe.transpose(pT[:, h, j * P:(j + 1) * P], xn[:, k % 2, j, h * P:(h + 1) * P], ident[:])
                    mm.then_inc(xT_ready, 1)

            def rows_by(weights, lhs, dst, ready):
                for n in range(2):
                    for a in range(2):
                        t = 2 * n + a
                        for h in range(CH):
                            mm = pe.matmul(dst[:, n, a], lhs[:, h, t * P:(t + 1) * P], weights[:, h],
                                           start=(h == 0), stop=(h == CH - 1))
                    mm.then_inc(ready, 1)

            for c in range(2):
                turn_heads(c, c, 1)
                project_heads(c)
            transpose(0, 0)
            pe.wait_ge(w_loaded, 16 * N_W)

            def body(b, last):
                for k in range(NK):
                    c = b * NK + k
                    if not (last and k >= NK - 2):
                        turn_heads(c + 2, k + 2, turn(b, k + 2))
                    pe.wait_ge(blend_done, 1 + 2 * c + 1)
                    if pK is pV:
                        pe.wait_ge(prod_done, 1 + 2 * c)
                    for m in range(CH):
                        for h in range(CH):
                            mm = pe.matmul(pK[:, m].rearrange("p a c -> p (a c)"), wk_sb[:, h, m * P:(m + 1) * P],
                                           xk[:, k % 2, h], start=(h == 0), stop=(h == CH - 1))
                        mm.then_inc(k_ready, 1)
                    if not (last and k == NK - 1):
                        transpose(c + 1, k + 1)
                    pe.wait_ge(blend_done, 1 + 2 * c + 2)
                    pe.wait_ge(gate_done, 1 + 2 * c)
                    rows_by(wr_sb, xr[:, k % 2], pR, r_ready)
                    if not (last and k >= NK - 2):
                        project_heads(c + 2)
                    pe.wait_ge(act_k_done, 1 + 2 * c + 2)
                    if pK is not pV:
                        pe.wait_ge(prod_done, 1 + 2 * c)
                    rows_by(wv_sb, act_k, pV, mv_ready)

            over_batches(pe, body)


def build(nc, ins, consts, out):
    def scratch(name, shape, dt=F32):
        return nc.dram_tensor(name, shape, dt, kind="Internal").ap()

    qk_parts = scratch("qk_parts", [2, B, 3, C, T], BF16)
    v_rows = scratch("v_rows", [B, W + T + W, H, VW])
    o_rows = scratch("o_rows", [B, T, C])
    x2 = scratch("x_after_first", [B, T, C])
    ffn = [ins[n] for n in ("L0_ffn_W_r", "L0_ffn_W_k", "L0_ffn_W_v", "L0_ffn_mu_r", "L0_ffn_mu_k")]
    project(nc, "proj_a", consts, ins["L0_attn_a_x"], ins["L0_attn_a_Wq"], ins["L0_attn_a_Wk"], ins["L0_attn_a_Wv"],
            None, qk_parts, v_rows)
    attend_full(nc, "full", consts, qk_parts, v_rows, o_rows)
    mix(nc, "mix_a", consts, ins["L0_attn_a_x"], o_rows, ins["L0_attn_a_Wo"], *ffn, x2)
    project(nc, "proj_b", consts, x2, ins["L0_attn_b_Wq"], ins["L0_attn_b_Wk"], ins["L0_attn_b_Wv"],
            [ins[f"L0_attn_b_b{n}"] for n in "qkv"], qk_parts, v_rows)
    attend_band(nc, "band", consts, qk_parts, v_rows, o_rows)
    mix(nc, "mix_b", consts, x2, o_rows, None, *ffn, out)


def constants():
    import numpy as np

    bf16 = mybir.dt.np(BF16)

    def three_parts(a):
        parts = []
        for _ in range(3):
            parts.append(a.astype(bf16))
            a = a - parts[-1].astype(np.float32)
        return parts

    p = np.arange(P)
    eye = np.eye(P, dtype=np.float32)
    slope = three_parts(np.array([2.0 ** (-8.0 * h / H) for h in range(1, H + 1)], np.float32))
    pos = np.arange(T)
    slopes = np.zeros((H, NPOS, T), bf16)
    positions = np.ones((NPOS + 3, T), bf16)
    for s in range(T // POS_STEP):
        for i in range(3):
            slopes[:, 3 * s + i, s * POS_STEP:(s + 1) * POS_STEP] = slope[i][:, None]
            positions[3 * s + i] = (pos // P * P - s * POS_STEP).astype(bf16)
    for i in range(3):
        slopes[:, NPOS - 3 + i] = slope[i][:, None]
        positions[NPOS - 3 + i] = (pos % P).astype(bf16)

    def masked(valid):
        return np.where(valid, 0.0, NEG).astype(bf16)

    c = np.arange(2 * P)
    band = (c[None, :] >= p[:, None]) & (c[None, :] - p[:, None] <= P)
    left, right = c[None, :] >= W, c[None, :] < 3 * W
    lower, upper = p[:, None] >= W, p[:, None] < W
    band_q = np.stack([masked(np.stack(v, 1)) for v in ((band & left, band), (band, band), (band, band & right))], 1)
    band_k = np.stack([masked(np.stack(v, 1)) for v in ((band & lower,) * 2, (band,) * 2, (band & upper,) * 2)], 1)
    return {
        "ident": eye, "identb": eye.astype(bf16),
        "mask_q": masked(p[None, :] <= p[:, None]), "mask_k": masked(p[None, :] >= p[:, None]),
        "slopes": slopes, "positions": positions, "band_q": band_q.astype(np.float32), "band_k": band_k,
    }


_TRANSPOSED = {"L0_attn_a_Wq", "L0_attn_a_Wk", "L0_attn_a_Wv", "L0_attn_a_Wo", "L0_ffn_W_r", "L0_ffn_W_k",
               "L0_ffn_W_v"}


def kernel(**inputs):
    import numpy as _np
    import concourse.bacc as _bacc
    from concourse import mybir as _mybir
    from concourse.bass_utils import run_bass_kernel_spmd as _run

    nc = _bacc.Bacc("TRN2", target_bir_lowering=False, num_devices=1)
    arrays = {}

    def given(name, a):
        arrays[name] = _np.ascontiguousarray(a)
        return nc.dram_tensor(name, a.shape, _mybir.dt.from_np(a.dtype), kind="ExternalInput").ap()

    ins = {n: given(f"in_{n}", _np.asarray(a).T if n in _TRANSPOSED else _np.asarray(a)) for n, a in inputs.items()}
    consts = {n: given(f"const_{n}", a) for n, a in constants().items()}
    out = nc.dram_tensor("out_x", (B, T, C), F32, kind="ExternalOutput").ap()
    build(nc, ins, consts, out)
    r = _run(nc, [arrays], core_ids=[0])
    return r.results[0]["out_x"]
```
